# Optimizing a Trainium2 kernel written in Bass

```python
import numpy as np
import jax
import jax.numpy as jnp

def _softmax(x, axis=-1):
    return jax.nn.softmax(x, axis=axis)

def _gelu(x):
    return jax.nn.gelu(x, approximate=True)

def _silu(x):
    return jax.nn.silu(x)

def _sigmoid(x):
    return jax.nn.sigmoid(x)

def _layernorm(x, axis=-1, eps=1e-05):
    m = jnp.mean(x, axis=axis, keepdims=True)
    v = jnp.var(x, axis=axis, keepdims=True)
    return (x - m) / jnp.sqrt(v + eps)

def _scatter_add(tgt, idx, src, axis=0):
    return tgt.at[idx].add(src)

def _segment_sum(src, seg, n):
    return jax.ops.segment_sum(src, seg, n)
kernel_name = 'mk_gnn_ffn_d4_gnn_r32_0c450f'

def setup_inputs(seed: int=0):
    np.random.seed(seed)
    _w = jnp.asarray

    def _rec_inputs():
        import jax
        import jax.numpy as jnp
        _gk = jax.random.key(seed)
        x = -8.776e-05 + 1 * jax.random.normal(jax.random.fold_in(_gk, 1), (625, 256), jnp.float32)
        src = jax.random.randint(jax.random.fold_in(_gk, 2), (20000,), 0, 625, jnp.int32)
        dst = jnp.minimum((625 * jax.random.uniform(jax.random.fold_in(_gk, 3), (20000,)) ** 2.0).astype(jnp.int32), 19999)
        _o = jnp.argsort(dst, stable=True)
        src = src[_o]
        dst = dst[_o]
        edge_attr_128 = 0.000135552 + 1.00015 * jax.random.normal(jax.random.fold_in(_gk, 13), (20000, 128), jnp.float32)
        edge_attr_18 = 0.000318098 + 1.00013 * jax.random.normal(jax.random.fold_in(_gk, 14), (20000, 18), jnp.float32)
        edge_attr_256 = -8.513e-05 + 0.999844 * jax.random.normal(jax.random.fold_in(_gk, 15), (20000, 256), jnp.float32)
        edge_attr_54 = 0.000309991 + 1.00005 * jax.random.normal(jax.random.fold_in(_gk, 16), (20000, 54), jnp.float32)
        edge_type_2 = jax.random.randint(jax.random.fold_in(_gk, 18), (20000,), 0, 2, jnp.int32)
        edge_type_8 = jax.random.randint(jax.random.fold_in(_gk, 19), (20000,), 0, 8, jnp.int32)
        edge_weight = jax.random.uniform(jax.random.fold_in(_gk, 20), (20000,), jnp.float32, 0.0, 0.999998)
        node_type_2 = jax.random.randint(jax.random.fold_in(_gk, 21), (625,), 0, 2, jnp.int32)
        node_vec = jax.random.uniform(jax.random.fold_in(_gk, 22), (625,), jnp.float32, 0.0, 0.999994)
        return (x, src, dst, edge_attr_128, edge_attr_18, edge_attr_256, edge_attr_54, edge_type_2, edge_type_8, edge_weight, node_type_2, node_vec)
    x, src, dst, edge_attr_128, edge_attr_18, edge_attr_256, edge_attr_54, edge_type_2, edge_type_8, edge_weight, node_type_2, node_vec = _rec_inputs()

    def _L0_gnn_setup():
        import jax, jax.numpy as jnp
        import numpy as np
        N, E, C, MID = (625, 10000, 256, 64)
        NR, NS = (6, 3)
        F1_IN = NR * NS * NS
        F2_IN = NR * NS
        G = 64
        EPS = 1e-05
        NEG_SLOPE = 0.1

        def leaky(v):
            return jnp.where(v > 0, v, NEG_SLOPE * v)
        key = jax.random.key(seed)
        ks = jax.random.split(key, 26)

        def w(k, shape):
            fan_in = shape[0]
            return jax.random.normal(k, shape, dtype=jnp.float32) / jnp.sqrt(jnp.float32(fan_in))
        return {'x': jax.random.normal(ks[0], (N, C), dtype=jnp.float32), 'gate_edge': jax.random.normal(ks[1], (E, C), dtype=jnp.float32), 'feature1': jax.random.normal(ks[2], (E, F1_IN), dtype=jnp.float32), 'feature2': jax.random.normal(ks[3], (E, F2_IN), dtype=jnp.float32), 'edge_index': jax.random.randint(ks[4], (2, E), 0, N, dtype=jnp.int32), 'batch': jnp.sort(jax.random.randint(ks[5], (N,), 0, G, dtype=jnp.int32)), 'w_f1a': w(ks[6], (F1_IN, MID)), 'w_f1b': w(ks[7], (MID, C)), 'w_f2a': w(ks[8], (F2_IN, MID)), 'w_f2b': w(ks[9], (MID, C)), 'c1_wl': w(ks[10], (C, C)), 'c1_bl': jnp.zeros((C,), jnp.float32), 'c1_wr': w(ks[11], (C, C)), 'c2_wl': w(ks[12], (C, C)), 'c2_bl': jnp.zeros((C,), jnp.float32), 'c2_wr': w(ks[13], (C, C)), 'lin1_w': w(ks[14], (C, C)), 'lin1_b': jnp.zeros((C,), jnp.float32), 'lin2_w': w(ks[15], (C, C)), 'lin2_b': jnp.zeros((C,), jnp.float32), 'cat_w': w(ks[16], (2 * C, C)), 'cat_b': jnp.zeros((C,), jnp.float32), 'gn_w': jnp.ones((C,), jnp.float32), 'gn_b': jnp.zeros((C,), jnp.float32), 'gn_ms': jnp.ones((C,), jnp.float32)}
    _L0_gnn_all = _L0_gnn_setup()
    _L0_gnn_in = {k: v for k, v in _L0_gnn_all.items() if k in ('w_f1a', 'w_f1b', 'w_f2a', 'w_f2b', 'c1_wl', 'c1_bl', 'c1_wr', 'c2_wl', 'c2_bl', 'c2_wr', 'lin1_w', 'lin1_b', 'lin2_w', 'lin2_b', 'cat_w', 'cat_b', 'gn_w', 'gn_b', 'gn_ms')}
    del _L0_gnn_all

    def _L0_ffn_setup():
        import jax, jax.numpy as jnp
        import numpy as np
        BN_EPS = 0.001

        def _bn(h, g, b, m, v):
            return g * (h - m) * jax.lax.rsqrt(v + BN_EPS) + b
        key = jax.random.key(seed)
        ks = jax.random.split(key, 8)
        B, F, Df = (256, 64, 256)
        E, H, D = (8, 256, 256)
        s1 = 1.0 / np.sqrt(Df)
        s2 = 1.0 / np.sqrt(H)
        return {'x': jax.random.normal(ks[0], (B, F, Df), jnp.float32), 'Wr': jax.random.normal(ks[1], (Df, E), jnp.float32) * s1, 'br': jnp.zeros((E,), jnp.float32), 'W1': jax.random.normal(ks[2], (E, Df, H), jnp.float32) * s1, 'b1': jnp.zeros((E, H), jnp.float32), 'g1': jnp.ones((E, H), jnp.float32), 'be1': jnp.zeros((E, H), jnp.float32), 'm1': jnp.zeros((E, H), jnp.float32), 'v1': jnp.ones((E, H), jnp.float32), 'W2': jax.random.normal(ks[3], (E, H, H), jnp.float32) * s2, 'b2': jnp.zeros((E, H), jnp.float32), 'g2': jnp.ones((E, H), jnp.float32), 'be2': jnp.zeros((E, H), jnp.float32), 'm2': jnp.zeros((E, H), jnp.float32), 'v2': jnp.ones((E, H), jnp.float32), 'Wo': jax.random.normal(ks[4], (E, H, D), jnp.float32) * s2, 'bo': jnp.zeros((E, D), jnp.float32)}
    _L0_ffn_all = _L0_ffn_setup()
    _L0_ffn_in = {k: v for k, v in _L0_ffn_all.items() if k in ('Wr', 'br', 'W1', 'b1', 'g1', 'be1', 'm1', 'v1', 'W2', 'b2', 'g2', 'be2', 'm2', 'v2', 'Wo', 'bo')}
    del _L0_ffn_all

    def _L1_gnn_setup():
        import jax, jax.numpy as jnp
        import numpy as np
        N, E, R, H, D = (30000, 9375, 8, 8, 32)
        IN_F = 256
        NEG_SLOPE = 0.2
        key = jax.random.key(seed)
        k = jax.random.split(key, 6)
        x = jax.random.normal(k[0], (N, IN_F), dtype=jnp.float32)
        W = jax.random.normal(k[1], (R, H * D, IN_F), dtype=jnp.float32) * 0.05
        attn_src = jax.random.normal(k[2], (H, D), dtype=jnp.float32) * 0.1
        attn_dst = jax.random.normal(k[3], (H, D), dtype=jnp.float32) * 0.1
        edge_index = jax.random.randint(k[4], (2, E), 0, N, dtype=jnp.int64) if jax.config.read('jax_enable_x64') else jax.random.randint(k[4], (2, E), 0, N, dtype=jnp.int32)
        edge_type = jax.random.randint(k[5], (E,), 0, R, dtype=edge_index.dtype)
        return dict(x=x, W=W, attn_src=attn_src, attn_dst=attn_dst, edge_index=edge_index, edge_type=edge_type)
    _L1_gnn_all = _L1_gnn_setup()
    _L1_gnn_in = {k: v for k, v in _L1_gnn_all.items() if k in ('W', 'attn_src', 'attn_dst')}
    del _L1_gnn_all

    def _L1_ffn_setup():
        import jax, jax.numpy as jnp
        import numpy as np
        DIM = 256
        H = 8
        D = 64
        G = 64
        INNER = H * D
        SCALE = D ** (-0.5)
        key = jax.random.key(seed)
        ks = jax.random.split(key, 12)
        B, N = (4, 512)
        x = jax.random.normal(ks[0], (B, N, DIM), dtype=jnp.float32)
        s = lambda fan_in: 1.0 / np.sqrt(fan_in)
        W_fx = jax.random.normal(ks[1], (DIM, INNER), dtype=jnp.float32) * s(DIM)
        b_fx = jnp.zeros((INNER,), dtype=jnp.float32)
        W_x = jax.random.normal(ks[2], (DIM, INNER), dtype=jnp.float32) * s(DIM)
        b_x = jnp.zeros((INNER,), dtype=jnp.float32)
        A = jax.random.normal(ks[3], (G, D), dtype=jnp.float32)
        Q, _ = jnp.linalg.qr(A.T)
        W_slice = Q[:, :G].astype(jnp.float32)
        b_slice = jnp.zeros((G,), dtype=jnp.float32)
        W_q = jax.random.normal(ks[4], (D, D), dtype=jnp.float32) * s(D)
        W_k = jax.random.normal(ks[5], (D, D), dtype=jnp.float32) * s(D)
        W_v = jax.random.normal(ks[6], (D, D), dtype=jnp.float32) * s(D)
        W_out = jax.random.normal(ks[7], (INNER, DIM), dtype=jnp.float32) * s(INNER)
        b_out = jnp.zeros((DIM,), dtype=jnp.float32)
        temperature = jnp.ones((1, H, 1, 1), dtype=jnp.float32) * 0.5
        return {'x': x, 'W_fx': W_fx, 'b_fx': b_fx, 'W_x': W_x, 'b_x': b_x, 'W_slice': W_slice, 'b_slice': b_slice, 'W_q': W_q, 'W_k': W_k, 'W_v': W_v, 'W_out': W_out, 'b_out': b_out, 'temperature': temperature}
    _L1_ffn_all = _L1_ffn_setup()
    _L1_ffn_in = {k: v for k, v in _L1_ffn_all.items() if k in ('W_fx', 'b_fx', 'W_x', 'b_x', 'W_slice', 'b_slice', 'W_q', 'W_k', 'W_v', 'W_out', 'b_out', 'temperature')}
    del _L1_ffn_all

    def _L2_gnn_setup():
        import jax, jax.numpy as jnp
        import numpy as np
        N, D, E = (50000, 256, 12500)
        T = 2
        H = 512
        ETYPES = (0, 1)
        NTYPES = (0, 1)
        key = jax.random.key(seed)
        ks = jax.random.split(key, 12)
        inp = {'node_feature': jax.random.normal(ks[0], (N, D), jnp.float32), 'src': jax.random.randint(ks[1], (E,), 0, N), 'dst': jax.random.randint(ks[2], (E,), 0, N), 'edge_types': jax.random.randint(ks[3], (E,), 0, T), 'node_types': jax.random.randint(ks[4], (N,), 0, T), 'W0': jax.random.normal(ks[5], (T, 2 * D, H), jnp.float32) / np.sqrt(2 * D), 'b0': jnp.zeros((T, H), jnp.float32), 'W1': jax.random.normal(ks[6], (T, H, H), jnp.float32) / np.sqrt(H), 'b1': jnp.zeros((T, H), jnp.float32), 'W2': jax.random.normal(ks[7], (T, H, D), jnp.float32) / np.sqrt(H), 'b2': jnp.zeros((T, D), jnp.float32)}
        return inp
    _L2_gnn_all = _L2_gnn_setup()
    _L2_gnn_in = {k: v for k, v in _L2_gnn_all.items() if k in ('W0', 'b0', 'W1', 'b1', 'W2', 'b2')}
    del _L2_gnn_all

    def _L2_ffn_setup():
        import jax, jax.numpy as jnp
        import numpy as np
        C = 256
        HID = 1024
        E = 8
        TEMP = 1.0
        key = jax.random.key(seed)
        ks = jax.random.split(key, 7)
        x = jax.random.normal(ks[0], (8, 512, C), dtype=jnp.float32)
        W1 = jax.random.normal(ks[1], (C, HID), dtype=jnp.float32) * 0.02
        b1 = jnp.zeros((HID,), dtype=jnp.float32)
        Wg = jax.random.normal(ks[2], (HID, E), dtype=jnp.float32) * 0.02
        bg = jnp.zeros((E,), dtype=jnp.float32)
        Wd = jax.random.normal(ks[3], (E, HID, C), dtype=jnp.float32) * 0.02
        bd = jnp.zeros((E, C), dtype=jnp.float32)
        return {'x': x, 'W1': W1, 'b1': b1, 'Wg': Wg, 'bg': bg, 'Wd': Wd, 'bd': bd}
    _L2_ffn_all = _L2_ffn_setup()
    _L2_ffn_in = {k: v for k, v in _L2_ffn_all.items() if k in ('W1', 'b1', 'Wg', 'bg', 'Wd', 'bd')}
    del _L2_ffn_all

    def _L3_gnn_setup():
        import jax, jax.numpy as jnp
        import numpy as np
        N, E = (50000, 12500)
        IN_CH, OUT_CH, MSG_DIM, TIME_DIM = (256, 256, 128, 128)
        HEADS = 2
        C = OUT_CH // HEADS
        EDGE_DIM = MSG_DIM + TIME_DIM
        key = jax.random.key(seed)
        ks = jax.random.split(key, 16)
        x = jax.random.normal(ks[0], (N, IN_CH), dtype=jnp.float32)
        last_update = jax.random.uniform(ks[1], (N,), dtype=jnp.float32)
        t = jax.random.uniform(ks[2], (E,), dtype=jnp.float32)
        msg = jax.random.normal(ks[3], (E, MSG_DIM), dtype=jnp.float32)
        edge_index = jax.random.randint(ks[4], (2, E), 0, N, dtype=jnp.int64)
        s = 0.05
        Wt = jax.random.normal(ks[5], (1, TIME_DIM), dtype=jnp.float32) * s
        bt = jax.random.normal(ks[6], (TIME_DIM,), dtype=jnp.float32) * s
        Wq = jax.random.normal(ks[7], (IN_CH, HEADS * C), dtype=jnp.float32) * s
        bq = jax.random.normal(ks[8], (HEADS * C,), dtype=jnp.float32) * s
        Wk = jax.random.normal(ks[9], (IN_CH, HEADS * C), dtype=jnp.float32) * s
        bk = jax.random.normal(ks[10], (HEADS * C,), dtype=jnp.float32) * s
        Wv = jax.random.normal(ks[11], (IN_CH, HEADS * C), dtype=jnp.float32) * s
        bv = jax.random.normal(ks[12], (HEADS * C,), dtype=jnp.float32) * s
        We = jax.random.normal(ks[13], (EDGE_DIM, HEADS * C), dtype=jnp.float32) * s
        Wskip = jax.random.normal(ks[14], (IN_CH, HEADS * C), dtype=jnp.float32) * s
        bskip = jax.random.normal(ks[15], (HEADS * C,), dtype=jnp.float32) * s
        return {'x': x, 'last_update': last_update, 't': t, 'msg': msg, 'edge_index': edge_index, 'Wt': Wt, 'bt': bt, 'Wq': Wq, 'bq': bq, 'Wk': Wk, 'bk': bk, 'Wv': Wv, 'bv': bv, 'We': We, 'Wskip': Wskip, 'bskip': bskip}
    _L3_gnn_all = _L3_gnn_setup()
    _L3_gnn_in = {k: v for k, v in _L3_gnn_all.items() if k in ('Wt', 'bt', 'Wq', 'bq', 'Wk', 'bk', 'Wv', 'bv', 'We', 'Wskip', 'bskip')}
    del _L3_gnn_all

    def _L3_ffn_setup():
        import jax, jax.numpy as jnp
        import numpy as np
        NUM_EXPERTS = 8
        TOP_K = 2
        B, S, D = (8, 256, 256)

        def _moe(tokens, router_w, w1, b1, w2, b2):
            N = tokens.shape[0]
            E = router_w.shape[0]
            logits = tokens.astype(jnp.float32) @ router_w.astype(jnp.float32).T
            probs = jax.nn.softmax(logits, axis=-1)
            rw, re = jax.lax.top_k(probs, TOP_K)
            if TOP_K > 1:
                rw = rw / jnp.maximum(rw.sum(-1, keepdims=True), 1e-12)
            rw = rw.astype(tokens.dtype)
            combine = jnp.zeros((N, E), tokens.dtype).at[jnp.arange(N)[:, None], re].set(rw)
            out = tokens
            for e in range(E):
                h = jax.nn.gelu(tokens @ w1[e] + b1[e], approximate=False)
                y = h @ w2[e] + b2[e]
                out = out + combine[:, e:e + 1] * y
            return out
        key = jax.random.key(seed)
        ks = jax.random.split(key, 4)
        scale = 1.0 / np.sqrt(D).astype(np.float32)
        return {'input_embeddings': jax.random.normal(ks[0], (B, S, D), jnp.float32), 'router_w': jax.random.normal(ks[1], (NUM_EXPERTS, D), jnp.float32) * scale, 'w1': jax.random.normal(ks[2], (NUM_EXPERTS, D, D), jnp.float32) * scale, 'b1': jnp.zeros((NUM_EXPERTS, D), jnp.float32), 'w2': jax.random.normal(ks[3], (NUM_EXPERTS, D, D), jnp.float32) * scale, 'b2': jnp.zeros((NUM_EXPERTS, D), jnp.float32)}
    _L3_ffn_all = _L3_ffn_setup()
    _L3_ffn_in = {k: v for k, v in _L3_ffn_all.items() if k in ('router_w', 'w1', 'b1', 'w2', 'b2')}
    del _L3_ffn_all
    return {'x': x, 'src': src, 'dst': dst, 'edge_attr_128': edge_attr_128, 'edge_attr_18': edge_attr_18, 'edge_attr_256': edge_attr_256, 'edge_attr_54': edge_attr_54, 'edge_type_2': edge_type_2, 'edge_type_8': edge_type_8, 'edge_weight': edge_weight, 'node_type_2': node_type_2, 'node_vec': node_vec, 'L0_gnn_w_f1a': _L0_gnn_in['w_f1a'], 'L0_gnn_w_f1b': _L0_gnn_in['w_f1b'], 'L0_gnn_w_f2a': _L0_gnn_in['w_f2a'], 'L0_gnn_w_f2b': _L0_gnn_in['w_f2b'], 'L0_gnn_c1_wl': _L0_gnn_in['c1_wl'], 'L0_gnn_c1_bl': _L0_gnn_in['c1_bl'], 'L0_gnn_c1_wr': _L0_gnn_in['c1_wr'], 'L0_gnn_c2_wl': _L0_gnn_in['c2_wl'], 'L0_gnn_c2_bl': _L0_gnn_in['c2_bl'], 'L0_gnn_c2_wr': _L0_gnn_in['c2_wr'], 'L0_gnn_lin1_w': _L0_gnn_in['lin1_w'], 'L0_gnn_lin1_b': _L0_gnn_in['lin1_b'], 'L0_gnn_lin2_w': _L0_gnn_in['lin2_w'], 'L0_gnn_lin2_b': _L0_gnn_in['lin2_b'], 'L0_gnn_cat_w': _L0_gnn_in['cat_w'], 'L0_gnn_cat_b': _L0_gnn_in['cat_b'], 'L0_gnn_gn_w': _L0_gnn_in['gn_w'], 'L0_gnn_gn_b': _L0_gnn_in['gn_b'], 'L0_gnn_gn_ms': _L0_gnn_in['gn_ms'], 'L0_ffn_Wr': _L0_ffn_in['Wr'], 'L0_ffn_br': _L0_ffn_in['br'], 'L0_ffn_W1': _L0_ffn_in['W1'], 'L0_ffn_b1': _L0_ffn_in['b1'], 'L0_ffn_g1': _L0_ffn_in['g1'], 'L0_ffn_be1': _L0_ffn_in['be1'], 'L0_ffn_m1': _L0_ffn_in['m1'], 'L0_ffn_v1': _L0_ffn_in['v1'], 'L0_ffn_W2': _L0_ffn_in['W2'], 'L0_ffn_b2': _L0_ffn_in['b2'], 'L0_ffn_g2': _L0_ffn_in['g2'], 'L0_ffn_be2': _L0_ffn_in['be2'], 'L0_ffn_m2': _L0_ffn_in['m2'], 'L0_ffn_v2': _L0_ffn_in['v2'], 'L0_ffn_Wo': _L0_ffn_in['Wo'], 'L0_ffn_bo': _L0_ffn_in['bo'], 'L1_gnn_W': _L1_gnn_in['W'], 'L1_gnn_attn_src': _L1_gnn_in['attn_src'], 'L1_gnn_attn_dst': _L1_gnn_in['attn_dst'], 'L1_ffn_W_fx': _L1_ffn_in['W_fx'], 'L1_ffn_b_fx': _L1_ffn_in['b_fx'], 'L1_ffn_W_x': _L1_ffn_in['W_x'], 'L1_ffn_b_x': _L1_ffn_in['b_x'], 'L1_ffn_W_slice': _L1_ffn_in['W_slice'], 'L1_ffn_b_slice': _L1_ffn_in['b_slice'], 'L1_ffn_W_q': _L1_ffn_in['W_q'], 'L1_ffn_W_k': _L1_ffn_in['W_k'], 'L1_ffn_W_v': _L1_ffn_in['W_v'], 'L1_ffn_W_out': _L1_ffn_in['W_out'], 'L1_ffn_b_out': _L1_ffn_in['b_out'], 'L1_ffn_temperature': _L1_ffn_in['temperature'], 'L2_gnn_W0': _L2_gnn_in['W0'], 'L2_gnn_b0': _L2_gnn_in['b0'], 'L2_gnn_W1': _L2_gnn_in['W1'], 'L2_gnn_b1': _L2_gnn_in['b1'], 'L2_gnn_W2': _L2_gnn_in['W2'], 'L2_gnn_b2': _L2_gnn_in['b2'], 'L2_ffn_W1': _L2_ffn_in['W1'], 'L2_ffn_b1': _L2_ffn_in['b1'], 'L2_ffn_Wg': _L2_ffn_in['Wg'], 'L2_ffn_bg': _L2_ffn_in['bg'], 'L2_ffn_Wd': _L2_ffn_in['Wd'], 'L2_ffn_bd': _L2_ffn_in['bd'], 'L3_gnn_Wt': _L3_gnn_in['Wt'], 'L3_gnn_bt': _L3_gnn_in['bt'], 'L3_gnn_Wq': _L3_gnn_in['Wq'], 'L3_gnn_bq': _L3_gnn_in['bq'], 'L3_gnn_Wk': _L3_gnn_in['Wk'], 'L3_gnn_bk': _L3_gnn_in['bk'], 'L3_gnn_Wv': _L3_gnn_in['Wv'], 'L3_gnn_bv': _L3_gnn_in['bv'], 'L3_gnn_We': _L3_gnn_in['We'], 'L3_gnn_Wskip': _L3_gnn_in['Wskip'], 'L3_gnn_bskip': _L3_gnn_in['bskip'], 'L3_ffn_router_w': _L3_ffn_in['router_w'], 'L3_ffn_w1': _L3_ffn_in['w1'], 'L3_ffn_b1': _L3_ffn_in['b1'], 'L3_ffn_w2': _L3_ffn_in['w2'], 'L3_ffn_b2': _L3_ffn_in['b2']}

def reference(x, src, dst, edge_attr_128, edge_attr_18, edge_attr_256, edge_attr_54, edge_type_2, edge_type_8, edge_weight, node_type_2, node_vec, L0_gnn_w_f1a, L0_gnn_w_f1b, L0_gnn_w_f2a, L0_gnn_w_f2b, L0_gnn_c1_wl, L0_gnn_c1_bl, L0_gnn_c1_wr, L0_gnn_c2_wl, L0_gnn_c2_bl, L0_gnn_c2_wr, L0_gnn_lin1_w, L0_gnn_lin1_b, L0_gnn_lin2_w, L0_gnn_lin2_b, L0_gnn_cat_w, L0_gnn_cat_b, L0_gnn_gn_w, L0_gnn_gn_b, L0_gnn_gn_ms, L0_ffn_Wr, L0_ffn_br, L0_ffn_W1, L0_ffn_b1, L0_ffn_g1, L0_ffn_be1, L0_ffn_m1, L0_ffn_v1, L0_ffn_W2, L0_ffn_b2, L0_ffn_g2, L0_ffn_be2, L0_ffn_m2, L0_ffn_v2, L0_ffn_Wo, L0_ffn_bo, L1_gnn_W, L1_gnn_attn_src, L1_gnn_attn_dst, L1_ffn_W_fx, L1_ffn_b_fx, L1_ffn_W_x, L1_ffn_b_x, L1_ffn_W_slice, L1_ffn_b_slice, L1_ffn_W_q, L1_ffn_W_k, L1_ffn_W_v, L1_ffn_W_out, L1_ffn_b_out, L1_ffn_temperature, L2_gnn_W0, L2_gnn_b0, L2_gnn_W1, L2_gnn_b1, L2_gnn_W2, L2_gnn_b2, L2_ffn_W1, L2_ffn_b1, L2_ffn_Wg, L2_ffn_bg, L2_ffn_Wd, L2_ffn_bd, L3_gnn_Wt, L3_gnn_bt, L3_gnn_Wq, L3_gnn_bq, L3_gnn_Wk, L3_gnn_bk, L3_gnn_Wv, L3_gnn_bv, L3_gnn_We, L3_gnn_Wskip, L3_gnn_bskip, L3_ffn_router_w, L3_ffn_w1, L3_ffn_b1, L3_ffn_w2, L3_ffn_b2):
    import jax
    import jax.numpy as jnp

    def _L0_gnn_ref(x, gate_edge, feature1, feature2, edge_index, batch, w_f1a, w_f1b, w_f2a, w_f2b, c1_wl, c1_bl, c1_wr, c2_wl, c2_bl, c2_wr, lin1_w, lin1_b, lin2_w, lin2_b, cat_w, cat_b, gn_w, gn_b, gn_ms):
        import jax, jax.numpy as jnp
        import numpy as np
        N, E, C, MID = (625, 10000, 256, 64)
        NR, NS = (6, 3)
        F1_IN = NR * NS * NS
        F2_IN = NR * NS
        G = 64
        EPS = 1e-05
        NEG_SLOPE = 0.1

        def leaky(v):
            return jnp.where(v > 0, v, NEG_SLOPE * v)
        src, dst = (edge_index[0], edge_index[1])
        f1 = feature1 @ w_f1a @ w_f1b * gate_edge
        h1 = jax.ops.segment_sum(x[src] * f1, dst, num_segments=N)
        h1 = h1 @ c1_wl + c1_bl + x @ c1_wr
        h1 = leaky(h1 @ lin1_w + lin1_b)
        _dead = feature2 @ w_f2a @ w_f2b
        f2 = f1 * gate_edge
        h2 = jax.ops.segment_sum(x[src] * f2, dst, num_segments=N)
        h2 = h2 @ c2_wl + c2_bl + x @ c2_wr
        h2 = leaky(h2 @ lin2_w + lin2_b)
        h = jnp.concatenate([h1, h2], axis=1) @ cat_w + cat_b
        cnt = jnp.maximum(jax.ops.segment_sum(jnp.ones((N,), h.dtype), batch, num_segments=G), 1.0)[:, None]
        mean = jax.ops.segment_sum(h, batch, num_segments=G) / cnt
        out = h - mean[batch] * gn_ms
        var = jax.ops.segment_sum(out * out, batch, num_segments=G) / cnt
        std = jnp.sqrt(var + EPS)[batch]
        return gn_w * out / std + gn_b

    def _L0_ffn_ref(x, Wr, br, W1, b1, g1, be1, m1, v1, W2, b2, g2, be2, m2, v2, Wo, bo):
        import jax, jax.numpy as jnp
        import numpy as np
        BN_EPS = 0.001

        def _bn(h, g, b, m, v):
            return g * (h - m) * jax.lax.rsqrt(v + BN_EPS) + b
        feat = jnp.mean(x, axis=0)
        w = jax.nn.softmax(feat @ Wr + br, axis=-1)
        h = jnp.einsum('bfd,edh->bfeh', x, W1) + b1
        h = jax.nn.relu(_bn(h, g1, be1, m1, v1))
        h = jnp.einsum('bfeh,ehk->bfek', h, W2) + b2
        h = jax.nn.relu(_bn(h, g2, be2, m2, v2))
        y = jnp.einsum('bfeh,ehd->bfed', h, Wo) + bo
        return jnp.einsum('bfed,fe->bfd', y, w)

    def _L1_gnn_ref(x, W, attn_src, attn_dst, edge_index, edge_type):
        import jax, jax.numpy as jnp
        import numpy as np
        N, E, R, H, D = (30000, 9375, 8, 8, 32)
        IN_F = 256
        NEG_SLOPE = 0.2
        n = x.shape[0]
        r = W.shape[0]
        h, d = attn_src.shape
        h_all = jnp.einsum('nf,rof->rno', x, W).reshape(r, n, h, d)
        src, dst = (edge_index[0], edge_index[1])
        h_src = h_all[edge_type, src]
        h_dst = h_all[edge_type, dst]
        scores = jnp.einsum('ehd,hd->eh', h_src, attn_src) + jnp.einsum('ehd,hd->eh', h_dst, attn_dst)
        scores = jnp.where(scores > 0, scores, NEG_SLOPE * scores)
        amax = jnp.maximum(jax.ops.segment_max(scores, dst, num_segments=n), 0.0)
        w = jnp.exp(scores - amax[dst])
        denom = jax.ops.segment_sum(w, dst, num_segments=n) + 1e-12
        w = w / denom[dst]
        msg = h_src * w[..., None]
        out = jax.ops.segment_sum(msg, dst, num_segments=n)
        return out.reshape(n, h * d)

    def _L1_ffn_ref(x, W_fx, b_fx, W_x, b_x, W_slice, b_slice, W_q, W_k, W_v, W_out, b_out, temperature):
        import jax, jax.numpy as jnp
        import numpy as np
        DIM = 256
        H = 8
        D = 64
        G = 64
        INNER = H * D
        SCALE = D ** (-0.5)
        B, N, _ = x.shape
        fx_mid = (x @ W_fx + b_fx).reshape(B, N, H, D).transpose(0, 2, 1, 3)
        x_mid = (x @ W_x + b_x).reshape(B, N, H, D).transpose(0, 2, 1, 3)
        temp = jnp.clip(temperature, 0.1, 5.0)
        slice_weights = jax.nn.softmax((x_mid @ W_slice + b_slice) / temp, axis=-1)
        slice_norm = slice_weights.sum(axis=2)
        slice_token = jnp.einsum('bhnc,bhng->bhgc', fx_mid, slice_weights)
        slice_token = slice_token / (slice_norm[..., None] + 1e-05)
        q = slice_token @ W_q
        k = slice_token @ W_k
        v = slice_token @ W_v
        attn = jax.nn.softmax(jnp.einsum('bhgc,bhkc->bhgk', q, k) * SCALE, axis=-1)
        out_slice = jnp.einsum('bhgk,bhkc->bhgc', attn, v)
        out_x = jnp.einsum('bhgc,bhng->bhnc', out_slice, slice_weights)
        out_x = out_x.transpose(0, 2, 1, 3).reshape(B, N, INNER)
        return out_x @ W_out + b_out

    def _L2_gnn_ref(node_feature, W0, b0, W1, b1, W2, b2, src, dst, edge_types, node_types):
        import jax, jax.numpy as jnp
        import numpy as np
        N, D, E = (50000, 256, 12500)
        T = 2
        H = 512
        ETYPES = (0, 1)
        NTYPES = (0, 1)
        agg = jnp.zeros_like(node_feature)
        for et in ETYPES:
            w = (edge_types == et).astype(node_feature.dtype)
            msg = jax.ops.segment_sum(node_feature[src] * w[:, None], dst, num_segments=node_feature.shape[0])
            recv = jax.ops.segment_sum(w, dst, num_segments=node_feature.shape[0]) > 0
            agg = jnp.where(recv[:, None], msg, agg)
        inp = jnp.concatenate([agg, node_feature], axis=-1)
        out = node_feature
        for t in NTYPES:
            h = jax.nn.relu(inp @ W0[t] + b0[t])
            h = jax.nn.relu(h @ W1[t] + b1[t])
            y = h @ W2[t] + b2[t]
            out = jnp.where((node_types == t)[:, None], y, out)
        return out

    def _L2_ffn_ref(x, W1, b1, Wg, bg, Wd, bd):
        import jax, jax.numpy as jnp
        import numpy as np
        C = 256
        HID = 1024
        E = 8
        TEMP = 1.0
        orig_shape = x.shape
        xf = x.reshape(-1, orig_shape[-1])
        H = jax.nn.gelu(xf @ W1 + b1, approximate=False)
        probs = jax.nn.softmax((H @ Wg + bg) / TEMP, axis=-1)
        assign = jnp.argmax(probs, axis=-1)
        out = jnp.zeros_like(xf)
        for e in range(Wd.shape[0]):
            y = H @ Wd[e] + bd[e]
            sel = (assign == e)[:, None]
            out = out + jnp.where(sel, probs[:, e:e + 1] * y, 0.0)
        return out.reshape(orig_shape)

    def _L3_gnn_ref(x, last_update, t, msg, edge_index, Wt, bt, Wq, bq, Wk, bk, Wv, bv, We, Wskip, bskip):
        import jax, jax.numpy as jnp
        import numpy as np
        N, E = (50000, 12500)
        IN_CH, OUT_CH, MSG_DIM, TIME_DIM = (256, 256, 128, 128)
        HEADS = 2
        C = OUT_CH // HEADS
        EDGE_DIM = MSG_DIM + TIME_DIM
        n = x.shape[0]
        src, dst = (edge_index[0], edge_index[1])
        rel_t = last_update[src] - t
        rel_t_enc = jnp.cos(rel_t[:, None] * Wt[0][None, :] + bt)
        edge_attr = jnp.concatenate([rel_t_enc, msg], axis=-1)
        q = (x @ Wq + bq).reshape(n, HEADS, C)
        k = (x @ Wk + bk).reshape(n, HEADS, C)
        v = (x @ Wv + bv).reshape(n, HEADS, C)
        e = (edge_attr @ We).reshape(-1, HEADS, C)
        key_j = k[src] + e
        alpha = jnp.einsum('ehc,ehc->eh', q[dst], key_j) / jnp.sqrt(jnp.float32(C))
        amax = jax.ops.segment_max(alpha, dst, num_segments=n)
        alpha = jnp.exp(alpha - amax[dst])
        asum = jax.ops.segment_sum(alpha, dst, num_segments=n)
        alpha = alpha / (asum[dst] + 1e-16)
        out_e = (v[src] + e) * alpha[..., None]
        out = jax.ops.segment_sum(out_e, dst, num_segments=n).reshape(n, HEADS * C)
        out = out + (x @ Wskip + bskip)
        return out

    def _L3_ffn_ref(input_embeddings, router_w, w1, b1, w2, b2):
        import jax, jax.numpy as jnp
        import numpy as np
        NUM_EXPERTS = 8
        TOP_K = 2
        B, S, D = (8, 256, 256)

        def _moe(tokens, router_w, w1, b1, w2, b2):
            N = tokens.shape[0]
            E = router_w.shape[0]
            logits = tokens.astype(jnp.float32) @ router_w.astype(jnp.float32).T
            probs = jax.nn.softmax(logits, axis=-1)
            rw, re = jax.lax.top_k(probs, TOP_K)
            if TOP_K > 1:
                rw = rw / jnp.maximum(rw.sum(-1, keepdims=True), 1e-12)
            rw = rw.astype(tokens.dtype)
            combine = jnp.zeros((N, E), tokens.dtype).at[jnp.arange(N)[:, None], re].set(rw)
            out = tokens
            for e in range(E):
                h = jax.nn.gelu(tokens @ w1[e] + b1[e], approximate=False)
                y = h @ w2[e] + b2[e]
                out = out + combine[:, e:e + 1] * y
            return out
        b, s, d = input_embeddings.shape
        tokens = input_embeddings.reshape(b * s, d)
        return _moe(tokens, router_w, w1, b1, w2, b2).reshape(b, s, d)
    edge_index = jnp.stack([src, dst])
    batch0 = jnp.zeros((625,), jnp.int32)
    x = x + _L0_gnn_ref(_layernorm(x, axis=-1), edge_attr_256, edge_attr_54, edge_attr_18, edge_index, batch0, L0_gnn_w_f1a, L0_gnn_w_f1b, L0_gnn_w_f2a, L0_gnn_w_f2b, L0_gnn_c1_wl, L0_gnn_c1_bl, L0_gnn_c1_wr, L0_gnn_c2_wl, L0_gnn_c2_bl, L0_gnn_c2_wr, L0_gnn_lin1_w, L0_gnn_lin1_b, L0_gnn_lin2_w, L0_gnn_lin2_b, L0_gnn_cat_w, L0_gnn_cat_b, L0_gnn_gn_w, L0_gnn_gn_b, L0_gnn_gn_ms)
    x = x + _L0_ffn_ref(_layernorm(x, axis=-1)[None], L0_ffn_Wr, L0_ffn_br, L0_ffn_W1, L0_ffn_b1, L0_ffn_g1, L0_ffn_be1, L0_ffn_m1, L0_ffn_v1, L0_ffn_W2, L0_ffn_b2, L0_ffn_g2, L0_ffn_be2, L0_ffn_m2, L0_ffn_v2, L0_ffn_Wo, L0_ffn_bo)[0]
    x = x + _L1_gnn_ref(_layernorm(x, axis=-1), L1_gnn_W, L1_gnn_attn_src, L1_gnn_attn_dst, edge_index, edge_type_8)
    x = x + _L1_ffn_ref(_layernorm(x, axis=-1)[None], L1_ffn_W_fx, L1_ffn_b_fx, L1_ffn_W_x, L1_ffn_b_x, L1_ffn_W_slice, L1_ffn_b_slice, L1_ffn_W_q, L1_ffn_W_k, L1_ffn_W_v, L1_ffn_W_out, L1_ffn_b_out, L1_ffn_temperature)[0]
    x = x + _L2_gnn_ref(_layernorm(x, axis=-1), L2_gnn_W0, L2_gnn_b0, L2_gnn_W1, L2_gnn_b1, L2_gnn_W2, L2_gnn_b2, src, dst, edge_type_2, node_type_2)
    x = x + _L2_ffn_ref(_layernorm(x, axis=-1)[None], L2_ffn_W1, L2_ffn_b1, L2_ffn_Wg, L2_ffn_bg, L2_ffn_Wd, L2_ffn_bd)[0]
    x = x + _L3_gnn_ref(_layernorm(x, axis=-1), node_vec, edge_weight, edge_attr_128, edge_index, L3_gnn_Wt, L3_gnn_bt, L3_gnn_Wq, L3_gnn_bq, L3_gnn_Wk, L3_gnn_bk, L3_gnn_Wv, L3_gnn_bv, L3_gnn_We, L3_gnn_Wskip, L3_gnn_bskip)
    x = x + _L3_ffn_ref(_layernorm(x, axis=-1)[None], L3_ffn_router_w, L3_ffn_w1, L3_ffn_b1, L3_ffn_w2, L3_ffn_b2)[0]
    return x

_drawn_inputs = setup_inputs


def setup_inputs(seed=0):
    import zlib

    import numpy as np

    out = dict(_drawn_inputs(seed))
    spreads = {'L0_gnn_c1_bl': (0.0, 0.676),
     'L0_gnn_c2_bl': (0.0, 0.798),
     'L0_gnn_lin1_b': (0.0, 0.692),
     'L0_gnn_lin2_b': (0.0, 0.686),
     'L0_gnn_cat_b': (0.0, 0.499),
     'L0_gnn_gn_w': (1.0, 0.2),
     'L0_gnn_gn_b': (0.0, 0.1),
     'L0_gnn_gn_ms': (1.0, 0.2),
     'L0_ffn_br': (0.0, 0.1),
     'L0_ffn_b1': (0.0, 0.1),
     'L0_ffn_g1': (1.0, 0.2),
     'L0_ffn_be1': (0.0, 0.1),
     'L0_ffn_m1': (0.0, 0.1),
     'L0_ffn_v1': (1.0, 0.2),
     'L0_ffn_b2': (0.0, 0.1),
     'L0_ffn_g2': (1.0, 0.2),
     'L0_ffn_be2': (0.0, 0.1),
     'L0_ffn_m2': (0.0, 0.1),
     'L0_ffn_v2': (1.0, 0.2),
     'L0_ffn_bo': (0.0, 0.1),
     'L1_ffn_b_fx': (0.0, 0.1),
     'L1_ffn_b_x': (0.0, 0.589),
     'L1_ffn_b_slice': (0.0, 0.782),
     'L1_ffn_b_out': (0.0, 0.1),
     'L1_ffn_temperature': (0.5, 0.6),
     'L2_gnn_b0': (0.0, 0.299),
     'L2_gnn_b1': (0.0, 0.1),
     'L2_gnn_b2': (0.0, 0.1),
     'L2_ffn_b1': (0.0, 0.792),
     'L2_ffn_bg': (0.0, 0.508),
     'L2_ffn_bd': (0.0, 0.652),
     'L3_ffn_b1': (0.0, 0.587),
     'L3_ffn_b2': (0.0, 0.402)}
    factors = {'edge_weight': 8.0,
     'node_vec': 8.0,
     'L1_ffn_W_slice': 2.999,
     'L1_ffn_W_q': 8.0,
     'L1_ffn_W_k': 8.0,
     'L2_ffn_W1': 4.292,
     'L2_ffn_Wg': 4.801,
     'L2_ffn_Wd': 4.912,
     'L3_gnn_Wt': 8.0,
     'L3_gnn_bt': 24.595,
     'L3_gnn_bq': 17.664,
     'L3_gnn_bk': 200.0,
     'L3_gnn_bv': 3.746,
     'L3_gnn_bskip': 4.161}
    for name, (base, spread) in spreads.items():
        noise = np.random.default_rng([zlib.crc32(name.encode()), seed]).standard_normal(out[name].shape)
        drawn = base * np.exp(spread * noise) if base else spread * noise
        out[name] = jnp.asarray(drawn.astype(out[name].dtype))
    for name, factor in factors.items():
        out[name] = (out[name] * factor).astype(out[name].dtype)
    return out
```

```python
import numpy as np
import concourse.bass as bass
from concourse import mybir
from contextlib import ExitStack

LAYERS = 8

N, C, E = 625, 256, 20000
P, W = 125, 5
TE = E // P
EP = 128
T = (E + W * (EP - 1)) // EP
U = 6
T += -T % U
TH = T // 2
NR, NH, HD = 8, 8, 32
KVW = 2 * C + 1
PAD = 1.0e6
BIG = 1.0e30
HALVES = [(0, 320), (320, 305)]


def rowsplit(a):
    k = a.shape[0] // 128
    return a.reshape(k, 128, -1).transpose(1, 0, 2).reshape(128, -1)


def stack(a):
    e, r, m = a.shape
    return a.reshape(e, r // 128, 128, m).transpose(2, 0, 1, 3).reshape(128, -1)


def twice(a):
    z = np.zeros((128, 128), a.dtype)
    z[:64, :64] = a
    z[64:, 64:] = a
    return z


def per_row(a, rows=128):
    return np.broadcast_to(a.reshape(1, -1), (rows, a.size))


def blobs(i):
    def attn_blocks():
        z = np.zeros((C, 16), np.float32)
        for h in range(NH):
            z[h * HD:(h + 1) * HD, h] = i["L1_gnn_attn_src"][h]
            z[h * HD:(h + 1) * HD, 8 + h] = i["L1_gnn_attn_dst"][h]
        return rowsplit(z)

    row = lambda a: a.reshape(1, -1)
    col = lambda a: rowsplit(a.reshape(-1, 1))
    b = [None] * 8
    b[0] = [("f1aT", i["L0_gnn_w_f1a"].T), ("f1b", i["L0_gnn_w_f1b"])]
    b[0] += [(n, rowsplit(i["L0_gnn_" + n])) for n in ("c1_wl", "c1_wr", "c2_wl", "c2_wr", "lin1_w", "lin2_w", "cat_w")]
    b[0] += [(n, col(i["L0_gnn_" + n])) for n in ("c1_bl", "c2_bl", "lin1_b", "lin2_b", "cat_b", "gn_w", "gn_b", "gn_ms")]
    b[1] = [("Wr", rowsplit(i["L0_ffn_Wr"])), ("br", row(i["L0_ffn_br"]))]
    b[1] += [(n, stack(i["L0_ffn_" + n])) for n in ("W1", "W2", "Wo")]
    b[1] += [(n, col(i["L0_ffn_" + n])) for n in ("b1", "g1", "be1", "m1", "v1", "b2", "g2", "be2", "m2", "v2")]
    b[1] += [("bo", i["L0_ffn_bo"])]
    w = i["L1_gnn_W"]
    b[2] = [("WT", stack(w.transpose(0, 2, 1))), ("attn", attn_blocks()), ("Wn", stack(w))]
    b[3] = [("W_fx", rowsplit(i["L1_ffn_W_fx"])), ("b_fx", row(i["L1_ffn_b_fx"])),
            ("W_x", rowsplit(i["L1_ffn_W_x"])), ("b_x", col(i["L1_ffn_b_x"])),
            ("W_slice", twice(i["L1_ffn_W_slice"])), ("b_slice", row(np.tile(i["L1_ffn_b_slice"], 8))),
            ("W_q", twice(i["L1_ffn_W_q"])), ("W_k", twice(i["L1_ffn_W_k"])), ("W_v", twice(i["L1_ffn_W_v"])),
            ("W_out", rowsplit(i["L1_ffn_W_out"])), ("b_out", row(i["L1_ffn_b_out"])),
            ("temp", per_row(i["L1_ffn_temperature"]))]
    b[4] = [("W0", stack(i["L2_gnn_W0"])), ("W1", stack(i["L2_gnn_W1"])), ("W2", stack(i["L2_gnn_W2"])),
            ("b0", col(i["L2_gnn_b0"])), ("b1", col(i["L2_gnn_b1"])), ("b2", row(i["L2_gnn_b2"]))]
    b[5] = [("W1", rowsplit(i["L2_ffn_W1"])), ("b1", col(i["L2_ffn_b1"])), ("Wg", rowsplit(i["L2_ffn_Wg"])),
            ("bg", row(i["L2_ffn_bg"])), ("Wd", stack(i["L2_ffn_Wd"])), ("bd", i["L2_ffn_bd"])]
    b[6] = [(n, rowsplit(i["L3_gnn_" + n])) for n in ("Wq", "Wk", "Wv", "Wskip", "We")]
    b[6] += [(n, row(i["L3_gnn_" + n])) for n in ("bq", "bk", "bv", "bskip")]
    b[6] += [("Wt", per_row(i["L3_gnn_Wt"])), ("bt", per_row(i["L3_gnn_bt"]))]
    b[7] = [("router", rowsplit(i["L3_ffn_router_w"].T)), ("w1", stack(i["L3_ffn_w1"])), ("b1", col(i["L3_ffn_b1"])),
            ("w2", stack(i["L3_ffn_w2"])), ("b2", i["L3_ffn_b2"])]
    return b


def blob_places(parts):
    places, at = {}, 0
    for name, a in parts:
        places[name] = (at, a.shape[0], a.shape[1])
        at += a.shape[1]
    return places, at


def build(nc, d, places, widths):
    f32, i32, bf16, f16 = mybir.dt.float32, mybir.dt.int32, mybir.dt.bfloat16, mybir.dt.float16
    ALU, ACT, AX = mybir.AluOpType, mybir.ActivationFunctionType, mybir.AxisListType
    ds = bass.ds
    ctx = ExitStack()
    with ctx:
        def sb(name, shape, dt=f32):
            return ctx.enter_context(nc.sbuf_tensor(name, shape, dt))

        sems = {}

        def sem(name):
            if name not in sems:
                sems[name] = ctx.enter_context(nc.semaphore(name))
            return sems[name]

        X = sb("X", [P, W, C])
        XN = sb("XN", [P, W, C])
        XNT = sb("XNT", [128, 2, N])
        ident = sb("ident", [128, 128])
        ones = sb("ones", [128, 128])
        iota = sb("iota", [128, T])
        zeros = sb("zeros", [128, 256])
        srt = sb("srt", [128, T, 8], i32)
        dloc = sb("dloc", [128, T])
        wid = sb("wid", [128, T])
        widi = sb("widi", [128, T], i32)
        idx_hs = sb("idx_hs", [128, T], i32)
        idx_hd = sb("idx_hd", [128, T], i32)
        typ = sb("typ", [128, T, 2])
        recv1 = sb("recv1", [P, W])
        ixb = sb("ixb", [128, 2 * U], i32)
        oh = sb("oh", [128, 3, P])
        stats = sb("stats", [P, W, 6])
        aggr = sb("aggr", [P, W, 2])
        rstd = sb("rstd", [P, W])
        small = sb("small", [128, 40])
        A_SIZE, B_SIZE = 21700, 23904
        arena = [sb("arena_gnn", [128, A_SIZE]), sb("arena_ffn", [128, B_SIZE])]
        size = [A_SIZE, B_SIZE]
        PS = [ctx.enter_context(nc.psum_tensor(f"PS{b}", [128, 512], f32)) for b in range(8)]

        def dram(name, shape, dt=f32):
            return nc.dram_tensor(name, shape, dt).ap()
        rec_tab = dram("rec_tab", (EP * T, 8), i32)
        edge_tab = dram("edge_tab", (E, 310))
        xn_tab = dram("xn_tab", (N, C))
        s_tab = dram("s_tab", (NR * N, 16))
        h_tab = dram("h_tab", (NR * N, C))
        kv_tab = dram("kv_tab", (N, KVW))
        ve_tab = dram("ve_tab", (T, EP, C))

        class Layer:
            def __init__(self, n, blob=True):
                self.n, self.ar = n, arena[n % 2]
                self.at = widths[n] if blob else 0

            def w(self, name, **dims):
                at, rows, cols = places[self.n][name]
                ap = self.ar[0:rows, at:at + cols]
                if not dims:
                    return ap
                keys = " ".join(dims)
                return ap.rearrange(f"p ({keys} m) -> p {keys} m", **dims)

            def work(self, rows, cols, at=None, **dims):
                if at is None:
                    at = self.at
                    self.at += cols
                    assert self.at <= size[self.n % 2], (self.n, self.at)
                ap = self.ar[0:rows, at:at + cols]
                if not dims:
                    return ap
                keys = " ".join(dims)
                return ap.rearrange(f"p ({keys} m) -> p {keys} m", **dims)

        groups = {}
        order = []
        emptied = {"act": 0, "dve": 0}

        def plan(stage, count, engine):
            groups[stage] = (len(order), count, engine)
            for _ in range(count):
                emptied[engine] += 1
                order.append((engine, emptied[engine]))

        def bank(stage, u):
            return PS[(groups[stage][0] + u) % 8]

        def wait_empty(eng, stage, u=None):
            first, count, _ = groups[stage]
            engine, k = order[first + (count - 1 if u is None else u)]
            eng.wait_ge(sem("emptied_by_" + engine), k)

        def wait_bank(eng, stage, u):
            g = groups[stage][0] + u
            if g >= 8:
                eng.wait_ge(sem("emptied_by_" + order[g - 8][0]), order[g - 8][1])

        def wait_full(eng, stage, u):
            eng.wait_ge(sem("product_ready"), groups[stage][0] + u + 1)

        def full(ins):
            ins.then_inc(sem("product_ready"), 1)

        def out_by(ins, engine):
            ins.then_inc(sem("emptied_by_" + engine), 1)

        EXPERTS = {1: ("mlp1", "mlp2", "mlpo"), 5: ("mlpo",), 7: ("mlp1", "mlpo")}

        def experts(kinds):
            return [(kind, s - lag) for s in range(8 + len(kinds) - 1)
                    for lag, kind in enumerate(kinds) if 0 <= s - lag < 8]

        plan("sort_total", 2, "act")


        for l in range(8):
            plan(f"xnt{l}", W, "act")
            if l == 0:
                plan("l0_wc", 1, "act")
                plan("l0_accT", W, "act")
                for s in (1, 2):
                    plan(f"l0_conv{s}", 4, "act")
                    plan(f"l0_lin{s}", 4, "act")
                plan("l0_cat", 4, "act")
                plan("l0_back", W, "dve")
            if l == 1:
                plan("gate1", W, "dve")
                for kind, e in experts(EXPERTS[l]):
                    plan(f"{kind}_{l}_{e}", W if kind == "mlpo" else 4, "dve" if kind == "mlpo" else "act")
                plan(f"coefT{l}", W, "act")
                plan(f"bias{l}", W, "dve")
            if l == 2:
                plan("l1_v", 8, "act")
                plan("l1_s", W, "act")
                for r in range(NR):
                    plan(f"l1_h{r}", W, "act")
                plan("seg_dst0", 2, "act")
                plan("seg_ends0", 1, "act")
                plan("scoreT0", 2 * NH, "act")
                plan("ends0", 4, "act")
                plan("carry0", 4, "act")
                plan("amax0", 2 * NH, "act")
            if l == 3:
                plan("xmT", 8, "act")
                plan("fx", W, "act")
                plan("slice", W, "dve")
                plan("swT", W, "act")
                plan("token", 4, "dve")
                for s in ("tokT", "qT", "kT", "v", "lg", "pT", "os"):
                    plan("t_" + s, 4, "dve" if s == "lg" else "act")
                plan("oxT", 8, "act")
                plan("l3_out", W, "dve")
            if l == 4:
                plan("aggT", W, "act")
                for t in range(2):
                    plan(f"g0_{t}", 8, "act")
                    plan(f"g1_{t}", 8, "act")
                    plan(f"g2_{t}", W, "dve")
            if l == 5:
                plan("hid", 16, "act")
                plan("gate5", W, "dve")
                for kind, e in experts(EXPERTS[l]):
                    plan(f"{kind}_{l}_{e}", W, "dve")
                plan(f"coefT{l}", W, "act")
                plan(f"bias{l}", W, "dve")
            if l == 6:
                for s in ("q", "k", "v"):
                    plan("l3_" + s, W, "act")
                plan("l3_skip", W, "dve")
                plan("seg_dst1", 2, "act")
                plan("seg_ends1", 1, "act")
                plan("scoreT1", 2 * 2, "act")
                plan("ends1", 4, "act")
                plan("carry1", 4, "act")
                plan("amax1", 2 * 2, "act")
            if l == 7:
                plan("gate7", W, "dve")
                for kind, e in experts(EXPERTS[l]):
                    plan(f"{kind}_{l}_{e}", W if kind == "mlpo" else 4, "dve" if kind == "mlpo" else "act")
                plan(f"coefT{l}", W, "act")
                plan(f"bias{l}", W, "dve")

        steps = {"vector": 0, "scalar": 0, "pool": 0}

        def linker(eng, name):
            def link(ins):
                steps[name] += 1
                ins.then_inc(sem(name + "_step"), 1)
                eng.wait_ge(sem(name + "_step"), steps[name])
            return link

        def tiles(eng, body, rest=0):
            for b in range(U):
                body(0, b)
            with eng.Fori(1, T // U) as i:
                for b in range(U):
                    body(i, b)
            for b in range(rest):
                body(T // U, b)

        def tile_at(i, b, lag=0):
            if isinstance(i, int) and not 0 <= i * U + b - lag < T:
                return None
            return i - (b < lag), i * U + (b - lag), (b - lag) % U

        def wait_over(eng, name, value):
            if not isinstance(value, int) or value > 0:
                eng.wait_ge(sem(name), value)

        srt_f = srt[:, :, :].bitcast(f32)
        dst_all = srt_f[:, :, 1]
        S = Layer(1, blob=False)
        iota_i = S.work(128, N).bitcast(i32)
        iota_n = S.work(128, N)
        dstz = S.work(128, T)
        raw = S.work(P, 5 * TE, f=5)
        raw_i = raw.bitcast(i32)
        dstf = S.work(P, TE)
        rec = S.work(P, TE * 8, t=TE)
        rec_i = rec.bitcast(i32)
        pads = S.work(128, T * 8, t=T)
        earlier = S.work(P, 2 * TE)
        rank = S.work(P, TE)
        junk = S.work(P, 2 * N)
        before = S.work(128, N)
        total = S.work(128, N)
        start = S.work(128, N)
        pos = S.work(P, TE)
        pos_i = S.work(P, TE).bitcast(i32)
        low_i = S.work(P, TE).bitcast(i32)
        rows_i = S.work(P, TE).bitcast(i32)
        low = S.work(P, TE)
        strict = S.work(P, 128)
        last_row = S.work(128, 128)
        oh16 = S.work(P, 2 * 314, b=2).bitcast(bf16)[:, :, 0:N]
        iota16 = S.work(P, 314).bitcast(f16)[:, 0:N]
        strict16 = S.work(P, 64).bitcast(bf16)
        recb = S.work(P, 4 * 8, b=4)
        zeros_16 = zeros[0:P, :].bitcast(bf16)
        sel0 = sb("sel0", [128, 8])
        sel127 = sb("sel127", [128, 8])
        ntype = sb("ntype", [P, W])
        ntype_i = sb("ntype_i", [P, W], i32)

        def sort_sync(sp):
            for n, name in enumerate(("dst", "src", "edge_type_8", "edge_type_2")):
                sp.dma_start(raw_i[:, n, :], d[name].rearrange("(p t) -> p t", p=P)).then_inc(sem("edges_loaded"), 16)
            sp.dma_start(raw[:, 4, :], d["edge_weight"].rearrange("(p t) -> p t", p=P)).then_inc(sem("edges_loaded"), 16)
            sp.dma_start(ntype_i[:, :], d["node_type_2"].rearrange("(w p) -> p w", p=P),
                         allow_slow_non_contiguous=True).then_inc(sem("edges_loaded"), 16)
            sp.dma_start(X[:, :, :], d["x"].rearrange("(w p) c -> p w c", p=P)).then_inc(sem("x_loaded"), 16)
            load_blob(sp, 0)
            sp.wait_ge(sem("pads_made"), 3)
            sp.dma_start(rec_tab.rearrange("(i t) f -> i t f", t=T), pads.bitcast(i32)).then_inc(sem("pads_written"), 16)
            sp.dma_start(edge_tab[:, 54:310], d["edge_attr_256"]).then_inc(sem("edge_tab_written"), 16)
            sp.dma_start(edge_tab[:, 0:54], d["edge_attr_54"]).then_inc(sem("edge_tab_written"), 16)
            sp.wait_ge(sem("xn_ready"), 1)
            sp.dma_start(xn_tab.rearrange("(w p) c -> p w c", p=P), XN[:, :, :]).then_inc(sem("xn_written"), 16)
            for b in range(4):
                sp.wait_ge(sem(f"record_scattered{b}"), 16 * TE // 4)
            sp.dma_start(srt[:, :, :], rec_tab.rearrange("(i t) f -> i t f", t=T)).then_inc(sem("sorted_loaded"), 16)
            sp.wait_ge(sem("sort_done"), 1)
            load_blob(sp, 1)

        def load_blob(sp, l):
            w = widths[l]
            for c in range(0, w, 4096):
                n = min(4096, w - c)
                sp.dma_start(arena[l % 2][:, c:c + n], d[f"blob{l}"][:, c:c + n]).then_inc(sem("blob_gnn" if l % 2 == 0 else "blob_ffn"), 16)

        def blob_count(l):
            return 16 * sum(-(-widths[k] // 4096) for k in range(l % 2, l + 1, 2))

        def wait_blob(eng, l):
            eng.wait_ge(sem("blob_gnn" if l % 2 == 0 else "blob_ffn"), blob_count(l))

        def sort_pool(pool):
            link = linker(pool, "pool")
            pool.memset(ones[:, :], 1.0)
            pool.memset(zeros[:, :], 0.0).then_inc(sem("constants"), 1)
            pool.iota(iota_i, pattern=[[1, N]], base=0, channel_multiplier=0).then_inc(sem("constants"), 1)
            pool.memset(rec_i[:, :, 6:8], 0)
            pool.iota(rec_i[:, :, 5], pattern=[[1, TE]], base=0, channel_multiplier=TE).then_inc(sem("constants"), 1)
            pool.memset(pads, 0.0).then_inc(sem("pads_made"), 1)
            pool.wait_ge(sem("pads_made"), 1)
            pool.memset(pads[:, :, 1], PAD).then_inc(sem("pads_made"), 1)
            pool.memset(pads[:, 0:1, 7], 0.0).then_inc(sem("pads_made"), 1)
            link(pool.memset(ident[:, :], 0.0))
            link(pool.affine_select(out=ident[:, :], in_=ident[:, :], compare_op=ALU.not_equal, fill=1.0, base=0,
                                    pattern=[[-1, 128]], channel_multiplier=1))
            link(pool.memset(strict, 1.0))
            link(pool.affine_select(out=strict, in_=strict, compare_op=ALU.is_gt, fill=0.0, base=0,
                                    pattern=[[1, 128]], channel_multiplier=-1))
            link(pool.memset(last_row, 0.0))
            link(pool.affine_select(out=last_row, in_=last_row, compare_op=ALU.not_equal, fill=1.0, base=-127,
                                    pattern=[[0, 128]], channel_multiplier=1))
            pool.tensor_copy(sel127[:, :], last_row[:, 0:8]).then_inc(sem("constants"), 1)
            link(pool.memset(sel0[:, :], 0.0))
            pool.affine_select(out=sel0[:, :], in_=sel0[:, :], compare_op=ALU.not_equal, fill=1.0, base=0,
                               pattern=[[0, 8]], channel_multiplier=1).then_inc(sem("constants"), 1)
            pool.wait_ge(sem("pads_written"), 16)
            pool.wait_ge(sem("places_ready"), 1)

            def scatter(i, b):
                t = i * 4 + b
                if not isinstance(i, int):
                    pool.wait_ge(sem(f"record_scattered{b}"), 16 * i)
                pool.tensor_copy(ixb[0:P, b:b + 1], rows_i[:, ds(t, 1)]).then_inc(sem("indices_copied"), 1)
                pool.tensor_copy(recb[:, b, :], rec[:, ds(t, 1), :].rearrange("p a f -> p (a f)")).then_inc(sem("indices_copied"), 1)
                pool.wait_ge(sem("indices_copied"), 2)
                pool.indirect_dma_start(rec_tab, bass.IndirectOffsetOnAxis(ap=ixb[0:P, b:b + 1], axis=0),
                                        recb[:, b, :].bitcast(i32), None).then_inc(sem(f"record_scattered{b}"), 16)
                pool.sem_inc(sem("indices_copied"), -2)

            for b in range(4):
                scatter(0, b)
            with pool.Fori(1, TE // 4) as i:
                for b in range(4):
                    scatter(i, b)

        def sort_vector(dve):
            link = linker(dve, "vector")
            dve.wait_ge(sem("constants"), 2)
            link(dve.tensor_copy(iota_n, iota_i))
            dve.tensor_copy(iota[:, :], iota_n[:, 0:T])
            dve.tensor_copy(iota16, iota_n[0:P, :])
            dve.wait_ge(sem("edges_loaded"), 96)
            dve.tensor_copy(ntype[:, :], ntype_i[:, :])
            link(dve.tensor_copy(dstf, raw_i[:, 0, :]))
            dve.wait_ge(sem("constants"), 5)
            dve.wait_ge(sem("pool_step"), 7)
            dve.tensor_copy(strict16, strict)
            dve.tensor_copy(rec_i[:, :, 0], raw_i[:, 1, :])
            dve.tensor_copy(rec[:, :, 1], dstf)
            dve.tensor_copy(rec_i[:, :, 2], raw_i[:, 2, :])
            dve.tensor_copy(rec_i[:, :, 3], raw_i[:, 3, :])
            dve.tensor_copy(rec[:, :, 4], raw[:, 4, :])
            def onehot(i, b):
                if not isinstance(i, int):
                    dve.wait_ge(sem("onehot_added"), i * 2 + b - 1)
                dve.tensor_scalar(oh16[:, b, :], iota16, dstf[:, ds(i * 2 + b, 1)], None, ALU.is_equal).then_inc(sem("onehot_ready"), 1)
            for b in range(2):
                onehot(0, b)
            with dve.Fori(1, TE // 2) as i:
                for b in range(2):
                    onehot(i, b)
            dve.memset(earlier[:, 0:TE], 1.0)
            link(dve.memset(earlier[:, TE:2 * TE], 0.0))

            def ranks(i, b):
                t = i * 2 + b
                if not isinstance(i, int):
                    dve.wait_ge(sem("ranked"), t - 1)
                dve.scalar_tensor_tensor(junk[0:P, TE * b:TE * b + TE], dstf, dstf[:, ds(t, 1)], earlier[:, ds(TE - t, TE)],
                                         ALU.is_equal, ALU.mult, accum_out=rank[:, ds(t, 1)]).then_inc(sem("ranked"), 1)
            for b in range(2):
                ranks(0, b)
            with dve.Fori(1, TE // 2) as i:
                for b in range(2):
                    ranks(i, b)
            dve.wait_ge(sem("ranked"), TE)
            wait_empty(dve, "sort_total")
            for w in range(W):
                c = slice(w * P, (w + 1) * P)
                ins = dve.tensor_tensor_scan(start[:, c], total[:, c], zeros[:, 0:P], 0.0, ALU.add, ALU.add)
            link(ins)
            count = start.rearrange("p (w n) -> p w n", w=W)[:, :, P - 1]
            wt, wt_i = small[:, 0:W], small[:, 8:8 + W].bitcast(i32)
            link(dve.tensor_scalar(wt_i, count, float(EP - 1), None, ALU.add))
            link(dve.tensor_scalar(wt_i, wt_i, 7, None, ALU.arith_shift_right))
            link(dve.tensor_copy(wt, wt_i))
            incl, wstart, wpos = small[:, 16:16 + W], small[:, 24:24 + W], small[:, 32:32 + W]
            link(dve.tensor_tensor_scan(incl, wt, zeros[:, 0:W], 0.0, ALU.add, ALU.add))
            link(dve.tensor_tensor(wstart, incl, wt, ALU.subtract))
            dve.tensor_scalar(wpos, wstart, float(EP), None, ALU.mult)
            link(dve.tensor_tensor(start, start, total, ALU.subtract))
            for w in range(W):
                c = slice(w * P, (w + 1) * P)
                ins = dve.tensor_scalar(start[:, c], start[:, c], wpos[:, w:w + 1], None, ALU.add)
            link(ins)
            link(dve.tensor_tensor(before, before, start, ALU.add))
            def find(i, b):
                t = i * 2 + b
                if not isinstance(i, int):
                    dve.wait_ge(sem("place_found"), t - 1)
                dve.scalar_tensor_tensor(junk[0:P, N * b:N * b + N], iota_n[0:P, :], dstf[:, ds(t, 1)], before[0:P, :],
                                         ALU.is_equal, ALU.mult, accum_out=pos[:, ds(t, 1)]).then_inc(sem("place_found"), 1)
            for b in range(2):
                find(0, b)
            with dve.Fori(1, TE // 2) as i:
                for b in range(2):
                    find(i, b)
            dve.wait_ge(sem("place_found"), TE)
            link(dve.tensor_tensor(pos, pos, rank, ALU.add))
            link(dve.tensor_copy(pos_i, pos))
            dve.tensor_scalar(low_i, pos_i, 127, None, ALU.bitwise_and)
            link(dve.tensor_scalar(pos_i, pos_i, 7, None, ALU.arith_shift_right))
            dve.tensor_copy(low, low_i)
            link(dve.tensor_copy(pos, pos_i))
            dve.scalar_tensor_tensor(rows_i, low, float(T), pos, ALU.mult, ALU.add).then_inc(sem("places_ready"), 1)
            link(dve.memset(wid[:, :], 0.0))
            for w in range(1, W):
                link(dve.scalar_tensor_tensor(wid[:, :], iota[:, 0:T], wstart[:, w:w + 1], wid[:, :], ALU.is_ge, ALU.add))
            dve.tensor_copy(widi[:, :], wid[:, :])
            layer_norm_vector(dve, 0, link)
            dve.wait_ge(sem("sorted_loaded"), 16)
            link(dve.scalar_tensor_tensor(dloc[:, :], wid[:, :], -float(P), dst_all, ALU.mult, ALU.add))
            link(dve.tensor_scalar(dstz, dst_all, float(N), None, ALU.is_lt))
            link(dve.tensor_tensor(dstz, dstz, dst_all, ALU.mult))
            dve.scalar_tensor_tensor(idx_hs[:, :], srt[:, :, 2], float(N), srt[:, :, 0], ALU.mult, ALU.add)
            dve.scalar_tensor_tensor(idx_hd[:, :], srt[:, :, 2], float(N), dstz, ALU.mult, ALU.add)
            for k in range(2):
                ins = dve.tensor_scalar(typ[:, :, k], srt[:, :, 3], float(k), None, ALU.is_equal)
            ins.then_inc(sem("sort_done"), 1)

        def sort_tensor(pe):
            pe.wait_ge(sem("onehot_ready"), 1)
            for b, n in ((0, 512), (1, N - 512)):
                pe.matmul(PS[b][:, 0:n], zeros_16[:, 0:128], zeros_16[:, 0:n], start=True, stop=False)

            def add(t, b):
                pe.wait_ge(sem("onehot_ready"), t + 1)
                pe.matmul(PS[0][:, :], strict16, oh16[:, b, 0:512], start=False, stop=False)
                pe.matmul(PS[1][:, 0:N - 512], strict16, oh16[:, b, 512:N], start=False, stop=False).then_inc(sem("onehot_added"), 1)
            with pe.Fori(0, TE // 2) as i:
                for b in range(2):
                    add(i * 2 + b, b)
            for b, n in ((0, 512), (1, N - 512)):
                ins = pe.matmul(PS[b][:, 0:n], zeros_16[:, 0:128], zeros_16[:, 0:n], start=False, stop=True)
            ins.then_inc(sem("histogram_ready"), 1)
            pe.wait_ge(sem("histogram_copied"), 2)
            for u, (c, n) in enumerate(((0, 512), (512, N - 512))):
                full(pe.matmul(bank("sort_total", u)[:, 0:n], last_row, before[:, c:c + n], start=True, stop=True))

        def sort_scalar(act):
            act.wait_ge(sem("histogram_ready"), 1)
            act.activation(before[:, 0:512], PS[0][:, :], ACT.Copy).then_inc(sem("histogram_copied"), 1)
            act.activation(before[:, 512:N], PS[1][:, 0:N - 512], ACT.Copy).then_inc(sem("histogram_copied"), 1)
            for u, (c, n) in enumerate(((0, 512), (512, N - 512))):
                wait_full(act, "sort_total", u)
                out_by(act.activation(total[:, c:c + n], bank("sort_total", u)[:, 0:n], ACT.Copy), "act")
            std_scalar(act, 0)

        def layer_norm_vector(dve, l, link):
            if l == 0:
                dve.wait_ge(sem("x_loaded"), 16)
            for w in range(W):
                ins = dve.bn_stats(stats[:, w, :], X[:, w, :])
            link(ins)
            for w in range(W):
                ins = dve.bn_aggr(aggr[:, w, :], stats[:, w, :])
            link(ins)
            dve.tensor_scalar(rstd[:, :], aggr[:, :, 1], 1e-5, None, ALU.add).then_inc(sem("variance_ready"), 1)
            dve.wait_ge(sem("deviation_ready"), l + 1)
            link(dve.reciprocal(rstd[:, :], rstd[:, :]))
            for w in range(W):
                ins = dve.tensor_scalar(XN[:, w, :], X[:, w, :], aggr[:, w, 0:1], rstd[:, w:w + 1], ALU.subtract, ALU.mult)
            ins.then_inc(sem("xn_ready"), 1)

        def std_scalar(act, l):
            act.wait_ge(sem("variance_ready"), l + 1)
            act.activation(rstd[:, :], rstd[:, :], ACT.Sqrt).then_inc(sem("deviation_ready"), 1)

        def turn(pe, stage, u, outs):
            wait_bank(pe, stage, u)
            for (c, m), a in outs:
                k = a.shape[0]
                ins = pe.transpose(bank(stage, u)[0:a.shape[1], c:c + k], a, ident[0:k, 0:k])
            full(ins)

        def turn_nodes(pe, stage, a, k):
            for w in range(W):
                turn(pe, stage, w, [((P * j, P), a[:, w, 128 * j:128 * j + 128]) for j in range(k)])

        def turned_nodes(act, stage, out, k):
            for w in range(W):
                wait_full(act, stage, w)
                out_by(act.activation(out[:, :, P * w:P * w + P],
                                      bank(stage, w)[:, 0:k * P].rearrange("p (k n) -> p k n", k=k), ACT.Copy), "act")

        def xnt_tensor(pe, l):
            pe.wait_ge(sem("xn_ready"), l + 1)
            turn_nodes(pe, f"xnt{l}", XN, 2)

        def xnt_scalar(act, l):
            turned_nodes(act, f"xnt{l}", XNT, 2)

        def lin(pe, stage, pairs, M):
            for m in range(M // 128):
                for h, (c, n) in enumerate(HALVES):
                    u = 2 * m + h
                    wait_bank(pe, stage, u)
                    todo = [(w[:, k, 128 * m:128 * m + 128], r[:, k, c:c + n]) for w, r in pairs for k in range(w.shape[1])]
                    for j, (w, r) in enumerate(todo):
                        ins = pe.matmul(bank(stage, u)[:, 0:n], w, r, start=j == 0, stop=j == len(todo) - 1)
                    full(ins)

        def lin_out(act, stage, out, M, func, bias=None, scale=1.0):
            for m in range(M // 128):
                for h, (c, n) in enumerate(HALVES):
                    u = 2 * m + h
                    wait_full(act, stage, u)
                    out_by(act.activation(out[:, m, c:c + n], bank(stage, u)[:, 0:n], func,
                                          bias=0.0 if bias is None else bias[:, m:m + 1],
                                          scale=scale if isinstance(scale, float) else scale[:, m:m + 1]), "act")

        def nodes(pe, stage, a, w, n, bias=None):
            for v in range(W):
                node_group(pe, stage, v, a, w, n, bias)

        def node_group(pe, stage, v, a, w, n, bias=None):
            wait_bank(pe, stage, v)
            K = w.shape[1]
            for k in range(K):
                ins = pe.matmul(bank(stage, v)[0:P, 0:n], a[:, k, P * v:P * v + P], w[:, k, :],
                                start=k == 0, stop=k == K - 1 and bias is None)
            if bias is not None:
                ins = pe.matmul(bank(stage, v)[0:P, 0:n], ones[0:1, 0:P], bias, start=False, stop=True)
            full(ins)

        def wait_x(dve, stage, v):
            dve.wait_ge(sem("emptied_by_dve"), order[groups[stage][0] + v][1] - W)

        def add_to_x(dve, stage, n=C):
            for v in range(W):
                wait_full(dve, stage, v)
                out_by(dve.tensor_tensor(X[:, v, :], bank(stage, v)[0:P, 0:n], X[:, v, :], ALU.add), "dve")

        def gathers(pool, loop, streams, free):
            def body(i, b):
                i, t, b = tile_at(i, b)
                wait_over(pool, free, t - U + 1)
                if isinstance(i, int):
                    for name, *_ in streams:
                        wait_over(pool, f"gathered_{name}{b}", LOOPS[name].index(loop) * (T // U) * 16)
                for k, (name, idx, table, buf) in enumerate(streams):
                    pool.tensor_copy(ixb[:, k * U + b:k * U + b + 1], idx[:, ds(t, 1)]).then_inc(sem("indices_copied"), 1)
                pool.wait_ge(sem("indices_copied"), len(streams))
                for k, (name, idx, table, buf) in enumerate(streams):
                    pool.indirect_dma_start(buf[:, b, :], None, table,
                                            bass.IndirectOffsetOnAxis(ap=ixb[:, k * U + b:k * U + b + 1], axis=0))\
                        .then_inc(sem(f"gathered_{name}{b}"), 16)
                pool.sem_inc(sem("indices_copied"), -len(streams))
            tiles(pool, body)

        LOOPS = {"a": ("l0", "l1s", "l1m", "l2", "l3"), "b": ("l0", "l1s", "l3")}

        def wait_gathered(eng, name, loop, i, b):
            eng.wait_ge(sem(f"gathered_{name}{b}"), (i + (LOOPS[name].index(loop) * (T // U) + 1)) * 16)

        def onehot_of(dve, t, slot):
            return dve.tensor_scalar(oh[:, slot, :], iota[:, 0:P], dloc[:, ds(t, 1)], None, ALU.is_equal)

        def accumulate(dve, loop, tile, acc, psum, n):
            i, t, b = tile
            w = dve.value_load(widi[0:1, ds(t, 1)], min_val=0, max_val=W - 1)
            dve.wait_ge(sem(loop + "_product"), t + 1)
            wait_over(dve, loop + "_summed", t)
            dve.tensor_tensor(acc[:, ds(w * n, n)], psum, acc[:, ds(w * n, n)], ALU.add).then_inc(sem(loop + "_summed"), 1)

        L0 = Layer(0)
        wc = L0.work(54, C)
        xg0 = L0.work(128, U * C, u=U)
        eg0 = L0.work(128, U * 310, u=U)
        f54T = L0.work(54, 2 * 128, u=2)
        gx0 = L0.work(128, 2 * C, u=2)
        msg0 = L0.work(128, 3 * 512, u=3)
        acc0 = L0.work(P, W * 512)
        accT = L0.work(128, 4 * N, k=4)
        conv = L0.work(128, 2 * N, k=2)
        linv = L0.work(128, 2 * N, k=2)
        hT = L0.work(128, 4 * N, k=4)
        catT = accT[:, 0:2, :]
        gnst = L0.work(128, 64)

        def l0_pool(pool):
            pool.wait_ge(sem("sort_done"), 1)
            pool.wait_ge(sem("xn_written"), 16)
            pool.wait_ge(sem("edge_tab_written"), 32)
            gathers(pool, "l0", [("a", srt[:, :, 0], xn_tab, xg0), ("b", srt[:, :, 5], edge_tab, eg0)], "l0_messages")

        def l0_tensor(pe):
            wait_blob(pe, 0)
            wait_bank(pe, "l0_wc", 0)
            full(pe.matmul(bank("l0_wc", 0)[0:54, 0:C], L0.w("f1aT"), L0.w("f1b"), start=True, stop=True))
            wait_empty(pe, "l0_wc")

            def body(i, b):
                if tile := tile_at(i, b):
                    _, t, s = tile
                    wait_gathered(pe, "b", "l0", *tile[::2])
                    wait_over(pe, "l0_featuresT", t - 1)
                    pe.transpose(PS[s % 2][:, 0:128], eg0[:, s, 0:128], ident[:, :]).then_inc(sem("l0_turned"), 1)
                if tile := tile_at(i, b, 1):
                    _, t, s = tile
                    pe.wait_ge(sem("l0_featuresT"), t + 1)
                    wait_over(pe, "l0_gated", t - 1)
                    pe.matmul(PS[2 + s % 2][:, 0:C], f54T[:, s % 2, :], wc, start=True, stop=True).then_inc(sem("l0_gate"), 1)
                if tile := tile_at(i, b, 2):
                    _, t, s = tile
                    pe.wait_ge(sem("l0_messages"), t + 1)
                    wait_over(pe, "l0_summed", t - 1)
                    pe.matmul(PS[4 + s % 2][0:P, :], oh[:, s % 3, :], msg0[:, s % 3, :], start=True, stop=True)\
                        .then_inc(sem("l0_product"), 1)
            tiles(pe, body, 2)
            pe.wait_ge(sem("l0_summed"), T)
            for w in range(W):
                a = acc0.rearrange("p (w c) -> p w c", w=W)
                turn(pe, "l0_accT", w, [((P * k, P), a[:, w, 128 * k:128 * k + 128]) for k in range(4)])
            wait_empty(pe, "l0_accT")
            for s in (1, 2):
                lin(pe, f"l0_conv{s}", [(L0w(f"c{s}_wl", 2), accT[:, 2 * s - 2:2 * s, :]), (L0w(f"c{s}_wr", 2), XNT)], C)
                wait_empty(pe, f"l0_conv{s}")
                lin(pe, f"l0_lin{s}", [(L0w(f"lin{s}_w", 2), conv)], C)
            pe.wait_ge(sem("l0_leaky"), 2)
            lin(pe, "l0_cat", [(L0w("cat_w", 4), hT)], C)
            pe.wait_ge(sem("l0_normed"), 2)
            for w in range(W):
                turn(pe, "l0_back", w, [((128 * k, 128), catT[:, k, P * w:P * w + P]) for k in range(2)])

        def L0w(name, k=None):
            return L0.w(name, k=k) if k else L0.w(name)

        def l0_scalar(act):
            wait_full(act, "l0_wc", 0)
            out_by(act.activation(wc, bank("l0_wc", 0)[0:54, 0:C], ACT.Copy), "act")

            def body(i, b):
                _, t, s = tile_at(i, b)
                act.wait_ge(sem("l0_turned"), t + 1)
                wait_over(act, "l0_gate", t - 1)
                act.activation(f54T[:, s % 2, :], PS[s % 2][0:54, 0:128], ACT.Copy).then_inc(sem("l0_featuresT"), 1)
            tiles(act, body)
            turned_nodes(act, "l0_accT", accT, 4)
            wait_blob(act, 0)
            for s in (1, 2):
                lin_out(act, f"l0_conv{s}", conv, C, ACT.Identity, L0w(f"c{s}_bl", None))
                if s == 2:
                    act.wait_ge(sem("l0_leaky"), 1)
                lin_out(act, f"l0_lin{s}", linv, C, ACT.Identity, L0w(f"lin{s}_b", None))
            lin_out(act, "l0_cat", catT, C, ACT.Identity, L0w("cat_b", None))
            act.wait_ge(sem("l0_group_var"), 1)
            act.activation(gnst[:, 20:22], gnst[:, 18:20], ACT.Sqrt).then_inc(sem("l0_group_std"), 1)
            act.wait_ge(sem("l0_scaled"), 1)
            for k in range(2):
                act.activation(catT[:, k, :], catT[:, k, :], ACT.Identity, bias=gnst[:, 26 + k:27 + k],
                               scale=gnst[:, 22 + k:23 + k]).then_inc(sem("l0_normed"), 1)

        def l0_vector(dve):
            link = linker(dve, "vector")
            dve.memset(acc0, 0.0)
            def body(i, b):
                if tile := tile_at(i, b, 1):
                    i1, t, s = tile
                    dve.wait_ge(sem("l0_gate"), t + 1)
                    dve.wait_ge(sem("l0_gx"), t + 1)
                    wait_over(dve, "l0_product", t - 2)
                    dve.tensor_tensor(msg0[:, s % 3, 0:C], PS[2 + s % 2][:, 0:C], gx0[:, s % 2, :], ALU.mult).then_inc(sem("l0_gated"), 1)
                if tile2 := tile_at(i, b):
                    i0, t0, s0 = tile2
                    wait_over(dve, "l0_product", t0 - 2)
                    onehot_of(dve, t0, s0 % 3)
                if tile:
                    dve.wait_ge(sem("l0_gated"), t + 1)
                    dve.tensor_tensor(msg0[:, s % 3, C:2 * C], msg0[:, s % 3, 0:C], eg0[:, s, 54:310], ALU.mult).then_inc(sem("l0_messages"), 1)
                if tile2:
                    wait_gathered(dve, "a", "l0", i0, s0)
                    wait_gathered(dve, "b", "l0", i0, s0)
                    dve.tensor_tensor(gx0[:, s0 % 2, :], eg0[:, s0, 54:310], xg0[:, s0, :], ALU.mult).then_inc(sem("l0_gx"), 1)
                if tile := tile_at(i, b, 2):
                    accumulate(dve, "l0", tile, acc0, PS[4 + tile[2] % 2][0:P, :], 512)
            tiles(dve, body, 2)
            for s in (1, 2):
                wait_empty(dve, f"l0_lin{s}")
                dve.scalar_tensor_tensor(hT[:, 2 * s - 2:2 * s, :], linv, 0.1, linv, ALU.mult, ALU.max).then_inc(sem("l0_leaky"), 1)
            wait_empty(dve, "l0_cat")
            g = gnst
            for k in range(2):
                for h, (c, n) in enumerate(HALVES):
                    ins = dve.bn_stats(g[:, 12 * k + 6 * h:12 * k + 6 * h + 6], catT[:, k, c:c + n])
            link(ins)
            for k in range(2):
                ins = dve.bn_aggr(g[:, 30 + 2 * k:32 + 2 * k], g[:, 12 * k:12 * k + 12])
            link(ins)
            mean, var = g[:, 30:34:2], g[:, 31:35:2]
            ms, gw, gb = L0w("gn_ms", None), L0w("gn_w", None), L0w("gn_b", None)
            link(dve.tensor_tensor(g[:, 36:38], mean, ms, ALU.mult))
            link(dve.tensor_tensor(g[:, 38:40], mean, g[:, 36:38], ALU.subtract))
            link(dve.tensor_tensor(g[:, 40:42], g[:, 38:40], g[:, 38:40], ALU.mult))
            dve.scalar_tensor_tensor(g[:, 18:20], var, 1e-5, g[:, 40:42], ALU.add, ALU.add).then_inc(sem("l0_group_var"), 1)
            dve.wait_ge(sem("l0_group_std"), 1)
            link(dve.reciprocal(g[:, 24:26], g[:, 20:22]))
            link(dve.tensor_tensor(g[:, 22:24], g[:, 24:26], gw, ALU.mult))
            link(dve.tensor_tensor(g[:, 28:30], g[:, 36:38], g[:, 22:24], ALU.mult))
            dve.tensor_tensor(g[:, 26:28], gb, g[:, 28:30], ALU.subtract).then_inc(sem("l0_scaled"), 1)
            add_to_x(dve, "l0_back")

        def soft_max(dve, act_sem, lg, rows, mx, link):
            bc = lambda a: a.unsqueeze(2).broadcast_to((rows, W, 8))
            link(dve.tensor_reduce(mx, lg, AX.X, ALU.max))
            dve.tensor_tensor(lg, lg, bc(mx), ALU.subtract).then_inc(sem("gate_shifted"), 1)
            dve.wait_ge(sem("gate_exp"), act_sem)
            link(dve.tensor_reduce(mx, lg, AX.X, ALU.add))
            link(dve.reciprocal(mx, mx))
            link(dve.tensor_tensor(lg, lg, bc(mx), ALU.mult))

        def first_max(dve, lg, mx, hit, number, link):
            bc = lambda a: a.unsqueeze(2).broadcast_to((P, W, 8))
            io = iota[0:P, 0:8].unsqueeze(1).broadcast_to((P, W, 8))
            link(dve.tensor_reduce(mx, lg, AX.X, ALU.max))
            link(dve.tensor_tensor(hit, lg, bc(mx), ALU.is_equal))
            link(dve.scalar_tensor_tensor(hit, hit, -8.0, io, ALU.mult, ALU.add))
            link(dve.tensor_reduce(number, hit, AX.X, ALU.min))
            link(dve.tensor_scalar(number, number, 8.0, None, ALU.add))
            link(dve.tensor_tensor(hit, io, bc(number), ALU.is_equal))

        L1, L5, L7 = Layer(1), Layer(5), Layer(7)
        view = {}
        for l, lay in ((1, L1), (5, L5), (7, L7)):
            view[l] = dict(coef=lay.work(P, W * 8, w=W), hit=lay.work(P, W * 8, w=W), left=lay.work(P, W * 8, w=W),
                           mx=lay.work(P, W), number=lay.work(P, W), mx2=lay.work(P, W), 
                           coefT=lay.work(8, N, at=places[5]["W1"][0] if l == 5 else None))
        for l, lay in ((1, L1), (7, L7)):
            view[l].update(h1=lay.work(128, 4 * N, u=2, k=2), h2=lay.work(128, 4 * N, u=2, k=2))
        view[5].update(h=L5.work(128, 8 * N, k=8))
        bns = L1.work(128, 32, s=2)
        bnc = L1.work(128, 32, s=2)
        MLP = {1: ("W1", "W2", "Wo"), 7: ("w1", None, "w2")}
        GATE = {1: ("Wr", "br", "bo"), 5: ("Wg", "bg", "bd"), 7: ("router", None, "b2")}
        FFN = (1, 5, 7)
        lays = {1: L1, 5: L5, 7: L7}

        def expert_weight(l, name, e, k):
            a = lays[l].w(name, e=8, k=k)
            return a[:, e, :, :]

        def ffn_tensor(pe, l):
            lay, v = lays[l], view[l]
            wait_blob(pe, l)
            xnt_tensor(pe, l)
            wait_empty(pe, f"xnt{l}")
            wr, br, bo = GATE[l]
            bias = lay.w(br) if br else None
            if l == 5:
                lin(pe, "hid", [(lay.w("W1", k=2), XNT)], 1024)
                wait_empty(pe, "hid")
                nodes(pe, "gate5", v["h"], lay.w("Wg", k=8), 8, bias)
            else:
                nodes(pe, f"gate{l}", XNT, lay.w(wr, k=2), 8, bias)
            for kind, e in experts(EXPERTS[l]):
                stage = f"{kind}_{l}_{e}"
                if kind == "mlp1":
                    lin(pe, stage, [(expert_weight(l, MLP[l][0], e, 2), XNT)], C)
                elif kind == "mlp2":
                    wait_empty(pe, f"mlp1_{l}_{e}")
                    lin(pe, stage, [(expert_weight(l, MLP[l][1], e, 2), v["h1"][:, e % 2])], C)
                else:
                    if l == 1:
                        wait_empty(pe, f"mlp2_{l}_{e}")
                        nodes(pe, stage, v["h2"][:, e % 2], expert_weight(l, "Wo", e, 2), C)
                    elif l == 7:
                        wait_empty(pe, f"mlp1_{l}_{e}")
                        nodes(pe, stage, v["h1"][:, e % 2], expert_weight(l, "w2", e, 2), C)
                    else:
                        nodes(pe, stage, v["h"], expert_weight(l, "Wd", e, 8), C)
            pe.wait_ge(sem("coefficients_ready"), FFN.index(l) + 1)
            for w in range(W):
                turn(pe, f"coefT{l}", w, [((0, P), v["coef"][:, w, :])])
            wait_empty(pe, f"coefT{l}")
            for w in range(W):
                wait_bank(pe, f"bias{l}", w)
                full(pe.matmul(bank(f"bias{l}", w)[0:P, 0:C], v["coefT"][:, P * w:P * w + P], lay.w(bo), start=True, stop=True))

        def ffn_scalar(act, l):
            lay, v = lays[l], view[l]
            if l == 1:
                act.wait_ge(sem("bn_var"), 1)
                act.activation(bns, bns, ACT.Sqrt).then_inc(sem("bn_std"), 1)
            wait_blob(act, l)
            xnt_scalar(act, l)
            if l == 5:
                lin_out(act, "hid", v["h"], 1024, ACT.Gelu, lay.w("b1"))
            act.wait_ge(sem("gate_shifted"), FFN.index(l) + 1)
            act.activation(v["coef"], v["coef"], ACT.Exp).then_inc(sem("gate_exp"), 1)
            if l == 1:
                act.wait_ge(sem("bn_ready"), 1)
            for kind, e in experts(EXPERTS[l]):
                stage = f"{kind}_{l}_{e}"
                if l == 1 and kind in ("mlp1", "mlp2"):
                    s = int(kind == "mlp2")
                    lin_out(act, stage, v["h2" if s else "h1"][:, e % 2], C, ACT.Relu,
                            bnc[:, s, 2 * e:2 * e + 2], bns[:, s, 2 * e:2 * e + 2])
                elif l == 7 and kind == "mlp1":
                    lin_out(act, stage, v["h1"][:, e % 2], C, ACT.Gelu, lay.w("b1")[:, 2 * e:2 * e + 2])
            for w in range(W):
                wait_full(act, f"coefT{l}", w)
                out_by(act.activation(v["coefT"][:, P * w:P * w + P], bank(f"coefT{l}", w)[0:8, 0:P], ACT.Copy), "act")

        def ffn_vector(dve, l):
            link = linker(dve, "vector")
            lay, v = lays[l], view[l]
            if l == 1:
                wait_blob(dve, 1)
                at = places[1]["b1"][0]
                bn = lay.ar[:, at:at + 160].rearrange("p (s q c) -> p s q c", s=2, q=5)
                dve.tensor_scalar(bns, bn[:, :, 4, :], 1e-3, None, ALU.add).then_inc(sem("bn_var"), 1)
            for w in range(W):
                wait_full(dve, f"gate{l}", w)
                out_by(dve.tensor_copy(v["coef"][:, w, :], bank(f"gate{l}", w)[0:P, 0:8]), "dve")
            wait_empty(dve, f"gate{l}")
            soft_max(dve, FFN.index(l) + 1, v["coef"], P, v["mx"], link)
            if l == 5:
                first_max(dve, v["coef"], v["mx"], v["hit"], v["number"], link)
                link(dve.tensor_tensor(v["coef"], v["coef"], v["hit"], ALU.mult))
            if l == 7:
                first_max(dve, v["coef"], v["mx"], v["hit"], v["number"], link)
                link(dve.tensor_scalar(v["left"], v["hit"], -2.0, None, ALU.mult))
                link(dve.tensor_tensor(v["left"], v["left"], v["coef"], ALU.add))
                link(dve.tensor_tensor(v["coef"], v["coef"], v["hit"], ALU.mult))
                first_max(dve, v["left"], v["mx2"], v["hit"], v["number"], link)
                link(dve.tensor_tensor(v["left"], v["left"], v["hit"], ALU.mult))
                link(dve.tensor_tensor(v["coef"], v["coef"], v["left"], ALU.add))
                link(dve.tensor_tensor(v["mx"], v["mx"], v["mx2"], ALU.add))
                link(dve.tensor_scalar(v["mx"], v["mx"], 1e-12, None, ALU.max))
                link(dve.reciprocal(v["mx"], v["mx"]))
                link(dve.tensor_tensor(v["coef"], v["coef"], v["mx"].unsqueeze(2).broadcast_to((P, W, 8)), ALU.mult))
            dve.tensor_copy(v["hit"], v["coef"]).then_inc(sem("coefficients_ready"), 1)
            if l == 1:
                dve.wait_ge(sem("bn_std"), 1)
                link(dve.reciprocal(bns, bns))
                link(dve.tensor_tensor(bns, bns, bn[:, :, 1, :], ALU.mult))
                link(dve.tensor_tensor(bnc, bn[:, :, 0, :], bn[:, :, 3, :], ALU.subtract))
                link(dve.tensor_tensor(bnc, bnc, bns, ALU.mult))
                dve.tensor_tensor(bnc, bnc, bn[:, :, 2, :], ALU.add).then_inc(sem("bn_ready"), 1)
            if l == 7:
                link(dve.tensor_tensor(X[:, :, :], X[:, :, :], XN[:, :, :], ALU.add))
            for kind, e in experts(EXPERTS[l]):
                if kind == "mlpo":
                    for w in range(W):
                        stage = f"mlpo_{l}_{e}"
                        wait_full(dve, stage, w)
                        wait_x(dve, stage, w)
                        out_by(dve.scalar_tensor_tensor(X[:, w, :], bank(stage, w)[0:P, 0:C], v["coef"][:, w, e:e + 1],
                                                        X[:, w, :], ALU.mult, ALU.add), "dve")
            wait_empty(dve, f"mlpo_{l}_7")
            add_to_x(dve, f"bias{l}")
            wait_empty(dve, f"bias{l}")

        def max_views(lay, H, big):
            v = dict(scoreT=big[0], fwd=big[1], bwd=big[2])
            v["dstT"] = lay.work(TH, 256, h=2)
            v["edge"] = lay.work(TH, 258, h=2)
            v["first"] = lay.work(TH, 256, h=2)
            v["last"] = lay.work(TH, 256, h=2)
            v["ends"] = lay.work(8, 2 * T, e=2)
            v["joined"] = lay.work(8, T + 1)
            v["single"] = lay.work(8, T)
            v["rowf"] = lay.work(8, 2 * T, e=2)
            v["step"] = lay.work(8, T)
            v["run"] = lay.work(8, T)
            v["carry"] = lay.work(8, 2 * T, e=2)
            v["carryT"] = lay.work(TH, 4 * H, e=2, h=2)
            return v

        def edge_max_tensor(pe, k, H, v, sc):
            pe.wait_ge(sem("scores_ready"), k + 1)
            for h in range(2):
                turn(pe, f"seg_dst{k}", h, [((0, 128), dst_all[:, TH * h:TH * h + TH])])
            wait_bank(pe, f"seg_ends{k}", 0)
            b = bank(f"seg_ends{k}", 0)
            pe.matmul(b[0:8, 0:T], sel0[:, :], dst_all, start=True, stop=True)
            full(pe.matmul(b[0:8, 256:256 + T], sel127[:, :], dst_all, start=True, stop=True))
            for u in range(2 * H):
                a, h = divmod(u, 2)
                turn(pe, f"scoreT{k}", u, [((0, 128), sc[:, TH * h:TH * h + TH, a])])
            pe.wait_ge(sem("runs_ready"), k + 1)
            for u in range(4):
                e, h = divmod(u, 2)
                src = v["bwd"][:, :, h, 0] if e else v["fwd"][:, :, h, 127]
                turn(pe, f"ends{k}", u, [((0, TH), src)])
            pe.wait_ge(sem("carries_ready"), k + 1)
            for u in range(4):
                e, h = divmod(u, 2)
                turn(pe, f"carry{k}", u, [((0, H), v["carry"][0:H, e, TH * h:TH * h + TH])])
            pe.wait_ge(sem("maxima_ready"), k + 1)
            for u in range(2 * H):
                a, h = divmod(u, 2)
                turn(pe, f"amax{k}", u, [((0, TH), v["scoreT"][:, a, h, :])])

        def edge_max_scalar(act, k, H, v, amax):
            for h in range(2):
                wait_full(act, f"seg_dst{k}", h)
                out_by(act.activation(v["dstT"][:, h, :], bank(f"seg_dst{k}", h)[0:TH, 0:128], ACT.Copy), "act")
            wait_full(act, f"seg_ends{k}", 0)
            out_by(act.activation(v["ends"], bank(f"seg_ends{k}", 0)[0:8, :].rearrange("p (e t) -> p e t", e=2)[:, :, 0:T], ACT.Copy), "act")
            for u in range(2 * H):
                a, h = divmod(u, 2)
                wait_full(act, f"scoreT{k}", u)
                out_by(act.activation(v["scoreT"][:, a, h, :], bank(f"scoreT{k}", u)[0:TH, 0:128], ACT.Copy), "act")
            for u in range(4):
                e, h = divmod(u, 2)
                wait_full(act, f"ends{k}", u)
                out_by(act.activation(v["rowf"][0:H, e, TH * h:TH * h + TH], bank(f"ends{k}", u)[0:H, 0:TH], ACT.Copy), "act")
            for u in range(4):
                e, h = divmod(u, 2)
                wait_full(act, f"carry{k}", u)
                out_by(act.activation(v["carryT"][:, e, h, :], bank(f"carry{k}", u)[0:TH, 0:H], ACT.Copy), "act")
            for u in range(2 * H):
                a, h = divmod(u, 2)
                wait_full(act, f"amax{k}", u)
                out_by(act.activation(amax[:, TH * h:TH * h + TH, a], bank(f"amax{k}", u)[:, 0:TH], ACT.Copy), "act")

        def edge_max_vector(dve, k, H, v):
            link = linker(dve, "vector")
            wait_empty(dve, f"seg_ends{k}")

            def far(out, a, b):
                link(dve.tensor_tensor(out, a, b, ALU.is_equal))
                link(dve.tensor_scalar(out, out, 1.0, BIG, ALU.subtract, ALU.mult))

            dt, edge = v["dstT"], v["edge"]
            link(dve.memset(edge, -BIG))
            far(edge[:, :, 1:128], dt[:, :, 1:128], dt[:, :, 0:127])
            far(v["first"], dt, dt[:, :, 0:1].broadcast_to((TH, 2, 128)))
            far(v["last"], dt, dt[:, :, 127:128].broadcast_to((TH, 2, 128)))
            link(dve.memset(v["joined"], -BIG))
            far(v["joined"][:, 1:T], v["ends"][:, 0, 1:T], v["ends"][:, 1, 0:T - 1])
            far(v["single"], v["ends"][:, 0, :], v["ends"][:, 1, :])
            wait_empty(dve, f"scoreT{k}")
            for a in range(H):
                for h in range(2):
                    s = v["scoreT"][:, a, h, :]
                    dve.tensor_tensor_scan(v["fwd"][:, a, h, :], edge[:, h, 0:128], s, -BIG, ALU.add, ALU.max)
                    ins = dve.tensor_tensor_scan(v["bwd"][:, a, h, ::-1], edge[:, h, 128:0:-1], s[:, ::-1], -BIG, ALU.add, ALU.max)
            ins.then_inc(sem("runs_ready"), 1)
            wait_empty(dve, f"ends{k}")
            jn, step, run = v["joined"], v["step"], v["run"]
            link(dve.tensor_tensor(step, v["single"], jn[:, 0:T], ALU.add))
            link(dve.tensor_tensor_scan(run[0:H], step[0:H], v["rowf"][0:H, 0, :], -BIG, ALU.add, ALU.max))
            link(dve.memset(v["carry"], -BIG))
            dve.tensor_tensor(v["carry"][0:H, 0, 1:T], run[0:H, 0:T - 1], jn[0:H, 1:T], ALU.add)
            link(dve.tensor_tensor(step, v["single"], jn[:, 1:T + 1], ALU.add))
            link(dve.tensor_tensor_scan(run[0:H, ::-1], step[0:H, ::-1], v["rowf"][0:H, 1, ::-1], -BIG, ALU.add, ALU.max))
            dve.tensor_tensor(v["carry"][0:H, 1, 0:T - 1], run[0:H, 1:T], jn[0:H, 1:T], ALU.add).then_inc(sem("carries_ready"), 1)
            link(dve.tensor_tensor(v["scoreT"], v["fwd"], v["bwd"], ALU.max))
            wait_empty(dve, f"carry{k}")
            for e, mask in ((0, v["first"]), (1, v["last"])):
                for a in range(H):
                    for h in range(2):
                        m = v["scoreT"][:, a, h, :]
                        ins = dve.scalar_tensor_tensor(m, mask[:, h, :], v["carryT"][:, e, h, a:a + 1], m, ALU.add, ALU.max)
                if e == 0:
                    link(ins)
            ins.then_inc(sem("maxima_ready"), 1)

        G1 = Layer(2)
        vt = G1.work(128, 256, k=2)
        s16 = G1.work(P, W * 128, w=W)
        hbuf_at = G1.at
        hbuf = G1.work(P, 2 * W * C, u=2, w=W)
        hx = G1.work(128, U * C, u=U)
        sa = G1.work(128, U * 16, u=U)
        sd = G1.work(128, U * 16, u=U)
        msg1 = G1.work(128, 3 * C, u=3)
        acc1 = G1.work(P, W * 265)
        wt9 = G1.work(128, T * 9, t=T)
        wt_at, wn_at = places[2]["WT"][0], places[2]["Wn"][0]
        sc1 = G1.work(128, T * 8, at=wt_at, t=T)
        am1 = G1.work(128, T * 8, at=wt_at + T * 8, t=T)
        mv1 = max_views(G1, NH, [G1.work(TH, 2048, at=a, a=NH, h=2) for a in (wn_at, wn_at + 2048, hbuf_at)])

        def l1_sync(sp):
            wait_empty(sp, "l1_s")
            for w in range(W):
                sp.dma_start(s_tab.rearrange("(r w p) s -> w p r s", w=W, p=P)[w],
                             s16[:, w, :].rearrange("p (r s) -> p r s", r=NR)).then_inc(sem("s_written"), 16)
            for r in range(NR):
                wait_empty(sp, f"l1_h{r}")
                sp.dma_start(h_tab[r * N:(r + 1) * N, :].rearrange("(w p) c -> p w c", w=W), hbuf[:, r % 2])\
                    .then_inc(sem(f"h_written{r % 2}"), 16)

        def l1_pool(pool):
            pool.wait_ge(sem("s_written"), 16 * W)
            gathers(pool, "l1s", [("a", idx_hs, s_tab, sa), ("b", idx_hd, s_tab, sd)], "l1s_added")
            for k in range(2):
                pool.wait_ge(sem(f"h_written{k}"), 16 * NR // 2)
            gathers(pool, "l1m", [("a", idx_hs, h_tab, hx)], "l1m_messages")

        def l1_tensor(pe):
            wait_blob(pe, 2)
            xnt_tensor(pe, 2)
            wn, wtv, at = G1.w("Wn", r=NR, k=2), G1.w("WT", r=NR, k=2), G1.w("attn", k=2)
            for r in range(NR):
                wait_bank(pe, "l1_v", r)
                for f in range(2):
                    for k in range(2):
                        ins = pe.matmul(bank("l1_v", r)[:, 16 * f:16 * f + 16], wn[:, r, k, 128 * f:128 * f + 128],
                                        at[:, k, :], start=k == 0, stop=k == 1)
                full(ins)
            wait_empty(pe, "xnt2")
            wait_empty(pe, "l1_v")
            nodes(pe, "l1_s", XNT, vt, 128)
            for r in range(NR):
                nodes(pe, f"l1_h{r}", XNT, wtv[:, r], C)
            edge_max_tensor(pe, 0, NH, mv1, sc1)
            wait_empty(pe, "amax0")
            pe.wait_ge(sem("weights1_ready"), 1)

            def body(i, b):
                if tile := tile_at(i, b, 1):
                    _, t, s = tile
                    pe.wait_ge(sem("l1m_messages"), t + 1)
                    wait_over(pe, "l1m_summed", t - 1)
                    pe.matmul(PS[s % 2][0:P, 0:C], oh[:, s % 3, :], msg1[:, s % 3, :], start=True, stop=True)
                    pe.matmul(PS[s % 2][0:P, C:C + 9], oh[:, s % 3, :], wt9[:, ds(t, 1), :].rearrange("p a h -> p (a h)"),
                              start=True, stop=True).then_inc(sem("l1m_product"), 1)
            tiles(pe, body, 1)
            pe.wait_ge(sem("l1m_summed"), T)

        def l1_scalar(act):
            xnt_scalar(act, 2)
            for r in range(NR):
                wait_full(act, "l1_v", r)
                out_by(act.activation(vt[:, :, 16 * r:16 * r + 16], bank("l1_v", r)[:, 0:32].rearrange("p (f s) -> p f s", f=2), ACT.Copy), "act")
            for w in range(W):
                wait_full(act, "l1_s", w)
                out_by(act.activation(s16[:, w, :], bank("l1_s", w)[0:P, 0:128], ACT.Copy), "act")
            for r in range(NR):
                if r >= 2:
                    act.wait_ge(sem(f"h_written{r % 2}"), 16 * (r // 2))
                for w in range(W):
                    wait_full(act, f"l1_h{r}", w)
                    out_by(act.activation(hbuf[:, r % 2, w, :], bank(f"l1_h{r}", w)[0:P, 0:C], ACT.Copy), "act")
            edge_max_scalar(act, 0, NH, mv1, am1)
            act.wait_ge(sem("scores_shifted"), 1)
            act.activation(wt9[:, :, 0:8], sc1, ACT.Exp).then_inc(sem("weights1_ready"), 1)

        def l1_vector(dve):
            link = linker(dve, "vector")
            wait_empty(dve, "l1_h7")
            for k in range(2):
                dve.wait_ge(sem(f"h_written{k}"), 16 * NR // 2)

            def score(i, b):
                i, t, s = tile_at(i, b)
                wait_gathered(dve, "a", "l1s", i, s)
                wait_gathered(dve, "b", "l1s", i, s)
                dve.tensor_tensor(sc1[:, ds(t, 1), :].rearrange("p a h -> p (a h)"), sa[:, s, 0:8], sd[:, s, 8:16], ALU.add)\
                    .then_inc(sem("l1s_added"), 1)
            tiles(dve, score)
            dve.wait_ge(sem("l1s_added"), T)
            dve.scalar_tensor_tensor(sc1, sc1, 0.2, sc1, ALU.mult, ALU.max).then_inc(sem("scores_ready"), 1)
            dve.memset(acc1, 0.0)
            edge_max_vector(dve, 0, NH, mv1)
            wait_empty(dve, "amax0")
            link(dve.tensor_scalar(am1, am1, 0.0, None, ALU.max))
            dve.tensor_copy(wt9[:, :, 8], typ[:, :, 1])
            dve.tensor_tensor(sc1, sc1, am1, ALU.subtract).then_inc(sem("scores_shifted"), 1)
            dve.wait_ge(sem("weights1_ready"), 1)

            def body(i, b):
                if tile := tile_at(i, b):
                    i0, t, s = tile
                    wait_over(dve, "l1m_product", t - 2)
                    onehot_of(dve, t, s % 3)
                    wait_gathered(dve, "a", "l1m", i0, s)
                    w8 = wt9[:, ds(t, 1), 0:8].rearrange("p a h -> p (a h)")
                    dve.tensor_tensor(msg1[:, s % 3, :].rearrange("p (h d) -> p h d", h=NH),
                                      hx[:, s, :].rearrange("p (h d) -> p h d", h=NH),
                                      w8.unsqueeze(2).broadcast_to((128, NH, HD)), ALU.mult).then_inc(sem("l1m_messages"), 1)
                if tile := tile_at(i, b, 1):
                    accumulate(dve, "l1m", tile, acc1, PS[tile[2] % 2][0:P, 0:265], 265)
            tiles(dve, body, 1)
            dve.wait_ge(sem("l1m_summed"), T)
            a = acc1.rearrange("p (w c) -> p w c", w=W)
            den = a[:, :, C:C + 8]
            dve.tensor_scalar(recv1[:, :], a[:, :, C + 8], 0.0, None, ALU.is_gt)
            link(dve.tensor_scalar(den, den, 1e-12, None, ALU.add))
            link(dve.reciprocal(den, den))
            for w in range(W):
                o = a[:, w, 0:C].rearrange("p (h d) -> p h d", h=NH)
                link(dve.tensor_tensor(o, o, den[:, w, :].unsqueeze(2).broadcast_to((P, NH, HD)), ALU.mult))
                link(dve.tensor_tensor(X[:, w, :], X[:, w, :], a[:, w, 0:C], ALU.add))

        A3 = Layer(3)
        xmT = A3.work(128, 4 * N, k=4)
        fx = A3.work(P, W * 4 * 129, w=W, q=4)
        sw = A3.work(P, W * 512, w=W)
        swT = A3.work(128, 4 * N, k=4)
        oxT = A3.work(128, 4 * N, k=4)
        tok, tokT, qT, kT, vv, pr, prT, osl = (A3.work(128, 512, q=4) for _ in range(8))
        invt = A3.work(P, 8)
        smx = A3.work(P, 8)
        rn = A3.work(128, 8)
        DIAG = ((slice(0, 64), slice(0, 64)), (slice(64, 128), slice(64, 128)))

        def l1f_tensor(pe):
            wait_blob(pe, 3)
            xnt_tensor(pe, 3)
            wait_empty(pe, "xnt3")
            lin(pe, "xmT", [(A3.w("W_x", k=2), XNT)], 512)
            nodes(pe, "fx", XNT, A3.w("W_fx", k=2), 512, A3.w("b_fx"))
            wait_empty(pe, "xmT")
            for w in range(W):
                wait_bank(pe, "slice", w)
                pe.matmul(bank("slice", w)[0:P, :], ones[0:1, 0:P], A3.w("b_slice"), start=True, stop=False)
                for q in range(4):
                    ins = pe.matmul(bank("slice", w)[0:P, 128 * q:128 * q + 128], xmT[:, q, P * w:P * w + P], A3.w("W_slice"),
                                    start=False, stop=q == 3)
                full(ins)
            for w in range(W):
                pe.wait_ge(sem("slices_ready"), w + 1)
                turn(pe, "swT", w, [((P * k, P), sw[:, w, 128 * k:128 * k + 128]) for k in range(4)])
            wait_empty(pe, "fx")
            for q in range(4):
                wait_bank(pe, "token", q)
                for w in range(W):
                    ins = pe.matmul(bank("token", q)[:, 0:129], sw[:, w, 128 * q:128 * q + 128], fx[:, w, q, :],
                                    start=w == 0, stop=w == W - 1)
                full(ins)
            wait_empty(pe, "token")
            for q in range(4):
                turn(pe, "t_tokT", q, [((0, 128), tok[:, q, :])])

            def squares(stage, left, right):
                for q in range(4):
                    wait_bank(pe, stage, q)
                    full(pe.matmul(bank(stage, q)[:, 0:128], left(q), right(q), start=True, stop=True))
            wait_empty(pe, "t_tokT")
            squares("t_qT", lambda q: A3.w("W_q"), lambda q: tokT[:, q, :])
            squares("t_kT", lambda q: A3.w("W_k"), lambda q: tokT[:, q, :])
            squares("t_v", lambda q: tokT[:, q, :], lambda q: A3.w("W_v"))
            wait_empty(pe, "t_kT")
            squares("t_lg", lambda q: qT[:, q, :], lambda q: kT[:, q, :])
            pe.wait_ge(sem("slice_attention_ready"), 1)
            for q in range(4):
                turn(pe, "t_pT", q, [((0, 128), pr[:, q, :])])
            wait_empty(pe, "t_pT")
            squares("t_os", lambda q: prT[:, q, :], lambda q: vv[:, q, :])
            wait_empty(pe, "t_os")
            for q in range(4):
                for h, (c, n) in enumerate(HALVES):
                    wait_bank(pe, "oxT", 2 * q + h)
                    full(pe.matmul(bank("oxT", 2 * q + h)[:, 0:n], osl[:, q, :], swT[:, q, c:c + n], start=True, stop=True))
            wait_empty(pe, "oxT")
            nodes(pe, "l3_out", oxT, A3.w("W_out", k=4), C, A3.w("b_out"))

        def l1f_scalar(act):
            wait_blob(act, 3)
            xnt_scalar(act, 3)
            lin_out(act, "xmT", xmT, 512, ACT.Identity, A3.w("b_x"))
            for w in range(W):
                wait_full(act, "fx", w)
                out_by(act.activation(fx[:, w, :, 0:128], bank("fx", w)[0:P, :].rearrange("p (q c) -> p q c", q=4), ACT.Copy), "act")
            for w in range(W):
                act.wait_ge(sem("slice_shifted"), w + 1)
                act.activation(sw[:, w, :], sw[:, w, :], ACT.Exp).then_inc(sem("slice_exp"), 1)
            turned_nodes(act, "swT", swT, 4)

            def squares_out(stage, out, scale=1.0):
                for q in range(4):
                    wait_full(act, stage, q)
                    out_by(act.activation(out[:, q, :], bank(stage, q)[:, 0:128], ACT.Copy, scale=scale), "act")
            squares_out("t_tokT", tokT)
            squares_out("t_qT", qT, 64 ** -0.5)
            squares_out("t_kT", kT)
            squares_out("t_v", vv)
            wait_empty(act, "t_lg")
            for rows, cols in DIAG:
                ins = act.activation(pr[rows, :, cols], pr[rows, :, cols], ACT.Exp)
            ins.then_inc(sem("slice_attention_exp"), 1)
            squares_out("t_pT", prT)
            squares_out("t_os", osl)
            lin_out(act, "oxT", oxT, 512, ACT.Copy)

        def l1f_vector(dve):
            link = linker(dve, "vector")
            wait_blob(dve, 3)
            dve.memset(fx[:, :, :, 128:129], 1.0)
            dve.memset(tok, 0.0)
            link(dve.memset(pr, 0.0))
            link(dve.tensor_scalar(invt, A3.w("temp")[0:P, :], 0.1, 5.0, ALU.max, ALU.min))
            link(dve.reciprocal(invt, invt))
            bc = lambda a: a.unsqueeze(2).broadcast_to((P, 8, 64))
            for w in range(W):
                s = sw[:, w, :].rearrange("p (h g) -> p h g", h=8)
                wait_full(dve, "slice", w)
                out_by(dve.tensor_tensor(s, bank("slice", w)[0:P, :].rearrange("p (h g) -> p h g", h=8), bc(invt), ALU.mult), "dve")
                wait_empty(dve, "slice", w)
                link(dve.tensor_reduce(smx, s, AX.X, ALU.max))
                dve.tensor_tensor(s, s, bc(smx), ALU.subtract).then_inc(sem("slice_shifted"), 1)
            dve.wait_ge(sem("slice_shifted"), W)
            for w in range(W):
                s = sw[:, w, :].rearrange("p (h g) -> p h g", h=8)
                dve.wait_ge(sem("slice_exp"), w + 1)
                wait_over(dve, "slices_ready", w)
                link(dve.tensor_reduce(smx, s, AX.X, ALU.add))
                link(dve.reciprocal(smx, smx))
                dve.tensor_tensor(s, s, bc(smx), ALU.mult).then_inc(sem("slices_ready"), 1)
            for q in range(4):
                b = bank("token", q)
                wait_full(dve, "token", q)
                link(dve.tensor_scalar(rn[:, q:q + 1], b[:, 128:129], 1e-5, None, ALU.add))
                link(dve.reciprocal(rn[:, q:q + 1], rn[:, q:q + 1]))
                for rows, cols in DIAG:
                    ins = dve.tensor_scalar(tok[rows, q, cols], b[rows, cols], rn[rows, q:q + 1], None, ALU.mult)
                out_by(ins, "dve")
            for q in range(4):
                wait_full(dve, "t_lg", q)
                b = bank("t_lg", q)
                for rows, cols in DIAG:
                    ins = dve.tensor_reduce(rn[rows, q:q + 1], b[rows, cols], AX.X, ALU.max)
                link(ins)
                for rows, cols in DIAG:
                    ins = dve.tensor_scalar(pr[rows, q, cols], b[rows, cols], rn[rows, q:q + 1], None, ALU.subtract)
                out_by(ins, "dve")
            dve.wait_ge(sem("slice_attention_exp"), 1)
            for rows, cols in DIAG:
                ins = dve.tensor_reduce(rn[rows, 0:4], pr[rows, :, cols], AX.X, ALU.add)
            link(ins)
            link(dve.reciprocal(rn[:, 0:4], rn[:, 0:4]))
            for rows, cols in DIAG:
                ins = dve.tensor_tensor(pr[rows, :, cols], pr[rows, :, cols],
                                        rn[rows, 0:4].unsqueeze(2).broadcast_to((64, 4, 64)), ALU.mult)
            ins.then_inc(sem("slice_attention_ready"), 1)
            add_to_x(dve, "l3_out")
            wait_empty(dve, "l3_out")

        G2 = Layer(4)
        over_at = G2.at
        xg2 = G2.work(128, U * C, u=U)
        msg2 = G2.work(128, 3 * 512, u=3)
        h0T = G2.work(128, 4 * N, at=over_at, k=4)
        acc2 = G2.work(P, W * 512)
        h1T = G2.work(128, 4 * N, k=4)
        agg = G2.work(P, W * C, w=W)
        aggT = G2.work(128, 2 * N, k=2)
        nmask = G2.work(P, 4 * W, t=4)

        def l2_pool(pool):
            pool.wait_ge(sem("xn_written"), 32)
            gathers(pool, "l2", [("a", srt[:, :, 0], xn_tab, xg2)], "l2_messages")

        def l2_tensor(pe):
            wait_blob(pe, 4)
            xnt_tensor(pe, 4)
            wait_empty(pe, "xnt4")

            def body(i, b):
                if tile := tile_at(i, b, 1):
                    _, t, s = tile
                    pe.wait_ge(sem("l2_messages"), t + 1)
                    pe.wait_ge(sem("l2_onehots"), t + 1)
                    wait_over(pe, "l2_summed", t - 1)
                    pe.matmul(PS[s % 2][0:P, :], oh[:, s % 3, :], msg2[:, s % 3, :], start=True, stop=True).then_inc(sem("l2_product"), 1)
            tiles(pe, body, 1)
            pe.wait_ge(sem("agg_ready"), 1)
            turn_nodes(pe, "aggT", agg, 2)
            wait_empty(pe, "aggT")
            w0, w1, w2 = G2.w("W0", t=2, k=4), G2.w("W1", t=2, k=4), G2.w("W2", t=2, k=4)
            for t in range(2):
                lin(pe, f"g0_{t}", [(w0[:, t, 0:2], aggT), (w0[:, t, 2:4], XNT)], 512)
                wait_empty(pe, f"g0_{t}")
                lin(pe, f"g1_{t}", [(w1[:, t], h0T)], 512)
                wait_empty(pe, f"g1_{t}")
                nodes(pe, f"g2_{t}", h1T, w2[:, t], C, G2.w("b2")[:, t * C:(t + 1) * C])

        def l2_scalar(act):
            wait_blob(act, 4)
            xnt_scalar(act, 4)

            def body(i, b):
                i0, t, s = tile_at(i, b)
                wait_gathered(act, "a", "l2", i0, s)
                wait_over(act, "l2_product", t - 2)
                for k in range(2):
                    ins = act.activation(msg2[:, s % 3, k * C:(k + 1) * C], xg2[:, s, :], ACT.Copy,
                                         scale=typ[:, ds(t, 1), k])
                ins.then_inc(sem("l2_messages"), 1)
            tiles(act, body)
            turned_nodes(act, "aggT", aggT, 2)
            b0, b1 = G2.w("b0"), G2.w("b1")
            for t in range(2):
                lin_out(act, f"g0_{t}", h0T, 512, ACT.Relu, b0[:, 4 * t:4 * t + 4])
                lin_out(act, f"g1_{t}", h1T, 512, ACT.Relu, b1[:, 4 * t:4 * t + 4])

        def l2_vector(dve):
            link = linker(dve, "vector")
            dve.memset(acc2, 0.0)

            def body(i, b):
                if tile := tile_at(i, b):
                    _, t, s = tile
                    wait_over(dve, "l2_product", t - 2)
                    onehot_of(dve, t, s % 3).then_inc(sem("l2_onehots"), 1)
                if tile := tile_at(i, b, 1):
                    accumulate(dve, "l2", tile, acc2, PS[tile[2] % 2][0:P, :], 512)
            tiles(dve, body, 1)
            dve.wait_ge(sem("l2_summed"), T)
            a = acc2.rearrange("p (w c) -> p w c", w=W)
            link(dve.tensor_scalar(nmask[:, 2, :], recv1[:, :], -1.0, 1.0, ALU.mult, ALU.add))
            for w in range(W):
                ins = dve.tensor_scalar(agg[:, w, :], a[:, w, 0:C], nmask[:, 2, w:w + 1], None, ALU.mult)
            link(ins)
            for w in range(W):
                ins = dve.scalar_tensor_tensor(agg[:, w, :], a[:, w, C:2 * C], recv1[:, w:w + 1], agg[:, w, :], ALU.mult, ALU.add)
            ins.then_inc(sem("agg_ready"), 1)
            for t in range(2):
                ins = dve.tensor_scalar(nmask[:, t, :], ntype[:, :], float(t), None, ALU.is_equal)
            link(ins)
            link(dve.tensor_tensor(nmask[:, 3, :], nmask[:, 0, :], nmask[:, 1, :], ALU.add))
            link(dve.tensor_scalar(nmask[:, 3, :], nmask[:, 3, :], -1.0, 1.0, ALU.mult, ALU.add))
            for w in range(W):
                ins = dve.scalar_tensor_tensor(X[:, w, :], XN[:, w, :], nmask[:, 3, w:w + 1], X[:, w, :], ALU.mult, ALU.add)
            link(ins)
            for t in range(2):
                for w in range(W):
                    wait_full(dve, f"g2_{t}", w)
                    wait_x(dve, f"g2_{t}", w)
                    out_by(dve.scalar_tensor_tensor(X[:, w, :], bank(f"g2_{t}", w)[0:P, 0:C], nmask[:, t, w:w + 1], X[:, w, :],
                                                    ALU.mult, ALU.add), "dve")
            wait_empty(dve, "g2_1")

        G3 = Layer(6)
        qn = G3.work(P, W * C)
        kvb_at = G3.at
        kvb = G3.work(P, W * 512, w=W)
        kvg = G3.work(128, U * KVW, u=U)
        ea = G3.work(128, U * 128, u=U)
        wtp, btp = G3.work(128, 128), G3.work(128, 128)
        rel = G3.work(128, 2)
        arg = G3.work(128, 256, u=2)
        rnd = G3.work(128, 128)
        enc = G3.work(128, 256, u=2)
        eT = G3.work(128, 512, u=2, k=2)
        ohT = G3.work(P, 256, u=2)
        kj = G3.work(128, 512, u=2)
        prod = G3.work(128, 256)
        ve = G3.work(128, U * C, u=U)
        sc3 = G3.work(128, T * 2, t=T)
        am3 = G3.work(128, T * 2, t=T)
        acc3 = G3.work(P, W * 258)
        msg3 = G3.work(128, 3 * C, u=3)
        mv3 = max_views(G3, 2, [G3.work(TH, 512, at=kvb_at + 512 * j, a=2, h=2) for j in range(3)])
        TWO_PI = 2.0 * float(np.pi)
        ROUND = 1.5 * 2.0 ** 23

        def l3_sync(sp):
            sp.dma_start(kv_tab[:, 2 * C:KVW], d["node_vec"].rearrange("(n a) -> n a", a=1),
                         allow_slow_non_contiguous=True).then_inc(sem("kv_written"), 16)
            wait_empty(sp, "l3_v")
            sp.dma_start(kv_tab[:, 0:2 * C].rearrange("(w p) c -> p w c", w=W), kvb).then_inc(sem("kv_written"), 16)

            def store(i, b):
                i, t, s = tile_at(i, b)
                sp.wait_ge(sem("l3_values"), t + 1)
                sp.dma_start(ve_tab[ds(t, 1), :, :].rearrange("a p c -> p (a c)"), ve[:, s, :]).then_inc(sem(f"values_stored{s}"), 16)
            tiles(sp, store)
            for b in range(U):
                sp.wait_ge(sem(f"values_stored{b}"), 16 * (T // U))

            def load(i, b):
                i, t, s = tile_at(i, b)
                wait_over(sp, "l3m_messages", t - U + 1)
                sp.dma_start(ve[:, s, :], ve_tab[ds(t, 1), :, :].rearrange("a p c -> p (a c)")).then_inc(sem(f"values_loaded{s}"), 16)
            tiles(sp, load)

        def l3_pool(pool):
            pool.wait_ge(sem("kv_written"), 32)
            gathers(pool, "l3", [("a", srt[:, :, 0], kv_tab, kvg), ("b", srt[:, :, 5], d["edge_attr_128"], ea)], "l3_scored")

        def l3_tensor(pe):
            wait_blob(pe, 6)
            xnt_tensor(pe, 6)
            wait_empty(pe, "xnt6")
            for s in ("q", "k", "v", "skip"):
                nodes(pe, "l3_" + s, XNT, G3.w("W" + s, k=2), C, G3.w("b" + s))
            wait_empty(pe, "l3_v")
            wait_empty(pe, "l3_skip")
            we = G3.w("We", k=2)

            def body(i, b):
                if tile := tile_at(i, b, 1):
                    i1, t, s = tile
                    bk = PS[s % 2]
                    pe.wait_ge(sem("l3_encoded"), t + 1)
                    pe.wait_ge(sem("l3_onehots"), t + 1)
                    wait_gathered(pe, "b", "l3", i1, s)
                    wait_over(pe, "l3_copied", t - 1)
                    pe.transpose(bk[:, 0:128], enc[:, s % 2, :], ident[:, :])
                    pe.transpose(bk[:, 128:256], ea[:, s, :], ident[:, :])
                    pe.transpose(bk[0:P, 256:384], oh[:, s % 3, :], ident[:, :]).then_inc(sem("l3_turned"), 1)
                if tile := tile_at(i, b, 2):
                    _, t, s = tile
                    w = pe.value_load(widi[0:1, ds(t, 1)], min_val=0, max_val=W - 1)
                    pe.wait_ge(sem("l3_copied"), t + 1)
                    wait_over(pe, "l3_scored", t - 1)
                    for k in range(2):
                        pe.matmul(PS[2 + s % 2][:, 0:C], eT[:, s % 2, k, :], we[:, k, :], start=k == 0, stop=k == 1)
                    pe.matmul(PS[4 + s % 2][:, 0:C], ohT[:, s % 2, :], qn[:, ds(w * C, C)], start=True, stop=True)\
                        .then_inc(sem("l3_vectors"), 1)
            tiles(pe, body, 3)
            edge_max_tensor(pe, 1, 2, mv3, sc3)
            wait_empty(pe, "amax1")
            pe.wait_ge(sem("weights3_ready"), 1)

            def sums(i, b):
                if tile := tile_at(i, b, 1):
                    _, t, s = tile
                    pe.wait_ge(sem("l3m_messages"), t + 1)
                    pe.wait_ge(sem("l3m_onehots"), t + 1)
                    wait_over(pe, "l3m_summed", t - 1)
                    pe.matmul(PS[s % 2][0:P, 0:C], oh[:, s % 3, :], msg3[:, s % 3, :], start=True, stop=True)
                    pe.matmul(PS[s % 2][0:P, C:C + 2], oh[:, s % 3, :], sc3[:, ds(t, 1), :].rearrange("p a h -> p (a h)"),
                              start=True, stop=True).then_inc(sem("l3m_product"), 1)
            tiles(pe, sums, 1)
            pe.wait_ge(sem("l3m_summed"), T)

        def l3_scalar(act):
            xnt_scalar(act, 6)
            for w in range(W):
                wait_full(act, "l3_q", w)
                out_by(act.activation(qn[:, w * C:(w + 1) * C], bank("l3_q", w)[0:P, 0:C], ACT.Copy), "act")
            for k, s in enumerate("kv"):
                for w in range(W):
                    wait_full(act, "l3_" + s, w)
                    out_by(act.activation(kvb[:, w, k * C:(k + 1) * C], bank("l3_" + s, w)[0:P, 0:C], ACT.Copy), "act")

            def body(i, b):
                if tile := tile_at(i, b):
                    _, t, s = tile
                    act.wait_ge(sem("l3_angles"), t + 1)
                    wait_over(act, "l3_turned", t - 1)
                    act.activation(enc[:, s % 2, :], arg[:, s % 2, :], ACT.Sin, scale=6.2831850).then_inc(sem("l3_encoded"), 1)
                if tile := tile_at(i, b, 1):
                    _, t, s = tile
                    act.wait_ge(sem("l3_turned"), t + 1)
                    wait_over(act, "l3_vectors", t - 1)
                    act.activation(eT[:, s % 2, :, :], PS[s % 2][:, 0:256].rearrange("p (k e) -> p k e", k=2), ACT.Copy)
                    act.activation(ohT[:, s % 2, :], PS[s % 2][0:P, 256:384], ACT.Copy).then_inc(sem("l3_copied"), 1)
            tiles(act, body, 3)
            edge_max_scalar(act, 1, 2, mv3, am3)
            act.wait_ge(sem("scores_shifted"), 2)
            act.activation(sc3, sc3, ACT.Exp).then_inc(sem("weights3_ready"), 1)
            act.wait_ge(sem("weights3_ready"), 1)

            def weigh(i, b):
                i0, t, s = tile_at(i, b)
                act.wait_ge(sem(f"values_loaded{s}"), (i0 + 1) * 16)
                wait_over(act, "l3m_product", t - 2)
                for k in range(2):
                    ins = act.activation(msg3[:, s % 3, 128 * k:128 * k + 128], ve[:, s, 128 * k:128 * k + 128], ACT.Copy,
                                         scale=sc3[:, ds(t, 1), k])
                ins.then_inc(sem("l3m_messages"), 1)
            tiles(act, weigh)

        def l3_vector(dve):
            link = linker(dve, "vector")
            wait_blob(dve, 6)
            dve.tensor_scalar(wtp, G3.w("Wt"), 1.0 / TWO_PI, None, ALU.mult)
            link(dve.tensor_scalar(btp, G3.w("bt"), 1.0 / TWO_PI, 0.25, ALU.mult, ALU.add))
            add_to_x(dve, "l3_skip")

            def body(i, b):
                new, old = tile_at(i, b), tile_at(i, b, 3)
                if new:
                    i0, t, s = new
                    wait_gathered(dve, "a", "l3", i0, s)
                    dve.tensor_tensor(rel[:, s % 2:s % 2 + 1], kvg[:, s, 2 * C:KVW], srt_f[:, ds(t, 1), 4], ALU.subtract).then_inc(sem("l3_rel"), 1)
                if old:
                    i3, t3, s3 = old
                    dve.wait_ge(sem("l3_vectors"), t3 + 1)
                    e = PS[2 + s3 % 2][:, 0:C]
                    dve.tensor_tensor(kj[:, s3 % 2, :], e, kvg[:, s3, 0:C], ALU.add).then_inc(sem("l3_keys"), 1)
                if new:
                    dve.wait_ge(sem("l3_rel"), t + 1)
                    wait_over(dve, "l3_encoded", t - 1)
                    dve.scalar_tensor_tensor(arg[:, s % 2, :], wtp, rel[:, s % 2:s % 2 + 1], btp, ALU.mult, ALU.add).then_inc(sem("l3_turns"), 1)
                if old:
                    if not isinstance(i3, int) or i3 > 0:
                        dve.wait_ge(sem(f"values_stored{s3}"), i3 * 16)
                    dve.tensor_tensor(ve[:, s3, :], e, kvg[:, s3, C:2 * C], ALU.add).then_inc(sem("l3_values"), 1)
                if new:
                    dve.wait_ge(sem("l3_turns"), t + 1)
                    wait_over(dve, "l3_angles", t)
                    dve.tensor_scalar(rnd, arg[:, s % 2, :], ROUND, ROUND, ALU.add, ALU.subtract).then_inc(sem("l3_rounded"), 1)
                if old:
                    dve.wait_ge(sem("l3_keys"), t3 + 1)
                    wait_over(dve, "l3_scored", t3)
                    qd = PS[4 + s3 % 2]
                    dve.scalar_tensor_tensor(prod[:, 0:128], qd[:, 0:128], 1.0, kj[:, s3 % 2, 0:128], ALU.mult, ALU.mult, accum_out=sc3[:, ds(t3, 1), 0])
                if new:
                    dve.wait_ge(sem("l3_rounded"), t + 1)
                    dve.tensor_tensor(arg[:, s % 2, :], arg[:, s % 2, :], rnd, ALU.subtract).then_inc(sem("l3_angles"), 1)
                if old:
                    dve.scalar_tensor_tensor(prod[:, 128:256], qd[:, 128:256], 1.0, kj[:, s3 % 2, 128:256], ALU.mult, ALU.mult, accum_out=sc3[:, ds(t3, 1), 1])\
                        .then_inc(sem("l3_scored"), 1)
                if new:
                    wait_over(dve, "l3_turned", t - 2)
                    onehot_of(dve, t, s % 3).then_inc(sem("l3_onehots"), 1)
            tiles(dve, body, 3)
            dve.wait_ge(sem("l3_scored"), T)
            dve.tensor_scalar(sc3, sc3, 128.0 ** -0.5, None, ALU.mult).then_inc(sem("scores_ready"), 1)
            dve.memset(acc3, 0.0)
            edge_max_vector(dve, 1, 2, mv3)
            wait_empty(dve, "amax1")
            dve.wait_ge(sem("scores_ready"), 2)
            dve.tensor_tensor(sc3, sc3, am3, ALU.subtract).then_inc(sem("scores_shifted"), 1)

            def sums(i, b):
                if tile := tile_at(i, b):
                    _, t, s = tile
                    wait_over(dve, "l3m_product", t - 2)
                    onehot_of(dve, t, s % 3).then_inc(sem("l3m_onehots"), 1)
                if tile := tile_at(i, b, 1):
                    accumulate(dve, "l3m", tile, acc3, PS[tile[2] % 2][0:P, 0:258], 258)
            tiles(dve, sums, 1)
            dve.wait_ge(sem("l3m_summed"), T)
            wait_empty(dve, "l3_skip")
            a = acc3.rearrange("p (w c) -> p w c", w=W)
            den = a[:, :, C:C + 2]
            link(dve.tensor_scalar(den, den, 1e-16, None, ALU.add))
            link(dve.reciprocal(den, den))
            for w in range(W):
                for k in range(2):
                    ins = dve.scalar_tensor_tensor(X[:, w, 128 * k:128 * k + 128], a[:, w, 128 * k:128 * k + 128], den[:, w, k:k + 1],
                                                   X[:, w, 128 * k:128 * k + 128], ALU.mult, ALU.add)
            link(ins)

        block = ctx.enter_context(nc.Block())

        @block.sync
        def _(sp):
            sort_sync(sp)
            for l in range(2, LAYERS + LAYERS % 2):
                sp.wait_ge(sem("xn_ready"), l)
                if l < LAYERS:
                    load_blob(sp, l)
                if l == 3:
                    l1_sync(sp)
                if l == 5:
                    sp.dma_start(xn_tab.rearrange("(w p) c -> p w c", p=P), XN[:, :, :]).then_inc(sem("xn_written"), 16)
                if l == 7:
                    l3_sync(sp)
            sp.wait_ge(sem("x_ready"), 1)
            sp.dma_start(d["out"].rearrange("(w p) c -> p w c", p=P), X[:, :, :]).then_inc(sem("out_written"), 16)
            sp.wait_ge(sem("out_written"), 16)

        @block.gpsimd
        def _(pool):
            sort_pool(pool)
            l0_pool(pool)
            if LAYERS > 2:
                l1_pool(pool)
            if LAYERS > 4:
                l2_pool(pool)
            if LAYERS > 6:
                l3_pool(pool)

        @block.vector
        def _(dve):
            link = linker(dve, "vector")
            sort_vector(dve)
            programs = [l0_vector, lambda e: ffn_vector(e, 1), l1_vector, l1f_vector, l2_vector,
                        lambda e: ffn_vector(e, 5), l3_vector, lambda e: ffn_vector(e, 7)]
            for l in range(LAYERS):
                if l:
                    layer_norm_vector(dve, l, link)
                programs[l](dve)
                if l == 0:
                    wait_empty(dve, "l0_back")
            dve.memset(small[:, :], 0.0).then_inc(sem("x_ready"), 1)

        @block.scalar
        def _(act):
            sort_scalar(act)
            xnt_scalar(act, 0)
            programs = [l0_scalar, lambda e: ffn_scalar(e, 1), l1_scalar, l1f_scalar, l2_scalar,
                        lambda e: ffn_scalar(e, 5), l3_scalar, lambda e: ffn_scalar(e, 7)]
            for l in range(LAYERS):
                if l:
                    std_scalar(act, l)
                programs[l](act)

        @block.tensor
        def _(pe):
            sort_tensor(pe)
            xnt_tensor(pe, 0)
            programs = [l0_tensor, lambda e: ffn_tensor(e, 1), l1_tensor, l1f_tensor, l2_tensor,
                        lambda e: ffn_tensor(e, 5), l3_tensor, lambda e: ffn_tensor(e, 7)]
            for l in range(LAYERS):
                programs[l](pe)


DIRECT = ["x", "src", "dst", "edge_attr_128", "edge_attr_256", "edge_attr_54", "edge_type_2", "edge_type_8",
          "edge_weight", "node_type_2", "node_vec"]


def kernel(**inputs):
    import concourse.bacc as bacc
    from concourse.bass_utils import run_bass_kernel_spmd as run

    inputs = {k: np.ascontiguousarray(v) for k, v in inputs.items()}
    nc = bacc.Bacc("TRN2", target_bir_lowering=False, num_devices=1)
    arrays = {k: inputs[k] for k in DIRECT}
    places, widths = [], []
    for l, parts in enumerate(blobs(inputs)):
        at, width = blob_places(parts)
        blob = np.zeros((128, width), np.float32)
        for name, a in parts:
            c, rows, cols = at[name]
            blob[:rows, c:c + cols] = a
        arrays[f"blob{l}"] = blob
        places.append(at)
        widths.append(width)
    d, sent = {}, {}
    for name, a in arrays.items():
        sent[f"in_{name}_dram"] = a
        d[name] = nc.dram_tensor(f"in_{name}_dram", a.shape, mybir.dt.from_np(a.dtype), kind="ExternalInput").ap()
    d["out"] = nc.dram_tensor("out_0_dram", (N, C), mybir.dt.float32, kind="ExternalOutput").ap()
    build(nc, d, places, widths)
    r = run(nc, [sent], core_ids=[0])
    return r.results[0]["out_0_dram"]
```

```python
import numpy as np
import concourse.bass as bass
from concourse import mybir
from contextlib import ExitStack

LAYERS = 8

N, C, E = 625, 256, 20000
P, W = 125, 5
TE = E // P
EP = 128
U = 6
T = (E + W * (EP - 1)) // EP
T += -T % U
TH = T // 2
NPAD = T * EP - E
NPC = next(c for c in range(1, NPAD + 1) if NPAD % c == 0 and NPAD // c <= 128)
G = 4
NB = 4
REC = 8
ROW = REC + 54 + C + 128
SRC_I, SRC, DST, DLOC, TYPE8, TYPE2, WEIGHT = range(7)
NR, NH, HD = 8, 8, 32
KVW = 2 * C
PAD = 1.0e6
BIG = 1.0e30
HALVES = [(0, 320), (320, 305)]


def rowsplit(a):
    k = a.shape[0] // 128
    return a.reshape(k, 128, -1).transpose(1, 0, 2).reshape(128, -1)


def stack(a):
    e, r, m = a.shape
    return a.reshape(e, r // 128, 128, m).transpose(2, 0, 1, 3).reshape(128, -1)


def twice(a):
    z = np.zeros((128, 128), a.dtype)
    z[:64, :64] = a
    z[64:, 64:] = a
    return z


def per_row(a, rows=128):
    return np.broadcast_to(a.reshape(1, -1), (rows, a.size))


def blobs(i):
    def attn_blocks():
        z = np.zeros((C, 16), np.float32)
        for h in range(NH):
            z[h * HD:(h + 1) * HD, h] = i["L1_gnn_attn_src"][h]
            z[h * HD:(h + 1) * HD, 8 + h] = i["L1_gnn_attn_dst"][h]
        return rowsplit(z)

    row = lambda a: a.reshape(1, -1)
    col = lambda a: rowsplit(a.reshape(-1, 1))
    b = [None] * 8
    b[0] = [("f1aT", i["L0_gnn_w_f1a"].T), ("f1b", i["L0_gnn_w_f1b"])]
    b[0] += [(n, rowsplit(i["L0_gnn_" + n])) for n in ("c1_wl", "c1_wr", "c2_wl", "c2_wr", "lin1_w", "lin2_w", "cat_w")]
    b[0] += [(n, col(i["L0_gnn_" + n])) for n in ("c1_bl", "c2_bl", "lin1_b", "lin2_b", "cat_b", "gn_w", "gn_b", "gn_ms")]
    b[1] = [("Wr", rowsplit(i["L0_ffn_Wr"])), ("br", row(i["L0_ffn_br"]))]
    b[1] += [(n, stack(i["L0_ffn_" + n])) for n in ("W1", "W2", "Wo")]
    b[1] += [(n, col(i["L0_ffn_" + n])) for n in ("b1", "g1", "be1", "m1", "v1", "b2", "g2", "be2", "m2", "v2")]
    b[1] += [("bo", i["L0_ffn_bo"])]
    w = i["L1_gnn_W"]
    b[2] = [("WT", stack(w.transpose(0, 2, 1))), ("attn", attn_blocks()), ("Wn", stack(w))]
    b[3] = [("W_fx", rowsplit(i["L1_ffn_W_fx"])), ("b_fx", row(i["L1_ffn_b_fx"])),
            ("W_x", rowsplit(i["L1_ffn_W_x"])), ("b_x", col(i["L1_ffn_b_x"])),
            ("W_slice", twice(i["L1_ffn_W_slice"])), ("b_slice", row(np.tile(i["L1_ffn_b_slice"], 8))),
            ("W_q", twice(i["L1_ffn_W_q"])), ("W_k", twice(i["L1_ffn_W_k"])), ("W_v", twice(i["L1_ffn_W_v"])),
            ("W_out", rowsplit(i["L1_ffn_W_out"])), ("b_out", row(i["L1_ffn_b_out"])),
            ("temp", per_row(i["L1_ffn_temperature"]))]
    b[4] = [("W0", stack(i["L2_gnn_W0"])), ("W1", stack(i["L2_gnn_W1"])), ("W2", stack(i["L2_gnn_W2"])),
            ("b0", col(i["L2_gnn_b0"])), ("b1", col(i["L2_gnn_b1"])), ("b2", row(i["L2_gnn_b2"]))]
    b[5] = [("W1", rowsplit(i["L2_ffn_W1"])), ("b1", col(i["L2_ffn_b1"])), ("Wg", rowsplit(i["L2_ffn_Wg"])),
            ("bg", row(i["L2_ffn_bg"])), ("Wd", stack(i["L2_ffn_Wd"])), ("bd", i["L2_ffn_bd"])]
    b[6] = [(n, rowsplit(i["L3_gnn_" + n])) for n in ("Wq", "Wk", "Wv", "Wskip", "We")]
    b[6] += [(n, row(i["L3_gnn_" + n])) for n in ("bq", "bk", "bv", "bskip")]
    b[6] += [("Wt", per_row(i["L3_gnn_Wt"])), ("bt", per_row(i["L3_gnn_bt"]))]
    b[7] = [("router", rowsplit(i["L3_ffn_router_w"].T)), ("w1", stack(i["L3_ffn_w1"])), ("b1", col(i["L3_ffn_b1"])),
            ("w2", stack(i["L3_ffn_w2"])), ("b2", i["L3_ffn_b2"])]
    return b


def blob_places(parts):
    places, at = {}, 0
    for name, a in parts:
        places[name] = (at, a.shape[0], a.shape[1])
        at += a.shape[1]
    return places, at


def build(nc, d, places, widths):
    f32, i32, bf16, f16 = mybir.dt.float32, mybir.dt.int32, mybir.dt.bfloat16, mybir.dt.float16
    ALU, ACT, AX = mybir.AluOpType, mybir.ActivationFunctionType, mybir.AxisListType
    ds = bass.ds
    ctx = ExitStack()
    with ctx:
        def sb(name, shape, dt=f32):
            return ctx.enter_context(nc.sbuf_tensor(name, shape, dt))

        sems = {}

        def sem(name):
            if name not in sems:
                sems[name] = ctx.enter_context(nc.semaphore(name))
            return sems[name]

        X = sb("X", [P, W, C])
        XN = sb("XN", [P, W, C])
        XNT = sb("XNT", [128, 2, N])
        ident = sb("ident", [128, 128])
        ones = sb("ones", [128, 128])
        iota = sb("iota", [128, T])
        zeros = sb("zeros", [128, 256])
        srt = sb("srt", [128, T, REC - 1])
        wid = sb("wid", [1, T + U - 1])
        wids = sb("wids", [1, T])
        widi = sb("widi", [1, T], i32)
        idx_src = sb("idx_src", [128, T], i32)
        idx_hs = sb("idx_hs", [128, T], i32)
        typ = sb("typ", [128, T, 2])
        since = sb("since", [128, T])
        time_w = sb("time_w", [128, 256])
        recv1 = sb("recv1", [P, W])
        ixb = sb("ixb", [128, U], i32)
        oh = sb("oh", [128, 3, P])
        stats = sb("stats", [P, W, 6])
        aggr = sb("aggr", [P, W, 2])
        rstd = sb("rstd", [P, W])
        small = sb("small", [128, 56])
        A_SIZE, B_SIZE = 21500, 23904
        arena = [sb("arena_gnn", [128, A_SIZE]), sb("arena_ffn", [128, B_SIZE])]
        size = [A_SIZE, B_SIZE]
        PSUM = ctx.enter_context(nc.psum_tensor("PSUM", [128, 8 * 512], f32))
        PS = [PSUM[:, 512 * b:512 * b + 512] for b in range(8)]

        def dram(name, shape, dt=f32):
            return nc.dram_tensor(name, shape, dt).ap()
        edge_tab = dram("edge_tab", (EP * T, ROW))
        xn_tab = dram("xn_tab", (N, C + 1))
        h_tab = dram("h_tab", (NR * N, C + NH))
        he_tab = dram("he_tab", (T, EP, C))
        kv_tab = dram("kv_tab", (N, KVW))
        turn_tab = dram("turn_tab", (T, EP, 128))
        ve_tab = dram("ve_tab", (T, EP, C))

        class Layer:
            def __init__(self, n, blob=True):
                self.n, self.ar = n, arena[n % 2]
                self.at = widths[n] if blob else 0

            def w(self, name, **dims):
                at, rows, cols = places[self.n][name]
                ap = self.ar[0:rows, at:at + cols]
                if not dims:
                    return ap
                keys = " ".join(dims)
                return ap.rearrange(f"p ({keys} m) -> p {keys} m", **dims)

            def work(self, rows, cols, at=None, **dims):
                if at is None:
                    at = self.at
                    self.at += cols
                    assert self.at <= size[self.n % 2], (self.n, self.at)
                ap = self.ar[0:rows, at:at + cols]
                if not dims:
                    return ap
                keys = " ".join(dims)
                return ap.rearrange(f"p ({keys} m) -> p {keys} m", **dims)

        groups = {}
        order = []
        emptied = {"act": 0, "dve": 0}

        def plan(stage, count, engine):
            groups[stage] = (len(order), count, engine)
            for _ in range(count):
                emptied[engine] += 1
                order.append((engine, emptied[engine]))

        def bank(stage, u):
            return PS[(groups[stage][0] + u) % 8]

        def wait_empty(eng, stage, u=None):
            first, count, _ = groups[stage]
            engine, k = order[first + (count - 1 if u is None else u)]
            eng.wait_ge(sem("emptied_by_" + engine), k)

        def wait_bank(eng, stage, u):
            g = groups[stage][0] + u
            if g >= 8:
                eng.wait_ge(sem("emptied_by_" + order[g - 8][0]), order[g - 8][1])

        def wait_full(eng, stage, u):
            eng.wait_ge(sem("product_ready"), groups[stage][0] + u + 1)

        def full(ins):
            ins.then_inc(sem("product_ready"), 1)

        def out_by(ins, engine):
            ins.then_inc(sem("emptied_by_" + engine), 1)

        EXPERTS = {1: ("mlp1", "mlp2", "mlpo"), 5: ("mlpo",), 7: ("mlp1", "mlpo")}

        def experts(kinds):
            return [(kind, s - lag) for s in range(8 + len(kinds) - 1)
                    for lag, kind in enumerate(kinds) if 0 <= s - lag < 8]

        plan("sort_total", 2, "act")


        for l in range(8):
            if l == 2:
                plan("l1_v", 8, "act")
            plan(f"xnt{l}", W, "act")
            if l == 0:
                plan("l0_wc", 1, "act")
                plan("l0_accT", W, "act")
                for s in (1, 2):
                    plan(f"l0_conv{s}", 4, "act")
                    plan(f"l0_lin{s}", 4, "act")
                plan("l0_cat", 4, "act")
                plan("l0_back", W, "dve")
            if l == 1:
                plan("gate1", W, "dve")
                for kind, e in experts(EXPERTS[l]):
                    plan(f"{kind}_{l}_{e}", W if kind == "mlpo" else 4, "dve" if kind == "mlpo" else "act")
                plan(f"coefT{l}", W, "act")
                plan(f"bias{l}", W, "dve")
            if l == 2:
                plan("l1_s", W, "act")
                for r in range(NR):
                    plan(f"l1_h{r}", W, "act")
                plan("seg_dst0", 2, "act")
                plan("seg_ends0", 1, "act")
                plan("scoreT0", 2 * NH, "act")
                plan("ends0", 4, "act")
                plan("carry0", 4, "act")
                plan("amax0", 2 * NH, "act")
            if l == 3:
                plan("xmT", 8, "act")
                plan("fx", W, "act")
                plan("slice", W, "dve")
                plan("swT", W, "act")
                plan("token", 4, "dve")
                for s in ("tokT", "qT", "kT", "v", "lg", "pT", "os"):
                    plan("t_" + s, 4, "dve" if s == "lg" else "act")
                plan("oxT", 8, "act")
                plan("l3_out", W, "dve")
            if l == 4:
                plan("aggT", W, "act")
                for t in range(2):
                    plan(f"g0_{t}", 8, "act")
                    plan(f"g1_{t}", 8, "act")
                    plan(f"g2_{t}", W, "dve")
            if l == 5:
                plan("hid", 16, "act")
                plan("gate5", W, "dve")
                for kind, e in experts(EXPERTS[l]):
                    plan(f"{kind}_{l}_{e}", W, "dve")
                plan(f"coefT{l}", W, "act")
                plan(f"bias{l}", W, "dve")
            if l == 6:
                for s in ("q", "k", "v"):
                    plan("l3_" + s, W, "act")
                plan("l3_skip", W, "dve")
                plan("seg_dst1", 2, "act")
                plan("seg_ends1", 1, "act")
                plan("scoreT1", 2 * 2, "act")
                plan("ends1", 4, "act")
                plan("carry1", 4, "act")
                plan("amax1", 2 * 2, "act")
            if l == 7:
                plan("gate7", W, "dve")
                for kind, e in experts(EXPERTS[l]):
                    plan(f"{kind}_{l}_{e}", W if kind == "mlpo" else 4, "dve" if kind == "mlpo" else "act")
                plan(f"coefT{l}", W, "act")
                plan(f"bias{l}", W, "dve")

        steps = {"vector": 0, "scalar": 0, "pool": 0}

        def linker(eng, name):
            def link(ins):
                steps[name] += 1
                ins.then_inc(sem(name + "_step"), 1)
                eng.wait_ge(sem(name + "_step"), steps[name])
            return link

        def tiles(eng, body, rest=0):
            for b in range(U):
                body(0, b)
            with eng.Fori(1, T // U) as i:
                for b in range(U):
                    body(i, b)
            for b in range(rest):
                body(T // U, b)

        def tile_at(i, b, lag=0):
            if isinstance(i, int) and not 0 <= i * U + b - lag < T:
                return None
            return i - (b < lag), i * U + (b - lag), (b - lag) % U

        def wait_over(eng, name, value):
            if not isinstance(value, int) or value > 0:
                eng.wait_ge(sem(name), value)

        TWO_PI = 2.0 * float(np.pi)
        ROUND = 1.5 * 2.0 ** 23
        dst_all = srt[:, :, DST - 1]

        def field(t, f):
            return srt[:, ds(t, 1), f - 1]

        S = Layer(1, blob=False)
        iota_i = S.work(128, N).bitcast(i32)
        iota_n = S.work(128, N)
        pad_i = S.work(NPAD // NPC, NPC).bitcast(i32)
        pad_n, pad_at = S.work(NPAD // NPC, NPC), S.work(NPAD // NPC, NPC)
        pad_row = S.work(NPAD // NPC, ROW)
        raw = S.work(P, 5 * TE, f=5)
        raw_i = raw.bitcast(i32)
        dstf = S.work(P, TE)
        rec = S.work(P, TE * REC, t=TE)
        rec_i = rec.bitcast(i32)
        earlier = S.work(P, 2 * TE)
        rank = S.work(P, NB * G, g=NB)
        junk = S.work(P, 2 * N)
        junk2 = S.work(P, 2 * TE)
        before = S.work(128, N)
        total = S.work(128, N)
        start = S.work(128, N)
        pos = S.work(P, NB * G, g=NB)
        place = S.work(P, NB * G, g=NB).bitcast(i32)
        strict = S.work(P, 128)
        last_row = S.work(128, 128)
        oh16 = S.work(P, 4 * 314, b=4).bitcast(f16)[:, :, 0:N]
        iota16 = S.work(P, 314).bitcast(f16)[:, 0:N]
        strict16 = S.work(P, 64).bitcast(f16)
        edges = S.work(P, NB * G * ROW, g=NB, j=G)
        zeros_16 = zeros[:, :].bitcast(f16)
        sel0 = sb("sel0", [128, 8])
        sel127 = sb("sel127", [128, 8])
        ntype = sb("ntype", [P, W])
        ntype_i = sb("ntype_i", [P, W], i32)

        def groups_of_tiles(eng, body):
            for b in range(NB):
                body(b, b)
            with eng.Fori(1, TE // G // NB) as i:
                for b in range(NB):
                    body(i * NB + b, b)

        def wait_scattered(eng, g, b):
            if not isinstance(g, int):
                eng.wait_ge(sem(f"scattered{b}"), (g - b) * (16 * G // NB))

        def sort_sync(sp):
            for n, name in enumerate(("dst", "src", "edge_type_8", "edge_type_2")):
                sp.dma_start(raw_i[:, n, :], d[name].rearrange("(p t) -> p t", p=P)).then_inc(sem("edges_loaded"), 16)
            sp.dma_start(raw[:, 4, :], d["edge_weight"].rearrange("(p t) -> p t", p=P)).then_inc(sem("edges_loaded"), 16)
            sp.dma_start(ntype_i[:, :], d["node_type_2"].rearrange("(w p) -> p w", p=P),
                         allow_slow_non_contiguous=True).then_inc(sem("edges_loaded"), 16)
            at = places[6]["Wt"][0]
            sp.dma_start(time_w[:, :], d["blob6"][:, at:at + 256]).then_inc(sem("edges_loaded"), 16)
            sp.dma_start(X[:, :, :], d["x"].rearrange("(w p) c -> p w c", p=P)).then_inc(sem("x_loaded"), 16)
            load_blob(sp, 0)
            sp.dma_start(xn_tab[:, C:C + 1], d["node_vec"].rearrange("(n a) -> n a", a=1),
                         allow_slow_non_contiguous=True).then_inc(sem("xn_written"), 16)
            sp.wait_ge(sem("xn_ready"), 1)
            sp.dma_start(xn_tab[:, 0:C].rearrange("(w p) c -> p w c", p=P), XN[:, :, :]).then_inc(sem("xn_written"), 16)

            def features(g, b):
                wait_scattered(sp, g, b)
                at = REC
                for n in (54, C, 128):
                    src = d[f"edge_attr_{n}"].rearrange("(p t) c -> p t c", p=P)
                    sp.dma_start(edges[:, b, :, at:at + n], src[:, ds(g * G, G), :]).then_inc(sem(f"features_loaded{b}"), 16)
                    at += n
            groups_of_tiles(sp, features)
            for b in range(NB):
                sp.wait_ge(sem(f"scattered{b}"), 16 * TE // NB)
            sp.wait_ge(sem("pads_scattered"), 16 * NPC)

        def load_blob(sp, l):
            w = widths[l]
            for c in range(0, w, 4096):
                n = min(4096, w - c)
                sp.dma_start(arena[l % 2][:, c:c + n], d[f"blob{l}"][:, c:c + n]).then_inc(sem("blob_gnn" if l % 2 == 0 else "blob_ffn"), 16)

        def blob_count(l):
            return 16 * sum(-(-widths[k] // 4096) for k in range(l % 2, l + 1, 2))

        def wait_blob(eng, l):
            eng.wait_ge(sem("blob_gnn" if l % 2 == 0 else "blob_ffn"), blob_count(l))

        def sort_pool(pool):
            link = linker(pool, "pool")
            pool.memset(ones[:, :], 1.0)
            pool.memset(zeros[:, :], 0.0).then_inc(sem("constants"), 1)
            pool.iota(iota_i, pattern=[[1, N]], base=0, channel_multiplier=0).then_inc(sem("constants"), 1)
            pool.iota(pad_i, pattern=[[1, NPC]], base=0, channel_multiplier=NPC).then_inc(sem("constants"), 1)
            link(pool.memset(pad_row, 0.0))
            pool.memset(pad_row[:, DST:DLOC + 1], PAD).then_inc(sem("constants"), 1)
            link(pool.memset(ident[:, :], 0.0))
            link(pool.affine_select(out=ident[:, :], in_=ident[:, :], compare_op=ALU.not_equal, fill=1.0, base=0,
                                    pattern=[[-1, 128]], channel_multiplier=1))
            link(pool.memset(strict, 1.0))
            link(pool.affine_select(out=strict, in_=strict, compare_op=ALU.is_gt, fill=0.0, base=0,
                                    pattern=[[1, 128]], channel_multiplier=-1))
            link(pool.memset(last_row, 0.0))
            link(pool.affine_select(out=last_row, in_=last_row, compare_op=ALU.not_equal, fill=1.0, base=-127,
                                    pattern=[[0, 128]], channel_multiplier=1))
            pool.tensor_copy(sel127[:, :], last_row[:, 0:8]).then_inc(sem("constants"), 1)
            link(pool.memset(sel0[:, :], 0.0))
            pool.affine_select(out=sel0[:, :], in_=sel0[:, :], compare_op=ALU.not_equal, fill=1.0, base=0,
                               pattern=[[0, 8]], channel_multiplier=1).then_inc(sem("constants"), 1)
            pool.wait_ge(sem("pads_placed"), 1)
            for c in range(NPC):
                pool.indirect_dma_start(edge_tab, bass.IndirectOffsetOnAxis(ap=pad_i[:, c:c + 1], axis=0),
                                        pad_row, None).then_inc(sem("pads_scattered"), 16)

            def scatter(g, b):
                pool.wait_ge(sem(f"features_loaded{b}"), 48)
                pool.wait_ge(sem(f"group_placed{b}"), 1)
                for j in range(G):
                    pool.indirect_dma_start(edge_tab, bass.IndirectOffsetOnAxis(ap=place[:, b, j:j + 1], axis=0),
                                            edges[:, b, j, :], None).then_inc(sem(f"scattered{b}"), 16)
                pool.sem_inc(sem(f"features_loaded{b}"), -48)
                pool.sem_inc(sem(f"group_placed{b}"), -1)
            groups_of_tiles(pool, scatter)

        def sort_vector(dve):
            link = linker(dve, "vector")
            dve.wait_ge(sem("constants"), 2)
            link(dve.tensor_copy(iota_n, iota_i))
            dve.tensor_copy(iota[:, :], iota_n[:, 0:T])
            dve.tensor_copy(iota16, iota_n[0:P, :])
            dve.wait_ge(sem("edges_loaded"), 112)
            dve.tensor_scalar(time_w[:, 0:128], time_w[:, 0:128], 1.0 / TWO_PI, None, ALU.mult)
            dve.tensor_scalar(time_w[:, 128:256], time_w[:, 128:256], 1.0 / TWO_PI, 0.25, ALU.mult, ALU.add)
            dve.tensor_copy(ntype[:, :], ntype_i[:, :])
            link(dve.tensor_copy(dstf, raw_i[:, 0, :]))
            dve.wait_ge(sem("constants"), 6)
            dve.wait_ge(sem("pool_step"), 8)
            dve.tensor_copy(strict16, strict)
            def onehot(i, b):
                if not isinstance(i, int):
                    dve.wait_ge(sem("onehot_added"), i * 4 + b - 3)
                dve.tensor_scalar(oh16[:, b, :], iota16, dstf[:, ds(i * 4 + b, 1)], None, ALU.is_equal).then_inc(sem("onehot_ready"), 1)
            for b in range(4):
                onehot(0, b)
            with dve.Fori(1, TE // 4) as i:
                for b in range(4):
                    onehot(i, b)
            link(dve.memset(rec, 0.0))
            dve.tensor_copy(rec_i[:, :, SRC_I], raw_i[:, 1, :])
            dve.tensor_copy(rec[:, :, SRC], raw_i[:, 1, :])
            dve.tensor_copy(rec[:, :, DST], dstf)
            dve.tensor_copy(rec[:, :, TYPE8], raw_i[:, 2, :])
            dve.tensor_copy(rec[:, :, TYPE2], raw_i[:, 3, :])
            dve.tensor_copy(rec[:, :, WEIGHT], raw[:, 4, :])
            link(dve.tensor_scalar(rec[:, :, DLOC], dstf, float(P), None, ALU.is_ge))
            for w in range(2, W):
                link(dve.scalar_tensor_tensor(rec[:, :, DLOC], dstf, float(w * P), rec[:, :, DLOC], ALU.is_ge, ALU.add))
            link(dve.scalar_tensor_tensor(rec[:, :, DLOC], rec[:, :, DLOC], -float(P), dstf, ALU.mult, ALU.add))
            dve.memset(earlier[:, 0:TE], 1.0)
            link(dve.memset(earlier[:, TE:2 * TE], 0.0))

            wait_empty(dve, "sort_total")
            for w in range(W):
                c = slice(w * P, (w + 1) * P)
                ins = dve.tensor_tensor_scan(start[:, c], total[:, c], zeros[:, 0:P], 0.0, ALU.add, ALU.add)
            link(ins)
            count = small[:, 32:32 + W]
            link(dve.tensor_copy(count, start.rearrange("p (w n) -> p w n", w=W)[:, :, P - 1]))
            wt, wt_i = small[:, 0:W], small[:, 8:8 + W].bitcast(i32)
            link(dve.tensor_scalar(wt_i, count, float(EP - 1), None, ALU.add))
            link(dve.tensor_scalar(wt_i, wt_i, EP.bit_length() - 1, None, ALU.arith_shift_right))
            link(dve.tensor_copy(wt, wt_i))
            incl, wstart, wpos = small[:, 16:16 + W], small[:, 24:24 + W], small[:, 40:40 + W]
            link(dve.tensor_tensor_scan(incl, wt, zeros[:, 0:W], 0.0, ALU.add, ALU.add))
            link(dve.tensor_tensor(wstart, incl, wt, ALU.subtract))
            link(dve.tensor_scalar(wpos, wstart, float(EP), None, ALU.mult))
            gap0 = small[:, 48:48 + W]
            link(dve.tensor_tensor_scan(incl, count, zeros[:, 0:W], 0.0, ALU.add, ALU.add))
            link(dve.tensor_tensor(incl, incl, count, ALU.subtract))
            link(dve.tensor_tensor(gap0, wpos, incl, ALU.subtract))
            npp = NPAD // NPC
            link(dve.tensor_copy(pad_n, pad_i))
            link(dve.tensor_copy(pad_at, pad_n))
            hit = junk[0:npp, 0:NPC]
            for w in range(W):
                link(dve.tensor_scalar(hit, pad_n, gap0[0:npp, w:w + 1], count[0:npp, w:w + 1], ALU.is_ge, ALU.mult))
                link(dve.tensor_tensor(pad_at, pad_at, hit, ALU.add))
            dve.tensor_copy(pad_i, pad_at).then_inc(sem("pads_placed"), 1)
            link(dve.tensor_tensor(start, start, total, ALU.subtract))
            for w in range(W):
                c = slice(w * P, (w + 1) * P)
                ins = dve.tensor_scalar(start[:, c], start[:, c], wpos[:, w:w + 1], None, ALU.add)
            link(ins)
            link(dve.tensor_tensor(before, before, start, ALU.add))
            link(dve.memset(wid[:, :], 0.0))
            for w in range(1, W):
                link(dve.scalar_tensor_tensor(wid[:, 0:T], iota[0:1, :], wstart[0:1, w:w + 1], wid[:, 0:T], ALU.is_ge, ALU.add))
            link(dve.tensor_copy(wids[:, :], wid[:, U - 1:T + U - 1]))
            for k in reversed(range(U - 1)):
                link(dve.scalar_tensor_tensor(wids[:, :], wids[:, :], 8.0, wid[:, k:T + k], ALU.mult, ALU.add))
            dve.tensor_scalar(widi[:, :], wids[:, :], 512.0, None, ALU.mult)
            layer_norm_vector(dve, 0, link)

            def places_of(g, b):
                wait_scattered(dve, g, b)
                for j in range(G):
                    wait_over(dve, "ranked", g * G + j - 1)
                    dve.scalar_tensor_tensor(junk2[:, TE * (j % 2):TE * (j % 2) + TE], dstf, dstf[:, ds(g * G + j, 1)],
                                             earlier[:, ds(TE - g * G - j, TE)], ALU.is_equal, ALU.mult,
                                             accum_out=rank[:, b, j:j + 1]).then_inc(sem("ranked"), 1)
                    wait_over(dve, "place_found", g * G + j - 1)
                    dve.scalar_tensor_tensor(junk[0:P, N * (j % 2):N * (j % 2) + N], iota_n[0:P, :], dstf[:, ds(g * G + j, 1)],
                                             before[0:P, :], ALU.is_equal, ALU.mult, accum_out=pos[:, b, j:j + 1])\
                        .then_inc(sem("place_found"), 1)
                dve.tensor_copy(edges.bitcast(i32)[:, b, :, 0:REC], rec_i[:, ds(g * G, G), :])
                dve.wait_ge(sem("place_found"), g * G + G)
                dve.tensor_tensor(place[:, b, :], pos[:, b, :], rank[:, b, :], ALU.add).then_inc(sem(f"group_placed{b}"), 1)
            groups_of_tiles(dve, places_of)

        def sort_tensor(pe):
            pe.wait_ge(sem("onehot_ready"), 1)
            for b, n in ((0, 512), (1, N - 512)):
                pe.matmul(PS[b][:, 0:n], zeros_16[0:P, 0:128], zeros_16[0:P, 0:n], start=True, stop=False)

            def add(t, b):
                pe.wait_ge(sem("onehot_ready"), t + 1)
                pe.matmul(PS[0][:, :], strict16, oh16[:, b, 0:512], start=False, stop=False)
                pe.matmul(PS[1][:, 0:N - 512], strict16, oh16[:, b, 512:N], start=False, stop=False).then_inc(sem("onehot_added"), 1)
            with pe.Fori(0, TE // 4) as i:
                for b in range(4):
                    add(i * 4 + b, b)
            for b, n in ((0, 512), (1, N - 512)):
                ins = pe.matmul(PS[b][:, 0:n], zeros_16[0:P, 0:128], zeros_16[0:P, 0:n], start=False, stop=True)
            ins.then_inc(sem("histogram_ready"), 1)
            pe.wait_ge(sem("histogram_copied"), 2)
            for u, (c, n) in enumerate(((0, 512), (512, N - 512))):
                full(pe.matmul(bank("sort_total", u)[:, 0:n], last_row, before[:, c:c + n], start=True, stop=True))

        def sort_scalar(act):
            act.wait_ge(sem("histogram_ready"), 1)
            act.activation(before[:, 0:512], PS[0][:, :], ACT.Copy).then_inc(sem("histogram_copied"), 1)
            act.activation(before[:, 512:N], PS[1][:, 0:N - 512], ACT.Copy).then_inc(sem("histogram_copied"), 1)
            for u, (c, n) in enumerate(((0, 512), (512, N - 512))):
                wait_full(act, "sort_total", u)
                out_by(act.activation(total[:, c:c + n], bank("sort_total", u)[:, 0:n], ACT.Copy), "act")
            std_scalar(act, 0)

        def layer_norm_vector(dve, l, link):
            if l == 0:
                dve.wait_ge(sem("x_loaded"), 16)
            for w in range(W):
                ins = dve.bn_stats(stats[:, w, :], X[:, w, :])
            link(ins)
            for w in range(W):
                ins = dve.bn_aggr(aggr[:, w, :], stats[:, w, :])
            link(ins)
            dve.tensor_scalar(rstd[:, :], aggr[:, :, 1], 1e-5, None, ALU.add).then_inc(sem("variance_ready"), 1)
            dve.wait_ge(sem("deviation_ready"), l + 1)
            link(dve.reciprocal(rstd[:, :], rstd[:, :]))
            for w in range(W):
                ins = dve.tensor_scalar(XN[:, w, :], X[:, w, :], aggr[:, w, 0:1], rstd[:, w:w + 1], ALU.subtract, ALU.mult)
            ins.then_inc(sem("xn_ready"), 1)

        def std_scalar(act, l):
            act.wait_ge(sem("variance_ready"), l + 1)
            act.activation(rstd[:, :], rstd[:, :], ACT.Sqrt).then_inc(sem("deviation_ready"), 1)

        def turn(pe, stage, u, outs):
            wait_bank(pe, stage, u)
            for (c, m), a in outs:
                k = a.shape[0]
                ins = pe.transpose(bank(stage, u)[0:a.shape[1], c:c + k], a, ident[0:k, 0:k])
            full(ins)

        def turn_nodes(pe, stage, a, k):
            for w in range(W):
                turn(pe, stage, w, [((P * j, P), a[:, w, 128 * j:128 * j + 128]) for j in range(k)])

        def turned_nodes(act, stage, out, k):
            for w in range(W):
                wait_full(act, stage, w)
                out_by(act.activation(out[:, :, P * w:P * w + P],
                                      bank(stage, w)[:, 0:k * P].rearrange("p (k n) -> p k n", k=k), ACT.Copy), "act")

        def xnt_tensor(pe, l):
            pe.wait_ge(sem("xn_ready"), l + 1)
            turn_nodes(pe, f"xnt{l}", XN, 2)

        def xnt_scalar(act, l):
            turned_nodes(act, f"xnt{l}", XNT, 2)

        def lin(pe, stage, pairs, M):
            for m in range(M // 128):
                for h, (c, n) in enumerate(HALVES):
                    u = 2 * m + h
                    wait_bank(pe, stage, u)
                    todo = [(w[:, k, 128 * m:128 * m + 128], r[:, k, c:c + n]) for w, r in pairs for k in range(w.shape[1])]
                    for j, (w, r) in enumerate(todo):
                        ins = pe.matmul(bank(stage, u)[:, 0:n], w, r, start=j == 0, stop=j == len(todo) - 1)
                    full(ins)

        def lin_out(act, stage, out, M, func, bias=None, scale=1.0):
            for m in range(M // 128):
                for h, (c, n) in enumerate(HALVES):
                    u = 2 * m + h
                    wait_full(act, stage, u)
                    out_by(act.activation(out[:, m, c:c + n], bank(stage, u)[:, 0:n], func,
                                          bias=0.0 if bias is None else bias[:, m:m + 1],
                                          scale=scale if isinstance(scale, float) else scale[:, m:m + 1]), "act")

        def nodes(pe, stage, a, w, n, bias=None):
            for v in range(W):
                node_group(pe, stage, v, a, w, n, bias)

        def node_group(pe, stage, v, a, w, n, bias=None):
            wait_bank(pe, stage, v)
            K = w.shape[1]
            for k in range(K):
                ins = pe.matmul(bank(stage, v)[0:P, 0:n], a[:, k, P * v:P * v + P], w[:, k, :],
                                start=k == 0, stop=k == K - 1 and bias is None)
            if bias is not None:
                ins = pe.matmul(bank(stage, v)[0:P, 0:n], ones[0:1, 0:P], bias, start=False, stop=True)
            full(ins)

        def wait_x(dve, stage, v):
            dve.wait_ge(sem("emptied_by_dve"), order[groups[stage][0] + v][1] - W)

        def add_to_x(dve, stage, n=C):
            for v in range(W):
                wait_full(dve, stage, v)
                out_by(dve.tensor_tensor(X[:, v, :], bank(stage, v)[0:P, 0:n], X[:, v, :], ALU.add), "dve")

        def gathers(pool, loop, idx, table, buf, free, stored=None):
            for b in range(U):
                wait_over(pool, f"gathered{b}", LOOPS.index(loop) * (T // U) * 16)

            def body(i, b):
                i, t, b = tile_at(i, b)
                wait_over(pool, free, t - U + 1)
                if stored:
                    wait_over(pool, f"{stored}{b}", i * 16)
                if b % (U // 2) == 0:
                    if not isinstance(i, int):
                        for s in range(b + 1, b + U // 2):
                            wait_gathered(pool, loop, i - 1, s)
                    pool.tensor_copy(ixb[:, b:b + U // 2], idx[:, ds(t, U // 2)]).then_inc(sem("slot_ready"), 1)
                else:
                    pool.sem_inc(sem("slot_ready"), 1)
                pool.wait_ge(sem("slot_ready"), 1)
                pool.indirect_dma_start(buf[:, b, :], None, table,
                                        bass.IndirectOffsetOnAxis(ap=ixb[:, b:b + 1], axis=0)).then_inc(sem(f"gathered{b}"), 16)
                pool.sem_inc(sem("slot_ready"), -1)
            tiles(pool, body)

        LOOPS = ("l0", "l1s", "l2", "l3")

        def wait_gathered(eng, loop, i, b):
            eng.wait_ge(sem(f"gathered{b}"), (i + (LOOPS.index(loop) * (T // U) + 1)) * 16)

        def onehot_of(dve, t, slot):
            return dve.tensor_scalar(oh[:, slot, :], iota[:, 0:P], field(t, DLOC), None, ALU.is_equal)

        def open_sums(pe, n):
            for w in range(W):
                pe.matmul(PS[w][0:P, 0:n], zeros_16[:, 0:P], zeros_16[:, 0:n], start=True, stop=False)

        windows = {}

        def window_of(pe, i, b, lag):
            if tile := tile_at(i, b, lag):
                k = 0 if isinstance(i, int) else b
                if k == 0:
                    windows[0] = pe.value_load(widi[0:1, ds(tile[1], 1)], min_val=0, max_val=512 * 8 ** U)
                w = pe.scalar_reg_alu(ALU.logical_shift_right, windows[0], 3 * k) if k else windows[0]
                return pe.snap(pe.scalar_reg_alu(ALU.bitwise_and, w, 7 * 512), min_val=0, max_val=(W - 1) * 512)

        def add_up(pe, loop, w, onehot, part, n):
            pe.matmul(PSUM[0:P, ds(w, n)], onehot, part, start=False, stop=False).then_inc(sem(loop + "_product"), 1)

        def close_sums(pe, loop, n):
            for w in range(W):
                ins = pe.matmul(PS[w][0:P, 0:n], zeros_16[:, 0:P], zeros_16[:, 0:n], start=False, stop=True)
            ins.then_inc(sem(loop + "_summed"), 1)

        def take_sums(act, loop, acc, n):
            act.wait_ge(sem(loop + "_summed"), 1)
            for w in range(W):
                act.activation(acc[:, n * w:n * w + n], PS[w][0:P, 0:n], ACT.Copy).then_inc(sem(loop + "_taken"), 1)

        L0 = Layer(0)
        wc = L0.work(54, C)
        xg0 = L0.work(128, U * (C + 1), u=U)
        er0 = L0.work(128, U * (REC + 54 + C), u=U)
        f54T = L0.work(54, 2 * 128, u=2)
        gx0 = L0.work(128, 2 * C, u=2)
        msg0 = L0.work(128, 3 * 512, u=3)
        acc0 = L0.work(P, W * 512)
        accT = L0.work(128, 4 * N, k=4)
        conv = L0.work(128, 2 * N, k=2)
        linv = L0.work(128, 2 * N, k=2)
        hT = L0.work(128, 4 * N, k=4)
        catT = accT[:, 0:2, :]
        gnst = L0.work(128, 64)

        def l0_sync(sp):
            def body(i, b):
                i, t, s = tile_at(i, b)
                wait_over(sp, "l0_messages", t - U + 1)
                sp.dma_start(er0[:, s, :], edge_tab.rearrange("(t p) r -> t p r", p=EP)[ds(t, 1), :, 0:REC + 54 + C]
                             .rearrange("a p r -> p (a r)")).then_inc(sem(f"edges_back{s}"), 16)
            tiles(sp, body)

        def l0_pool(pool):
            pool.wait_ge(sem("xn_written"), 32)

            def body(i, b):
                pool.wait_ge(sem(f"edges_back{b}"), 16)
                pool.indirect_dma_start(xg0[:, b, :], None, xn_tab,
                                        bass.IndirectOffsetOnAxis(ap=er0[:, b, SRC_I:SRC_I + 1].bitcast(i32), axis=0))\
                    .then_inc(sem(f"gathered{b}"), 16)
                pool.sem_inc(sem(f"edges_back{b}"), -16)
            tiles(pool, body)

        def l0_tensor(pe):
            wait_blob(pe, 0)
            wait_bank(pe, "l0_wc", 0)
            full(pe.matmul(bank("l0_wc", 0)[0:54, 0:C], L0.w("f1aT"), L0.w("f1b"), start=True, stop=True))
            wait_empty(pe, "l0_wc")
            open_sums(pe, 512)

            def body(i, b):
                w = window_of(pe, i, b, 2)
                if tile := tile_at(i, b):
                    _, t, s = tile
                    wait_gathered(pe, "l0", *tile[::2])
                    wait_over(pe, "l0_featuresT", t)
                    pe.transpose(PS[5][:, 0:128], er0[:, s, REC:REC + 128], ident[:, :]).then_inc(sem("l0_turned"), 1)
                if tile := tile_at(i, b, 1):
                    _, t, s = tile
                    pe.wait_ge(sem("l0_featuresT"), t + 1)
                    wait_over(pe, "l0_gated", t - 1)
                    pe.matmul(PS[6 + s % 2][:, 0:C], f54T[:, s % 2, :], wc, start=True, stop=True).then_inc(sem("l0_gate"), 1)
                if tile := tile_at(i, b, 2):
                    _, t, s = tile
                    pe.wait_ge(sem("l0_messages"), t + 1)
                    add_up(pe, "l0", w, oh[:, s % 3, :], msg0[:, s % 3, :], 512)
            tiles(pe, body, 2)
            close_sums(pe, "l0", 512)
            pe.wait_ge(sem("l0_taken"), W)
            for w in range(W):
                a = acc0.rearrange("p (w c) -> p w c", w=W)
                turn(pe, "l0_accT", w, [((P * k, P), a[:, w, 128 * k:128 * k + 128]) for k in range(4)])
            wait_empty(pe, "l0_accT")
            for s in (1, 2):
                lin(pe, f"l0_conv{s}", [(L0w(f"c{s}_wl", 2), accT[:, 2 * s - 2:2 * s, :]), (L0w(f"c{s}_wr", 2), XNT)], C)
                wait_empty(pe, f"l0_conv{s}")
                lin(pe, f"l0_lin{s}", [(L0w(f"lin{s}_w", 2), conv)], C)
            pe.wait_ge(sem("l0_leaky"), 2)
            lin(pe, "l0_cat", [(L0w("cat_w", 4), hT)], C)
            pe.wait_ge(sem("l0_normed"), 2)
            for w in range(W):
                turn(pe, "l0_back", w, [((128 * k, 128), catT[:, k, P * w:P * w + P]) for k in range(2)])

        def L0w(name, k=None):
            return L0.w(name, k=k) if k else L0.w(name)

        def l0_scalar(act):
            wait_full(act, "l0_wc", 0)
            out_by(act.activation(wc, bank("l0_wc", 0)[0:54, 0:C], ACT.Copy), "act")

            def body(i, b):
                i, t, s = tile_at(i, b)
                wait_gathered(act, "l0", i, s)
                act.activation(since[:, ds(t, 1)], xg0[:, s, C:C + 1], ACT.Copy)
                act.activation(srt[:, ds(t, 1), :].rearrange("p a f -> p (a f)"), er0[:, s, SRC:REC], ACT.Copy).then_inc(sem("records_kept"), 1)
                act.wait_ge(sem("l0_turned"), t + 1)
                wait_over(act, "l0_gate", t - 1)
                act.activation(f54T[:, s % 2, :], PS[5][0:54, 0:128], ACT.Copy).then_inc(sem("l0_featuresT"), 1)
            tiles(act, body)
            take_sums(act, "l0", acc0, 512)
            turned_nodes(act, "l0_accT", accT, 4)
            wait_blob(act, 0)
            for s in (1, 2):
                lin_out(act, f"l0_conv{s}", conv, C, ACT.Identity, L0w(f"c{s}_bl", None))
                if s == 2:
                    act.wait_ge(sem("l0_leaky"), 1)
                lin_out(act, f"l0_lin{s}", linv, C, ACT.Identity, L0w(f"lin{s}_b", None))
            lin_out(act, "l0_cat", catT, C, ACT.Identity, L0w("cat_b", None))
            act.wait_ge(sem("l0_group_var"), 1)
            act.activation(gnst[:, 20:22], gnst[:, 18:20], ACT.Sqrt).then_inc(sem("l0_group_std"), 1)
            act.wait_ge(sem("l0_scaled"), 1)
            for k in range(2):
                act.activation(catT[:, k, :], catT[:, k, :], ACT.Identity, bias=gnst[:, 26 + k:27 + k],
                               scale=gnst[:, 22 + k:23 + k]).then_inc(sem("l0_normed"), 1)

        def l0_vector(dve):
            link = linker(dve, "vector")

            def body(i, b):
                if tile := tile_at(i, b, 1):
                    i1, t, s = tile
                    dve.wait_ge(sem("l0_gate"), t + 1)
                    dve.wait_ge(sem("l0_gx"), t + 1)
                    wait_over(dve, "l0_product", t - 2)
                    dve.tensor_tensor(msg0[:, s % 3, 0:C], PS[6 + s % 2][:, 0:C], gx0[:, s % 2, :], ALU.mult).then_inc(sem("l0_gated"), 1)
                if tile2 := tile_at(i, b):
                    i0, t0, s0 = tile2
                    wait_over(dve, "l0_product", t0 - 2)
                    wait_gathered(dve, "l0", i0, s0)
                    dve.tensor_scalar(oh[:, s0 % 3, :], iota[:, 0:P], er0[:, s0, DLOC:DLOC + 1], None, ALU.is_equal)
                if tile:
                    dve.wait_ge(sem("l0_gated"), t + 1)
                    dve.tensor_tensor(msg0[:, s % 3, C:2 * C], msg0[:, s % 3, 0:C], er0[:, s, REC + 54:], ALU.mult).then_inc(sem("l0_messages"), 1)
                if tile2:
                    dve.tensor_tensor(gx0[:, s0 % 2, :], er0[:, s0, REC + 54:], xg0[:, s0, 0:C], ALU.mult).then_inc(sem("l0_gx"), 1)
            tiles(dve, body, 1)
            dve.wait_ge(sem("records_kept"), T)
            dve.tensor_copy(idx_src[:, :], srt[:, :, SRC - 1])
            dve.tensor_tensor(since[:, :], since[:, :], srt[:, :, WEIGHT - 1], ALU.subtract)
            dve.scalar_tensor_tensor(idx_hs[:, :], srt[:, :, TYPE8 - 1], float(N), srt[:, :, SRC - 1], ALU.mult, ALU.add)
            for k in range(2):
                ins = dve.tensor_scalar(typ[:, :, k], srt[:, :, TYPE2 - 1], float(k), None, ALU.is_equal)
            ins.then_inc(sem("indices_ready"), 1)
            for s in (1, 2):
                wait_empty(dve, f"l0_lin{s}")
                dve.scalar_tensor_tensor(hT[:, 2 * s - 2:2 * s, :], linv, 0.1, linv, ALU.mult, ALU.max).then_inc(sem("l0_leaky"), 1)
            wait_empty(dve, "l0_cat")
            g = gnst
            for k in range(2):
                for h, (c, n) in enumerate(HALVES):
                    ins = dve.bn_stats(g[:, 12 * k + 6 * h:12 * k + 6 * h + 6], catT[:, k, c:c + n])
            link(ins)
            for k in range(2):
                ins = dve.bn_aggr(g[:, 30 + 2 * k:32 + 2 * k], g[:, 12 * k:12 * k + 12])
            link(ins)
            mean, var = g[:, 30:34:2], g[:, 31:35:2]
            ms, gw, gb = L0w("gn_ms", None), L0w("gn_w", None), L0w("gn_b", None)
            link(dve.tensor_tensor(g[:, 36:38], mean, ms, ALU.mult))
            link(dve.tensor_tensor(g[:, 38:40], mean, g[:, 36:38], ALU.subtract))
            link(dve.tensor_tensor(g[:, 40:42], g[:, 38:40], g[:, 38:40], ALU.mult))
            dve.scalar_tensor_tensor(g[:, 18:20], var, 1e-5, g[:, 40:42], ALU.add, ALU.add).then_inc(sem("l0_group_var"), 1)
            dve.wait_ge(sem("l0_group_std"), 1)
            link(dve.reciprocal(g[:, 24:26], g[:, 20:22]))
            link(dve.tensor_tensor(g[:, 22:24], g[:, 24:26], gw, ALU.mult))
            link(dve.tensor_tensor(g[:, 28:30], g[:, 36:38], g[:, 22:24], ALU.mult))
            dve.tensor_tensor(g[:, 26:28], gb, g[:, 28:30], ALU.subtract).then_inc(sem("l0_scaled"), 1)
            add_to_x(dve, "l0_back")

        def soft_max(dve, act_sem, lg, rows, mx, link):
            bc = lambda a: a.unsqueeze(2).broadcast_to((rows, W, 8))
            link(dve.tensor_reduce(mx, lg, AX.X, ALU.max))
            dve.tensor_tensor(lg, lg, bc(mx), ALU.subtract).then_inc(sem("gate_shifted"), 1)
            dve.wait_ge(sem("gate_exp"), act_sem)
            link(dve.tensor_reduce(mx, lg, AX.X, ALU.add))
            link(dve.reciprocal(mx, mx))
            link(dve.tensor_tensor(lg, lg, bc(mx), ALU.mult))

        def first_max(dve, lg, mx, hit, number, link):
            bc = lambda a: a.unsqueeze(2).broadcast_to((P, W, 8))
            io = iota[0:P, 0:8].unsqueeze(1).broadcast_to((P, W, 8))
            link(dve.tensor_reduce(mx, lg, AX.X, ALU.max))
            link(dve.tensor_tensor(hit, lg, bc(mx), ALU.is_equal))
            link(dve.scalar_tensor_tensor(hit, hit, -8.0, io, ALU.mult, ALU.add))
            link(dve.tensor_reduce(number, hit, AX.X, ALU.min))
            link(dve.tensor_scalar(number, number, 8.0, None, ALU.add))
            link(dve.tensor_tensor(hit, io, bc(number), ALU.is_equal))

        L1, L5, L7 = Layer(1), Layer(5), Layer(7)
        view = {}
        for l, lay in ((1, L1), (5, L5), (7, L7)):
            view[l] = dict(coef=lay.work(P, W * 8, w=W), hit=lay.work(P, W * 8, w=W), left=lay.work(P, W * 8, w=W),
                           mx=lay.work(P, W), number=lay.work(P, W), mx2=lay.work(P, W), 
                           coefT=lay.work(8, N, at=places[5]["W1"][0] if l == 5 else None))
        for l, lay in ((1, L1), (7, L7)):
            view[l].update(h1=lay.work(128, 4 * N, u=2, k=2), h2=lay.work(128, 4 * N, u=2, k=2))
        view[5].update(h=L5.work(128, 8 * N, k=8))
        bns = L1.work(128, 32, s=2)
        bnc = L1.work(128, 32, s=2)
        MLP = {1: ("W1", "W2", "Wo"), 7: ("w1", None, "w2")}
        GATE = {1: ("Wr", "br", "bo"), 5: ("Wg", "bg", "bd"), 7: ("router", None, "b2")}
        FFN = (1, 5, 7)
        lays = {1: L1, 5: L5, 7: L7}

        def expert_weight(l, name, e, k):
            a = lays[l].w(name, e=8, k=k)
            return a[:, e, :, :]

        def ffn_tensor(pe, l):
            lay, v = lays[l], view[l]
            wait_blob(pe, l)
            xnt_tensor(pe, l)
            wait_empty(pe, f"xnt{l}")
            wr, br, bo = GATE[l]
            bias = lay.w(br) if br else None
            if l == 5:
                lin(pe, "hid", [(lay.w("W1", k=2), XNT)], 1024)
                wait_empty(pe, "hid")
                nodes(pe, "gate5", v["h"], lay.w("Wg", k=8), 8, bias)
            else:
                nodes(pe, f"gate{l}", XNT, lay.w(wr, k=2), 8, bias)
            for kind, e in experts(EXPERTS[l]):
                stage = f"{kind}_{l}_{e}"
                if kind == "mlp1":
                    lin(pe, stage, [(expert_weight(l, MLP[l][0], e, 2), XNT)], C)
                elif kind == "mlp2":
                    wait_empty(pe, f"mlp1_{l}_{e}")
                    lin(pe, stage, [(expert_weight(l, MLP[l][1], e, 2), v["h1"][:, e % 2])], C)
                else:
                    if l == 1:
                        wait_empty(pe, f"mlp2_{l}_{e}")
                        nodes(pe, stage, v["h2"][:, e % 2], expert_weight(l, "Wo", e, 2), C)
                    elif l == 7:
                        wait_empty(pe, f"mlp1_{l}_{e}")
                        nodes(pe, stage, v["h1"][:, e % 2], expert_weight(l, "w2", e, 2), C)
                    else:
                        nodes(pe, stage, v["h"], expert_weight(l, "Wd", e, 8), C)
            pe.wait_ge(sem("coefficients_ready"), FFN.index(l) + 1)
            for w in range(W):
                turn(pe, f"coefT{l}", w, [((0, P), v["coef"][:, w, :])])
            wait_empty(pe, f"coefT{l}")
            for w in range(W):
                wait_bank(pe, f"bias{l}", w)
                full(pe.matmul(bank(f"bias{l}", w)[0:P, 0:C], v["coefT"][:, P * w:P * w + P], lay.w(bo), start=True, stop=True))

        def ffn_scalar(act, l):
            lay, v = lays[l], view[l]
            if l == 1:
                act.wait_ge(sem("bn_var"), 1)
                act.activation(bns, bns, ACT.Sqrt).then_inc(sem("bn_std"), 1)
            wait_blob(act, l)
            xnt_scalar(act, l)
            if l == 5:
                lin_out(act, "hid", v["h"], 1024, ACT.Gelu, lay.w("b1"))
            act.wait_ge(sem("gate_shifted"), FFN.index(l) + 1)
            act.activation(v["coef"], v["coef"], ACT.Exp).then_inc(sem("gate_exp"), 1)
            if l == 1:
                act.wait_ge(sem("bn_ready"), 1)
            for kind, e in experts(EXPERTS[l]):
                stage = f"{kind}_{l}_{e}"
                if l == 1 and kind in ("mlp1", "mlp2"):
                    s = int(kind == "mlp2")
                    lin_out(act, stage, v["h2" if s else "h1"][:, e % 2], C, ACT.Relu,
                            bnc[:, s, 2 * e:2 * e + 2], bns[:, s, 2 * e:2 * e + 2])
                elif l == 7 and kind == "mlp1":
                    lin_out(act, stage, v["h1"][:, e % 2], C, ACT.Gelu, lay.w("b1")[:, 2 * e:2 * e + 2])
            for w in range(W):
                wait_full(act, f"coefT{l}", w)
                out_by(act.activation(v["coefT"][:, P * w:P * w + P], bank(f"coefT{l}", w)[0:8, 0:P], ACT.Copy), "act")

        def ffn_vector(dve, l):
            link = linker(dve, "vector")
            lay, v = lays[l], view[l]
            if l == 1:
                wait_blob(dve, 1)
                at = places[1]["b1"][0]
                bn = lay.ar[:, at:at + 160].rearrange("p (s q c) -> p s q c", s=2, q=5)
                dve.tensor_scalar(bns, bn[:, :, 4, :], 1e-3, None, ALU.add).then_inc(sem("bn_var"), 1)
            for w in range(W):
                wait_full(dve, f"gate{l}", w)
                out_by(dve.tensor_copy(v["coef"][:, w, :], bank(f"gate{l}", w)[0:P, 0:8]), "dve")
            wait_empty(dve, f"gate{l}")
            soft_max(dve, FFN.index(l) + 1, v["coef"], P, v["mx"], link)
            if l == 5:
                first_max(dve, v["coef"], v["mx"], v["hit"], v["number"], link)
                link(dve.tensor_tensor(v["coef"], v["coef"], v["hit"], ALU.mult))
            if l == 7:
                first_max(dve, v["coef"], v["mx"], v["hit"], v["number"], link)
                link(dve.tensor_scalar(v["left"], v["hit"], -2.0, None, ALU.mult))
                link(dve.tensor_tensor(v["left"], v["left"], v["coef"], ALU.add))
                link(dve.tensor_tensor(v["coef"], v["coef"], v["hit"], ALU.mult))
                first_max(dve, v["left"], v["mx2"], v["hit"], v["number"], link)
                link(dve.tensor_tensor(v["left"], v["left"], v["hit"], ALU.mult))
                link(dve.tensor_tensor(v["coef"], v["coef"], v["left"], ALU.add))
                link(dve.tensor_tensor(v["mx"], v["mx"], v["mx2"], ALU.add))
                link(dve.tensor_scalar(v["mx"], v["mx"], 1e-12, None, ALU.max))
                link(dve.reciprocal(v["mx"], v["mx"]))
                link(dve.tensor_tensor(v["coef"], v["coef"], v["mx"].unsqueeze(2).broadcast_to((P, W, 8)), ALU.mult))
            dve.tensor_copy(v["hit"], v["coef"]).then_inc(sem("coefficients_ready"), 1)
            if l == 1:
                dve.wait_ge(sem("bn_std"), 1)
                link(dve.reciprocal(bns, bns))
                link(dve.tensor_tensor(bns, bns, bn[:, :, 1, :], ALU.mult))
                link(dve.tensor_tensor(bnc, bn[:, :, 0, :], bn[:, :, 3, :], ALU.subtract))
                link(dve.tensor_tensor(bnc, bnc, bns, ALU.mult))
                dve.tensor_tensor(bnc, bnc, bn[:, :, 2, :], ALU.add).then_inc(sem("bn_ready"), 1)
            if l == 7:
                link(dve.tensor_tensor(X[:, :, :], X[:, :, :], XN[:, :, :], ALU.add))
            for kind, e in experts(EXPERTS[l]):
                if kind == "mlpo":
                    for w in range(W):
                        stage = f"mlpo_{l}_{e}"
                        wait_full(dve, stage, w)
                        wait_x(dve, stage, w)
                        out_by(dve.scalar_tensor_tensor(X[:, w, :], bank(stage, w)[0:P, 0:C], v["coef"][:, w, e:e + 1],
                                                        X[:, w, :], ALU.mult, ALU.add), "dve")
            wait_empty(dve, f"mlpo_{l}_7")
            add_to_x(dve, f"bias{l}")
            wait_empty(dve, f"bias{l}")

        def max_views(lay, H, big):
            v = dict(scoreT=big[0], fwd=big[1], bwd=big[2])
            v["dstT"] = lay.work(TH, 256, h=2)
            v["edge"] = lay.work(TH, 258, h=2)
            v["first"] = lay.work(TH, 256, h=2)
            v["last"] = lay.work(TH, 256, h=2)
            v["ends"] = lay.work(8, 2 * T, e=2)
            v["joined"] = lay.work(8, T + 1)
            v["single"] = lay.work(8, T)
            v["rowf"] = lay.work(8, 2 * T, e=2)
            v["step"] = lay.work(8, T)
            v["run"] = lay.work(8, T)
            v["carry"] = lay.work(8, 2 * T, e=2)
            v["carryT"] = lay.work(TH, 4 * H, e=2, h=2)
            return v

        def edge_max_tensor(pe, k, H, v, sc):
            pe.wait_ge(sem("scores_ready"), k + 1)
            for h in range(2):
                turn(pe, f"seg_dst{k}", h, [((0, 128), dst_all[:, TH * h:TH * h + TH])])
            wait_bank(pe, f"seg_ends{k}", 0)
            b = bank(f"seg_ends{k}", 0)
            pe.matmul(b[0:8, 0:T], sel0[:, :], dst_all, start=True, stop=True)
            full(pe.matmul(b[0:8, 256:256 + T], sel127[:, :], dst_all, start=True, stop=True))
            for u in range(2 * H):
                a, h = divmod(u, 2)
                turn(pe, f"scoreT{k}", u, [((0, 128), sc[:, TH * h:TH * h + TH, a])])
            pe.wait_ge(sem("runs_ready"), k + 1)
            for u in range(4):
                e, h = divmod(u, 2)
                src = v["bwd"][:, :, h, 0] if e else v["fwd"][:, :, h, 127]
                turn(pe, f"ends{k}", u, [((0, TH), src)])
            pe.wait_ge(sem("carries_ready"), k + 1)
            for u in range(4):
                e, h = divmod(u, 2)
                turn(pe, f"carry{k}", u, [((0, H), v["carry"][0:H, e, TH * h:TH * h + TH])])
            pe.wait_ge(sem("maxima_ready"), k + 1)
            for u in range(2 * H):
                a, h = divmod(u, 2)
                turn(pe, f"amax{k}", u, [((0, TH), v["scoreT"][:, a, h, :])])

        def edge_max_scalar(act, k, H, v, amax):
            for h in range(2):
                wait_full(act, f"seg_dst{k}", h)
                out_by(act.activation(v["dstT"][:, h, :], bank(f"seg_dst{k}", h)[0:TH, 0:128], ACT.Copy), "act")
            wait_full(act, f"seg_ends{k}", 0)
            out_by(act.activation(v["ends"], bank(f"seg_ends{k}", 0)[0:8, :].rearrange("p (e t) -> p e t", e=2)[:, :, 0:T], ACT.Copy), "act")
            for u in range(2 * H):
                a, h = divmod(u, 2)
                wait_full(act, f"scoreT{k}", u)
                out_by(act.activation(v["scoreT"][:, a, h, :], bank(f"scoreT{k}", u)[0:TH, 0:128], ACT.Copy), "act")
            for u in range(4):
                e, h = divmod(u, 2)
                wait_full(act, f"ends{k}", u)
                out_by(act.activation(v["rowf"][0:H, e, TH * h:TH * h + TH], bank(f"ends{k}", u)[0:H, 0:TH], ACT.Copy), "act")
            for u in range(4):
                e, h = divmod(u, 2)
                wait_full(act, f"carry{k}", u)
                out_by(act.activation(v["carryT"][:, e, h, :], bank(f"carry{k}", u)[0:TH, 0:H], ACT.Copy), "act")
            for u in range(2 * H):
                a, h = divmod(u, 2)
                wait_full(act, f"amax{k}", u)
                out_by(act.activation(amax[:, TH * h:TH * h + TH, a], bank(f"amax{k}", u)[:, 0:TH], ACT.Copy), "act")

        def edge_max_vector(dve, k, H, v):
            link = linker(dve, "vector")
            wait_empty(dve, f"seg_ends{k}")

            def far(out, a, b):
                link(dve.tensor_tensor(out, a, b, ALU.is_equal))
                link(dve.tensor_scalar(out, out, 1.0, BIG, ALU.subtract, ALU.mult))

            dt, edge = v["dstT"], v["edge"]
            link(dve.memset(edge, -BIG))
            far(edge[:, :, 1:128], dt[:, :, 1:128], dt[:, :, 0:127])
            far(v["first"], dt, dt[:, :, 0:1].broadcast_to((TH, 2, 128)))
            far(v["last"], dt, dt[:, :, 127:128].broadcast_to((TH, 2, 128)))
            link(dve.memset(v["joined"], -BIG))
            far(v["joined"][:, 1:T], v["ends"][:, 0, 1:T], v["ends"][:, 1, 0:T - 1])
            far(v["single"], v["ends"][:, 0, :], v["ends"][:, 1, :])
            wait_empty(dve, f"scoreT{k}")
            for a in range(H):
                for h in range(2):
                    s = v["scoreT"][:, a, h, :]
                    dve.tensor_tensor_scan(v["fwd"][:, a, h, :], edge[:, h, 0:128], s, -BIG, ALU.add, ALU.max)
                    ins = dve.tensor_tensor_scan(v["bwd"][:, a, h, ::-1], edge[:, h, 128:0:-1], s[:, ::-1], -BIG, ALU.add, ALU.max)
            ins.then_inc(sem("runs_ready"), 1)
            wait_empty(dve, f"ends{k}")
            jn, step, run = v["joined"], v["step"], v["run"]
            link(dve.tensor_tensor(step, v["single"], jn[:, 0:T], ALU.add))
            link(dve.tensor_tensor_scan(run[0:H], step[0:H], v["rowf"][0:H, 0, :], -BIG, ALU.add, ALU.max))
            link(dve.memset(v["carry"], -BIG))
            dve.tensor_tensor(v["carry"][0:H, 0, 1:T], run[0:H, 0:T - 1], jn[0:H, 1:T], ALU.add)
            link(dve.tensor_tensor(step, v["single"], jn[:, 1:T + 1], ALU.add))
            link(dve.tensor_tensor_scan(run[0:H, ::-1], step[0:H, ::-1], v["rowf"][0:H, 1, ::-1], -BIG, ALU.add, ALU.max))
            dve.tensor_tensor(v["carry"][0:H, 1, 0:T - 1], run[0:H, 1:T], jn[0:H, 1:T], ALU.add).then_inc(sem("carries_ready"), 1)
            link(dve.tensor_tensor(v["scoreT"], v["fwd"], v["bwd"], ALU.max))
            wait_empty(dve, f"carry{k}")
            for e, mask in ((0, v["first"]), (1, v["last"])):
                for a in range(H):
                    for h in range(2):
                        m = v["scoreT"][:, a, h, :]
                        ins = dve.scalar_tensor_tensor(m, mask[:, h, :], v["carryT"][:, e, h, a:a + 1], m, ALU.add, ALU.max)
                if e == 0:
                    link(ins)
            ins.then_inc(sem("maxima_ready"), 1)

        G1 = Layer(2)
        vt = G1.work(128, 256, k=2)
        s16_any = G1.work(P, 8 * 128, at=G1.at + 64)
        s16 = G1.work(P, W * 128)
        hbuf_at = G1.at
        hbuf = G1.work(P, 2 * W * (C + NH), u=2, w=W)
        hx = G1.work(128, U * (C + NH), u=U)
        msg1 = G1.work(128, 3 * (C + 9), u=3)
        acc1 = G1.work(P, W * 265)
        wt9 = G1.work(128, T * 9, t=T)
        rel8 = G1.work(128, T * NR, t=T)
        ohT1 = G1.work(P, 2 * 128, u=2)
        picked = G1.work(128, 2 * NR * NH, u=2)
        ss1 = G1.work(128, T * NH, at=hbuf_at, t=T)
        wt_at, wn_at = places[2]["WT"][0], places[2]["Wn"][0]
        sc1 = G1.work(128, T * 8, at=wt_at, t=T)
        am1 = G1.work(128, T * 8, at=wt_at + T * 8, t=T)
        mv1 = max_views(G1, NH, [G1.work(TH, 2048, at=a, a=NH, h=2) for a in (wn_at, wn_at + 2048, hbuf_at)])

        def l1_sync(sp):
            for r in range(NR):
                wait_empty(sp, f"l1_h{r}")
                sp.dma_start(h_tab[r * N:(r + 1) * N, :].rearrange("(w p) c -> p w c", w=W), hbuf[:, r % 2])\
                    .then_inc(sem(f"h_written{r % 2}"), 16)

            def store(i, b):
                i, t, s = tile_at(i, b)
                wait_gathered(sp, "l1s", i, s)
                sp.dma_start(he_tab[ds(t, 1), :, :].rearrange("a p c -> p (a c)"), hx[:, s, 0:C]).then_inc(sem(f"rows_stored{s}"), 16)
            tiles(sp, store)
            for b in range(U):
                sp.wait_ge(sem(f"rows_stored{b}"), 16 * (T // U))
            sp.wait_ge(sem("l1s_kept"), T)

            def load(i, b):
                i, t, s = tile_at(i, b)
                wait_over(sp, "l1m_messages", t - U + 1)
                sp.dma_start(hx[:, s, 0:C], he_tab[ds(t, 1), :, :].rearrange("a p c -> p (a c)")).then_inc(sem(f"rows_loaded{s}"), 16)
            tiles(sp, load)

        def l1_pool(pool):
            pool.wait_ge(sem("indices_ready"), 1)
            for k in range(2):
                pool.wait_ge(sem(f"h_written{k}"), 16 * NR // 2)
            gathers(pool, "l1s", idx_hs, h_tab, hx, "l1s_kept", "rows_stored")

        def l1_tensor(pe):
            wait_blob(pe, 2)
            wn, wtv, at = G1.w("Wn", r=NR, k=2), G1.w("WT", r=NR, k=2), G1.w("attn", k=2)
            for r in range(NR):
                wait_bank(pe, "l1_v", r)
                for f in range(2):
                    for k in range(2):
                        ins = pe.matmul(bank("l1_v", r)[:, 16 * f:16 * f + 16], wn[:, r, k, 128 * f:128 * f + 128],
                                        at[:, k, :], start=k == 0, stop=k == 1)
                full(ins)
            wait_empty(pe, "l1_v")
            xnt_tensor(pe, 2)
            wait_empty(pe, "xnt2")
            nodes(pe, "l1_s", XNT, vt, 128)
            for r in range(NR):
                nodes(pe, f"l1_h{r}", XNT, wtv[:, r], C)
            wait_empty(pe, f"l1_h{NR - 1}")

            def scores(i, b):
                w = window_of(pe, i, b, 1)
                if tile := tile_at(i, b):
                    _, t, s = tile
                    pe.wait_ge(sem("l1s_onehots"), t + 1)
                    wait_over(pe, "l1s_copied", t - 1)
                    pe.transpose(PS[s % 2][0:P, 0:128], oh[:, s % 3, :], ident[:, :]).then_inc(sem("l1s_turned"), 1)
                if tile := tile_at(i, b, 1):
                    i1, t, s = tile
                    pe.wait_ge(sem("l1s_copied"), t + 1)
                    wait_over(pe, "l1s_picked", t - 1)
                    pe.matmul(PS[2 + s % 2][:, 0:NR * NH], ohT1[:, s % 2, :], s16_any[:, ds(pe.scalar_reg_alu(ALU.logical_shift_right, w, 2), NR * NH)],
                              start=True, stop=True).then_inc(sem("l1s_product"), 1)
            tiles(pe, scores, 3)
            edge_max_tensor(pe, 0, NH, mv1, sc1)
            wait_empty(pe, "amax0")
            open_sums(pe, 265)
            pe.wait_ge(sem("weights1_ready"), 1)

            def body(i, b):
                w = window_of(pe, i, b, 1)
                if tile := tile_at(i, b, 1):
                    _, t, s = tile
                    pe.wait_ge(sem("l1m_messages"), t + 1)
                    pe.wait_ge(sem("l1m_weights"), t + 1)
                    add_up(pe, "l1m", w, oh[:, s % 3, :], msg1[:, s % 3, :], C + 9)
            tiles(pe, body, 1)
            close_sums(pe, "l1m", 265)

        def l1_scalar(act):
            for r in range(NR):
                wait_full(act, "l1_v", r)
                for e in range(2):
                    ins = act.activation(vt[:, :, 64 * e + 8 * r:64 * e + 8 * r + 8],
                                         bank("l1_v", r)[:, 0:32].rearrange("p (f s) -> p f s", f=2)[:, :, 8 * e:8 * e + 8], ACT.Copy)
                out_by(ins, "act")
            xnt_scalar(act, 2)
            for w in range(W):
                wait_full(act, "l1_s", w)
                out_by(act.activation(s16[:, 128 * w:128 * w + 128], bank("l1_s", w)[0:P, 0:128], ACT.Copy), "act")
            for r in range(NR):
                if r >= 2:
                    act.wait_ge(sem(f"h_written{r % 2}"), 16 * (r // 2))
                wait_empty(act, "l1_s")
                act.activation(hbuf[:, r % 2, :, C:C + NH], s16.rearrange("p (w s) -> p w s", w=W)[:, :, 8 * r:8 * r + 8], ACT.Copy)
                for w in range(W):
                    wait_full(act, f"l1_h{r}", w)
                    out_by(act.activation(hbuf[:, r % 2, w, 0:C], bank(f"l1_h{r}", w)[0:P, 0:C], ACT.Copy), "act")

            def scores(i, b):
                i0, t, s = tile_at(i, b)
                act.wait_ge(sem("l1s_turned"), t + 1)
                wait_over(act, "l1s_product", t - 1)
                act.activation(ohT1[:, s % 2, :], PS[s % 2][0:P, 0:128], ACT.Copy).then_inc(sem("l1s_copied"), 1)
                wait_gathered(act, "l1s", i0, s)
                act.activation(ss1[:, ds(t, 1), :].rearrange("p a h -> p (a h)"), hx[:, s, C:C + NH], ACT.Copy)\
                    .then_inc(sem("l1s_kept"), 1)
            tiles(act, scores)
            edge_max_scalar(act, 0, NH, mv1, am1)
            act.wait_ge(sem("scores_shifted"), 1)
            act.activation(wt9[:, :, 0:8], sc1, ACT.Exp).then_inc(sem("weights1_ready"), 1)
            act.wait_ge(sem("weights1_ready"), 1)

            def append(i, b):
                _, t, s = tile_at(i, b)
                wait_over(act, "l1m_product", t - 2)
                act.activation(msg1[:, s % 3, C:C + 9], wt9[:, ds(t, 1), :].rearrange("p a h -> p (a h)"), ACT.Copy)\
                    .then_inc(sem("l1m_weights"), 1)
            tiles(act, append)
            take_sums(act, "l1m", acc1, 265)

        def l1_vector(dve):
            link = linker(dve, "vector")
            wait_empty(dve, "l1_h7")
            for k in range(2):
                dve.wait_ge(sem(f"h_written{k}"), 16 * NR // 2)

            dve.tensor_tensor(rel8, srt[:, :, TYPE8 - 1].unsqueeze(2).broadcast_to((128, T, NR)),
                              iota[:, 0:NR].unsqueeze(1).broadcast_to((128, T, NR)), ALU.is_equal).then_inc(sem("l1s_masks"), 1)

            def score(i, b):
                if tile := tile_at(i, b):
                    _, t, s = tile
                    wait_over(dve, "l1s_turned", t - 2)
                    onehot_of(dve, t, s % 3).then_inc(sem("l1s_onehots"), 1)
                if tile := tile_at(i, b, 2):
                    _, t, s = tile
                    dve.wait_ge(sem("l1s_product"), t + 1)
                    wait_over(dve, "l1s_reduced", t - 1)
                    dve.tensor_tensor(picked[:, s % 2, :].rearrange("p (r h) -> p r h", r=NR),
                                      PS[2 + s % 2][:, 0:NR * NH].rearrange("p (r h) -> p r h", r=NR),
                                      rel8[:, ds(t, 1), :].rearrange("p a r -> p (a r)").unsqueeze(2).broadcast_to((128, NR, NH)),
                                      ALU.mult).then_inc(sem("l1s_picked"), 1)
                if tile := tile_at(i, b, 3):
                    _, t, s = tile
                    dve.wait_ge(sem("l1s_picked"), t + 1)
                    dve.tensor_reduce(sc1[:, ds(t, 1), :].rearrange("p a h -> p (a h)"),
                                      picked[:, s % 2, :].rearrange("p (r h) -> p h r", r=NR), AX.X, ALU.add)\
                        .then_inc(sem("l1s_reduced"), 1)
            dve.wait_ge(sem("l1s_masks"), 1)
            tiles(dve, score, 3)
            dve.wait_ge(sem("l1s_reduced"), T)
            dve.wait_ge(sem("l1s_kept"), T)
            link(dve.tensor_tensor(sc1, sc1, ss1, ALU.add))
            dve.scalar_tensor_tensor(sc1, sc1, 0.2, sc1, ALU.mult, ALU.max).then_inc(sem("scores_ready"), 1)
            edge_max_vector(dve, 0, NH, mv1)
            wait_empty(dve, "amax0")
            link(dve.tensor_scalar(am1, am1, 0.0, None, ALU.max))
            dve.tensor_copy(wt9[:, :, 8], typ[:, :, 1])
            dve.tensor_tensor(sc1, sc1, am1, ALU.subtract).then_inc(sem("scores_shifted"), 1)
            dve.wait_ge(sem("weights1_ready"), 1)

            def body(i, b):
                if tile := tile_at(i, b):
                    i0, t, s = tile
                    wait_over(dve, "l1m_product", t - 2)
                    onehot_of(dve, t, s % 3)
                    dve.wait_ge(sem(f"rows_loaded{s}"), (i0 + 1) * 16)
                    w8 = wt9[:, ds(t, 1), 0:8].rearrange("p a h -> p (a h)")
                    dve.tensor_tensor(msg1[:, s % 3, 0:C].rearrange("p (h d) -> p h d", h=NH),
                                      hx[:, s, 0:C].rearrange("p (h d) -> p h d", h=NH),
                                      w8.unsqueeze(2).broadcast_to((128, NH, HD)), ALU.mult).then_inc(sem("l1m_messages"), 1)
            tiles(dve, body)
            dve.wait_ge(sem("l1m_taken"), W)
            a = acc1.rearrange("p (w c) -> p w c", w=W)
            den = a[:, :, C:C + 8]
            dve.tensor_scalar(recv1[:, :], a[:, :, C + 8], 0.0, None, ALU.is_gt)
            link(dve.tensor_scalar(den, den, 1e-12, None, ALU.add))
            link(dve.reciprocal(den, den))
            for w in range(W):
                o = a[:, w, 0:C].rearrange("p (h d) -> p h d", h=NH)
                link(dve.tensor_tensor(o, o, den[:, w, :].unsqueeze(2).broadcast_to((P, NH, HD)), ALU.mult))
                link(dve.tensor_tensor(X[:, w, :], X[:, w, :], a[:, w, 0:C], ALU.add))

        A3 = Layer(3)
        xmT = A3.work(128, 4 * N, k=4)
        fx = A3.work(P, W * 4 * 129, w=W, q=4)
        sw = A3.work(P, W * 512, w=W)
        swT = A3.work(128, 4 * N, k=4)
        oxT = A3.work(128, 4 * N, k=4)
        tok, tokT, qT, kT, vv, pr, prT, osl = (A3.work(128, 512, q=4) for _ in range(8))
        invt = A3.work(P, 8)
        smx = A3.work(P, 8)
        rn = A3.work(128, 8)
        DIAG = ((slice(0, 64), slice(0, 64)), (slice(64, 128), slice(64, 128)))

        def l1f_tensor(pe):
            wait_blob(pe, 3)
            xnt_tensor(pe, 3)
            wait_empty(pe, "xnt3")
            lin(pe, "xmT", [(A3.w("W_x", k=2), XNT)], 512)
            nodes(pe, "fx", XNT, A3.w("W_fx", k=2), 512, A3.w("b_fx"))
            wait_empty(pe, "xmT")
            for w in range(W):
                wait_bank(pe, "slice", w)
                pe.matmul(bank("slice", w)[0:P, :], ones[0:1, 0:P], A3.w("b_slice"), start=True, stop=False)
                for q in range(4):
                    ins = pe.matmul(bank("slice", w)[0:P, 128 * q:128 * q + 128], xmT[:, q, P * w:P * w + P], A3.w("W_slice"),
                                    start=False, stop=q == 3)
                full(ins)
            for w in range(W):
                pe.wait_ge(sem("slices_ready"), w + 1)
                turn(pe, "swT", w, [((P * k, P), sw[:, w, 128 * k:128 * k + 128]) for k in range(4)])
            wait_empty(pe, "fx")
            for q in range(4):
                wait_bank(pe, "token", q)
                for w in range(W):
                    ins = pe.matmul(bank("token", q)[:, 0:129], sw[:, w, 128 * q:128 * q + 128], fx[:, w, q, :],
                                    start=w == 0, stop=w == W - 1)
                full(ins)
            wait_empty(pe, "token")
            for q in range(4):
                turn(pe, "t_tokT", q, [((0, 128), tok[:, q, :])])

            def squares(stage, left, right):
                for q in range(4):
                    wait_bank(pe, stage, q)
                    full(pe.matmul(bank(stage, q)[:, 0:128], left(q), right(q), start=True, stop=True))
            wait_empty(pe, "t_tokT")
            squares("t_qT", lambda q: A3.w("W_q"), lambda q: tokT[:, q, :])
            squares("t_kT", lambda q: A3.w("W_k"), lambda q: tokT[:, q, :])
            squares("t_v", lambda q: tokT[:, q, :], lambda q: A3.w("W_v"))
            wait_empty(pe, "t_kT")
            squares("t_lg", lambda q: qT[:, q, :], lambda q: kT[:, q, :])
            pe.wait_ge(sem("slice_attention_ready"), 1)
            for q in range(4):
                turn(pe, "t_pT", q, [((0, 128), pr[:, q, :])])
            wait_empty(pe, "t_pT")
            squares("t_os", lambda q: prT[:, q, :], lambda q: vv[:, q, :])
            wait_empty(pe, "t_os")
            for q in range(4):
                for h, (c, n) in enumerate(HALVES):
                    wait_bank(pe, "oxT", 2 * q + h)
                    full(pe.matmul(bank("oxT", 2 * q + h)[:, 0:n], osl[:, q, :], swT[:, q, c:c + n], start=True, stop=True))
            wait_empty(pe, "oxT")
            nodes(pe, "l3_out", oxT, A3.w("W_out", k=4), C, A3.w("b_out"))

        def l1f_scalar(act):
            wait_blob(act, 3)
            xnt_scalar(act, 3)
            lin_out(act, "xmT", xmT, 512, ACT.Identity, A3.w("b_x"))
            for w in range(W):
                wait_full(act, "fx", w)
                out_by(act.activation(fx[:, w, :, 0:128], bank("fx", w)[0:P, :].rearrange("p (q c) -> p q c", q=4), ACT.Copy), "act")
            for w in range(W):
                act.wait_ge(sem("slice_shifted"), w + 1)
                act.activation(sw[:, w, :], sw[:, w, :], ACT.Exp).then_inc(sem("slice_exp"), 1)
            turned_nodes(act, "swT", swT, 4)

            def squares_out(stage, out, scale=1.0):
                for q in range(4):
                    wait_full(act, stage, q)
                    out_by(act.activation(out[:, q, :], bank(stage, q)[:, 0:128], ACT.Copy, scale=scale), "act")
            squares_out("t_tokT", tokT)
            squares_out("t_qT", qT, 64 ** -0.5)
            squares_out("t_kT", kT)
            squares_out("t_v", vv)
            wait_empty(act, "t_lg")
            for rows, cols in DIAG:
                ins = act.activation(pr[rows, :, cols], pr[rows, :, cols], ACT.Exp)
            ins.then_inc(sem("slice_attention_exp"), 1)
            squares_out("t_pT", prT)
            squares_out("t_os", osl)
            lin_out(act, "oxT", oxT, 512, ACT.Copy)

        def l1f_vector(dve):
            link = linker(dve, "vector")
            wait_blob(dve, 3)
            dve.memset(fx[:, :, :, 128:129], 1.0)
            dve.memset(tok, 0.0)
            link(dve.memset(pr, 0.0))
            link(dve.tensor_scalar(invt, A3.w("temp")[0:P, :], 0.1, 5.0, ALU.max, ALU.min))
            link(dve.reciprocal(invt, invt))
            bc = lambda a: a.unsqueeze(2).broadcast_to((P, 8, 64))
            for w in range(W):
                s = sw[:, w, :].rearrange("p (h g) -> p h g", h=8)
                wait_full(dve, "slice", w)
                out_by(dve.tensor_tensor(s, bank("slice", w)[0:P, :].rearrange("p (h g) -> p h g", h=8), bc(invt), ALU.mult), "dve")
                wait_empty(dve, "slice", w)
                link(dve.tensor_reduce(smx, s, AX.X, ALU.max))
                dve.tensor_tensor(s, s, bc(smx), ALU.subtract).then_inc(sem("slice_shifted"), 1)
            dve.wait_ge(sem("slice_shifted"), W)
            for w in range(W):
                s = sw[:, w, :].rearrange("p (h g) -> p h g", h=8)
                dve.wait_ge(sem("slice_exp"), w + 1)
                wait_over(dve, "slices_ready", w)
                link(dve.tensor_reduce(smx, s, AX.X, ALU.add))
                link(dve.reciprocal(smx, smx))
                dve.tensor_tensor(s, s, bc(smx), ALU.mult).then_inc(sem("slices_ready"), 1)
            for q in range(4):
                b = bank("token", q)
                wait_full(dve, "token", q)
                link(dve.tensor_scalar(rn[:, q:q + 1], b[:, 128:129], 1e-5, None, ALU.add))
                link(dve.reciprocal(rn[:, q:q + 1], rn[:, q:q + 1]))
                for rows, cols in DIAG:
                    ins = dve.tensor_scalar(tok[rows, q, cols], b[rows, cols], rn[rows, q:q + 1], None, ALU.mult)
                out_by(ins, "dve")
            for q in range(4):
                wait_full(dve, "t_lg", q)
                b = bank("t_lg", q)
                for rows, cols in DIAG:
                    ins = dve.tensor_reduce(rn[rows, q:q + 1], b[rows, cols], AX.X, ALU.max)
                link(ins)
                for rows, cols in DIAG:
                    ins = dve.tensor_scalar(pr[rows, q, cols], b[rows, cols], rn[rows, q:q + 1], None, ALU.subtract)
                out_by(ins, "dve")
            dve.wait_ge(sem("slice_attention_exp"), 1)
            for rows, cols in DIAG:
                ins = dve.tensor_reduce(rn[rows, 0:4], pr[rows, :, cols], AX.X, ALU.add)
            link(ins)
            link(dve.reciprocal(rn[:, 0:4], rn[:, 0:4]))
            for rows, cols in DIAG:
                ins = dve.tensor_tensor(pr[rows, :, cols], pr[rows, :, cols],
                                        rn[rows, 0:4].unsqueeze(2).broadcast_to((64, 4, 64)), ALU.mult)
            ins.then_inc(sem("slice_attention_ready"), 1)
            add_to_x(dve, "l3_out")
            wait_empty(dve, "l3_out")

        G2 = Layer(4)
        over_at = G2.at
        xg2 = G2.work(128, U * (C + 1), u=U)
        msg2 = G2.work(128, 3 * 512, u=3)
        h0T = G2.work(128, 4 * N, at=over_at, k=4)
        acc2 = G2.work(P, W * 512)
        turns = G2.work(128, U * 128, at=G2.at, u=U)
        whole = G2.work(128, 2 * 128, at=G2.at + U * 128, u=2)
        h1T = G2.work(128, 4 * N, k=4)
        agg = G2.work(P, W * C, w=W)
        aggT = G2.work(128, 2 * N, k=2)
        nmask = G2.work(P, 4 * W, t=4)

        def l2_sync(sp):
            def store(i, b):
                i, t, s = tile_at(i, b)
                sp.wait_ge(sem("l2_fractions"), t + 1)
                sp.dma_start(turn_tab[ds(t, 1), :, :].rearrange("a p c -> p (a c)"), turns[:, s, :]).then_inc(sem(f"turns_stored{s}"), 16)
            tiles(sp, store)
            for b in range(U):
                sp.wait_ge(sem(f"turns_stored{b}"), 16 * (T // U))

        def l2_pool(pool):
            pool.wait_ge(sem("xn_written"), 48)
            gathers(pool, "l2", idx_src, xn_tab, xg2, "l2_messages")

        def l2_tensor(pe):
            wait_blob(pe, 4)
            xnt_tensor(pe, 4)
            wait_empty(pe, "xnt4")
            open_sums(pe, 512)

            def body(i, b):
                w = window_of(pe, i, b, 1)
                if tile := tile_at(i, b, 1):
                    _, t, s = tile
                    pe.wait_ge(sem("l2_messages"), t + 1)
                    pe.wait_ge(sem("l2_onehots"), t + 1)
                    add_up(pe, "l2", w, oh[:, s % 3, :], msg2[:, s % 3, :], 512)
            tiles(pe, body, 1)
            close_sums(pe, "l2", 512)
            pe.wait_ge(sem("agg_ready"), 1)
            turn_nodes(pe, "aggT", agg, 2)
            wait_empty(pe, "aggT")
            w0, w1, w2 = G2.w("W0", t=2, k=4), G2.w("W1", t=2, k=4), G2.w("W2", t=2, k=4)
            for t in range(2):
                lin(pe, f"g0_{t}", [(w0[:, t, 0:2], aggT), (w0[:, t, 2:4], XNT)], 512)
                wait_empty(pe, f"g0_{t}")
                lin(pe, f"g1_{t}", [(w1[:, t], h0T)], 512)
                wait_empty(pe, f"g1_{t}")
                nodes(pe, f"g2_{t}", h1T, w2[:, t], C, G2.w("b2")[:, t * C:(t + 1) * C])

        def l2_scalar(act):
            wait_blob(act, 4)
            xnt_scalar(act, 4)

            def body(i, b):
                i0, t, s = tile_at(i, b)
                wait_gathered(act, "l2", i0, s)
                wait_over(act, "l2_product", t - 2)
                for k in range(2):
                    ins = act.activation(msg2[:, s % 3, k * C:(k + 1) * C], xg2[:, s, 0:C], ACT.Copy,
                                         scale=typ[:, ds(t, 1), k])
                ins.then_inc(sem("l2_messages"), 1)
            tiles(act, body)
            take_sums(act, "l2", acc2, 512)
            turned_nodes(act, "aggT", aggT, 2)
            b0, b1 = G2.w("b0"), G2.w("b1")
            for t in range(2):
                lin_out(act, f"g0_{t}", h0T, 512, ACT.Relu, b0[:, 4 * t:4 * t + 4])
                lin_out(act, f"g1_{t}", h1T, 512, ACT.Relu, b1[:, 4 * t:4 * t + 4])

        def l2_vector(dve):
            link = linker(dve, "vector")
            def body(i, b):
                new, old = tile_at(i, b), tile_at(i, b, 1)
                if new:
                    i0, t, s = new
                    wait_over(dve, f"turns_stored{s}", i0 * 16)
                    dve.scalar_tensor_tensor(turns[:, s, :], time_w[:, 0:128], since[:, ds(t, 1)], time_w[:, 128:256],
                                             ALU.mult, ALU.add).then_inc(sem("l2_turns"), 1)
                if old:
                    _, t1, s1 = old
                    dve.wait_ge(sem("l2_rounded"), t1 + 1)
                    dve.tensor_tensor(turns[:, s1, :], turns[:, s1, :], whole[:, s1 % 2, :], ALU.subtract).then_inc(sem("l2_fractions"), 1)
                if new:
                    wait_over(dve, "l2_product", t - 2)
                    onehot_of(dve, t, s % 3).then_inc(sem("l2_onehots"), 1)
                    dve.wait_ge(sem("l2_turns"), t + 1)
                    wait_over(dve, "l2_fractions", t - 1)
                    dve.tensor_scalar(whole[:, s % 2, :], turns[:, s, :], ROUND, ROUND, ALU.add, ALU.subtract).then_inc(sem("l2_rounded"), 1)
            tiles(dve, body, 1)
            for b in range(U):
                dve.wait_ge(sem(f"turns_stored{b}"), 16 * (T // U))
            dve.wait_ge(sem("l2_taken"), W)
            a = acc2.rearrange("p (w c) -> p w c", w=W)
            link(dve.tensor_scalar(nmask[:, 2, :], recv1[:, :], -1.0, 1.0, ALU.mult, ALU.add))
            for w in range(W):
                ins = dve.tensor_scalar(agg[:, w, :], a[:, w, 0:C], nmask[:, 2, w:w + 1], None, ALU.mult)
            link(ins)
            for w in range(W):
                ins = dve.scalar_tensor_tensor(agg[:, w, :], a[:, w, C:2 * C], recv1[:, w:w + 1], agg[:, w, :], ALU.mult, ALU.add)
            ins.then_inc(sem("agg_ready"), 1)
            for t in range(2):
                ins = dve.tensor_scalar(nmask[:, t, :], ntype[:, :], float(t), None, ALU.is_equal)
            link(ins)
            link(dve.tensor_tensor(nmask[:, 3, :], nmask[:, 0, :], nmask[:, 1, :], ALU.add))
            link(dve.tensor_scalar(nmask[:, 3, :], nmask[:, 3, :], -1.0, 1.0, ALU.mult, ALU.add))
            for w in range(W):
                ins = dve.scalar_tensor_tensor(X[:, w, :], XN[:, w, :], nmask[:, 3, w:w + 1], X[:, w, :], ALU.mult, ALU.add)
            link(ins)
            for t in range(2):
                for w in range(W):
                    wait_full(dve, f"g2_{t}", w)
                    wait_x(dve, f"g2_{t}", w)
                    out_by(dve.scalar_tensor_tensor(X[:, w, :], bank(f"g2_{t}", w)[0:P, 0:C], nmask[:, t, w:w + 1], X[:, w, :],
                                                    ALU.mult, ALU.add), "dve")
            wait_empty(dve, "g2_1")

        G3 = Layer(6)
        qn_any = G3.work(P, 8 * C, at=G3.at)
        qn = G3.work(P, W * C)
        kvb_at = G3.at
        kvb = G3.work(P, W * 512, w=W)
        kvg = G3.work(128, U * KVW, u=U)
        ea = G3.work(128, U * 256, u=U)
        enc = G3.work(128, 256, u=2)
        eT = G3.work(128, 512, u=2, k=2)
        ohT = G3.work(P, 256, u=2)
        kj = G3.work(128, 512, u=2)
        prod = G3.work(128, 256)
        ve = G3.work(128, U * C, u=U)
        sc3 = G3.work(128, T * 2, t=T)
        am3 = G3.work(128, T * 2, t=T)
        acc3 = G3.work(P, W * 258)
        msg3 = G3.work(128, 3 * (C + 2), u=3)
        mv3 = max_views(G3, 2, [G3.work(TH, 512, at=kvb_at + 512 * j, a=2, h=2) for j in range(3)])

        def l3_sync(sp):
            wait_empty(sp, "l3_v")
            sp.dma_start(kv_tab.rearrange("(w p) c -> p w c", w=W), kvb).then_inc(sem("kv_written"), 16)

            def body(i, b):
                if tile := tile_at(i, b):
                    _, t, s = tile
                    wait_over(sp, "l3_turned", t - U + 1)
                    sp.dma_start(ea[:, s, 0:128], turn_tab[ds(t, 1), :, :].rearrange("a p c -> p (a c)"))\
                        .then_inc(sem(f"features_back{s}"), 16)
                    sp.dma_start(ea[:, s, 128:256], edge_tab.rearrange("(t p) r -> t p r", p=EP)[ds(t, 1), :, ROW - 128:]
                                 .rearrange("a p r -> p (a r)")).then_inc(sem(f"features_back{s}"), 16)
                if tile := tile_at(i, b, 5):
                    _, t, s = tile
                    sp.wait_ge(sem("l3_values"), t + 1)
                    sp.dma_start(ve_tab[ds(t, 1), :, :].rearrange("a p c -> p (a c)"), ve[:, s, :])\
                        .then_inc(sem(f"values_stored{s}"), 16)
            tiles(sp, body, 5)
            for b in range(U):
                sp.wait_ge(sem(f"values_stored{b}"), 16 * (T // U))

            def load(i, b):
                i, t, s = tile_at(i, b)
                wait_over(sp, "l3m_messages", t - U + 1)
                wait_over(sp, "l3m_onehots", t - U + 1)
                sp.dma_start(ve[:, s, :], ve_tab[ds(t, 1), :, :].rearrange("a p c -> p (a c)")).then_inc(sem(f"values_loaded{s}"), 16)
            tiles(sp, load)

        def l3_pool(pool):
            pool.wait_ge(sem("kv_written"), 16)
            gathers(pool, "l3", idx_src, kv_tab, kvg, "l3_scored")

        def l3_tensor(pe):
            wait_blob(pe, 6)
            xnt_tensor(pe, 6)
            wait_empty(pe, "xnt6")
            for s in ("q", "k", "v", "skip"):
                nodes(pe, "l3_" + s, XNT, G3.w("W" + s, k=2), C, G3.w("b" + s))
            wait_empty(pe, "l3_v")
            wait_empty(pe, "l3_skip")
            we = G3.w("We", k=2)

            def body(i, b):
                w = window_of(pe, i, b, 2)
                if tile := tile_at(i, b, 1):
                    i1, t, s = tile
                    bk = PS[s % 2]
                    pe.wait_ge(sem("l3_encoded"), t + 1)
                    pe.wait_ge(sem("l3_onehots"), t + 1)
                    pe.wait_ge(sem(f"features_back{s}"), (i1 + 1) * 32)
                    wait_over(pe, "l3_copied", t - 1)
                    pe.transpose(bk[:, 0:128], enc[:, s % 2, :], ident[:, :])
                    pe.transpose(bk[:, 128:256], ea[:, s, 128:256], ident[:, :])
                    pe.transpose(bk[0:P, 256:384], oh[:, s % 3, :], ident[:, :]).then_inc(sem("l3_turned"), 1)
                if tile := tile_at(i, b, 2):
                    _, t, s = tile
                    pe.wait_ge(sem("l3_copied"), t + 1)
                    wait_over(pe, "l3_scored", t - 1)
                    for k in range(2):
                        pe.matmul(PS[2 + s % 2][:, 0:C], eT[:, s % 2, k, :], we[:, k, :], start=k == 0, stop=k == 1)
                    pe.matmul(PS[4 + s % 2][:, 0:C], ohT[:, s % 2, :], qn_any[:, ds(pe.scalar_reg_alu(ALU.logical_shift_right, w, 1), C)], start=True, stop=True)\
                        .then_inc(sem("l3_vectors"), 1)
            tiles(pe, body, 3)
            edge_max_tensor(pe, 1, 2, mv3, sc3)
            wait_empty(pe, "amax1")
            open_sums(pe, 258)
            pe.wait_ge(sem("weights3_ready"), 1)

            def sums(i, b):
                w = window_of(pe, i, b, 1)
                if tile := tile_at(i, b, 1):
                    _, t, s = tile
                    pe.wait_ge(sem("l3m_messages"), t + 1)
                    pe.wait_ge(sem("l3m_onehots"), t + 1)
                    add_up(pe, "l3m", w, oh[:, s % 3, :], msg3[:, s % 3, :], C + 2)
            tiles(pe, sums, 1)
            close_sums(pe, "l3m", 258)

        def l3_scalar(act):
            xnt_scalar(act, 6)
            for w in range(W):
                wait_full(act, "l3_q", w)
                out_by(act.activation(qn[:, w * C:(w + 1) * C], bank("l3_q", w)[0:P, 0:C], ACT.Copy), "act")
            for k, s in enumerate("kv"):
                for w in range(W):
                    wait_full(act, "l3_" + s, w)
                    out_by(act.activation(kvb[:, w, k * C:(k + 1) * C], bank("l3_" + s, w)[0:P, 0:C], ACT.Copy), "act")

            def body(i, b):
                if tile := tile_at(i, b):
                    i0, t, s = tile
                    act.wait_ge(sem(f"features_back{s}"), (i0 + 1) * 32)
                    wait_over(act, "l3_turned", t - 1)
                    act.activation(enc[:, s % 2, :], ea[:, s, 0:128], ACT.Sin, scale=6.2831850).then_inc(sem("l3_encoded"), 1)
                if tile := tile_at(i, b, 1):
                    _, t, s = tile
                    act.wait_ge(sem("l3_turned"), t + 1)
                    wait_over(act, "l3_vectors", t - 1)
                    act.activation(eT[:, s % 2, :, :], PS[s % 2][:, 0:256].rearrange("p (k e) -> p k e", k=2), ACT.Copy)
                    act.activation(ohT[:, s % 2, :], PS[s % 2][0:P, 256:384], ACT.Copy).then_inc(sem("l3_copied"), 1)
            tiles(act, body, 3)
            edge_max_scalar(act, 1, 2, mv3, am3)
            act.wait_ge(sem("scores_shifted"), 2)
            act.activation(sc3, sc3, ACT.Exp).then_inc(sem("weights3_ready"), 1)
            act.wait_ge(sem("weights3_ready"), 1)

            def weigh(i, b):
                i0, t, s = tile_at(i, b)
                act.wait_ge(sem(f"values_loaded{s}"), (i0 + 1) * 16)
                wait_over(act, "l3m_product", t - 2)
                act.activation(msg3[:, s % 3, 0:128], ve[:, s, 0:128], ACT.Copy, scale=sc3[:, ds(t, 1), 0])\
                    .then_inc(sem("l3m_messages"), 1)
            tiles(act, weigh)
            take_sums(act, "l3m", acc3, 258)

        def l3_vector(dve):
            link = linker(dve, "vector")
            add_to_x(dve, "l3_skip")

            def body(i, b):
                new, old = tile_at(i, b), tile_at(i, b, 3)
                if old:
                    i3, t3, s3 = old
                    wait_gathered(dve, "l3", i3, s3)
                    dve.wait_ge(sem("l3_vectors"), t3 + 1)
                    e = PS[2 + s3 % 2][:, 0:C]
                    dve.tensor_tensor(kj[:, s3 % 2, :], e, kvg[:, s3, 0:C], ALU.add).then_inc(sem("l3_keys"), 1)
                    wait_over(dve, f"values_stored{s3}", i3 * 16)
                    dve.tensor_tensor(ve[:, s3, :], e, kvg[:, s3, C:2 * C], ALU.add).then_inc(sem("l3_values"), 1)
                if new:
                    _, t, s = new
                    wait_over(dve, "l3_turned", t - 2)
                    onehot_of(dve, t, s % 3).then_inc(sem("l3_onehots"), 1)
                if old:
                    dve.wait_ge(sem("l3_keys"), t3 + 1)
                    wait_over(dve, "l3_scored", t3)
                    for k in range(2):
                        c = slice(128 * k, 128 * k + 128)
                        ins = dve.scalar_tensor_tensor(prod[:, c], PS[4 + s3 % 2][:, c], 1.0, kj[:, s3 % 2, c], ALU.mult, ALU.mult,
                                                       accum_out=sc3[:, ds(t3, 1), k])
                    ins.then_inc(sem("l3_scored"), 1)
            tiles(dve, body, 3)
            dve.wait_ge(sem("l3_scored"), T)
            dve.tensor_scalar(sc3, sc3, 128.0 ** -0.5, None, ALU.mult).then_inc(sem("scores_ready"), 1)
            edge_max_vector(dve, 1, 2, mv3)
            wait_empty(dve, "amax1")
            dve.wait_ge(sem("scores_ready"), 2)
            dve.tensor_tensor(sc3, sc3, am3, ALU.subtract).then_inc(sem("scores_shifted"), 1)

            dve.wait_ge(sem("weights3_ready"), 1)

            def sums(i, b):
                if tile := tile_at(i, b):
                    i0, t, s = tile
                    wait_over(dve, "l3m_product", t - 2)
                    dve.tensor_copy(msg3[:, s % 3, C:C + 2], sc3[:, ds(t, 1), :].rearrange("p a h -> p (a h)"))
                    onehot_of(dve, t, s % 3)
                    dve.wait_ge(sem(f"values_loaded{s}"), (i0 + 1) * 16)
                    dve.tensor_scalar(msg3[:, s % 3, 128:256], ve[:, s, 128:256], sc3[:, ds(t, 1), 1], None, ALU.mult)\
                        .then_inc(sem("l3m_onehots"), 1)
            tiles(dve, sums)
            dve.wait_ge(sem("l3m_taken"), W)
            wait_empty(dve, "l3_skip")
            a = acc3.rearrange("p (w c) -> p w c", w=W)
            den = a[:, :, C:C + 2]
            link(dve.tensor_scalar(den, den, 1e-16, None, ALU.add))
            link(dve.reciprocal(den, den))
            for w in range(W):
                for k in range(2):
                    ins = dve.scalar_tensor_tensor(X[:, w, 128 * k:128 * k + 128], a[:, w, 128 * k:128 * k + 128], den[:, w, k:k + 1],
                                                   X[:, w, 128 * k:128 * k + 128], ALU.mult, ALU.add)
            link(ins)

        block = ctx.enter_context(nc.Block())

        @block.sync
        def _(sp):
            sort_sync(sp)
            l0_sync(sp)
            load_blob(sp, 1)
            for l in range(2, LAYERS + LAYERS % 2):
                sp.wait_ge(sem("xn_ready"), l)
                if l == 5:
                    sp.dma_start(xn_tab[:, 0:C].rearrange("(w p) c -> p w c", p=P), XN[:, :, :]).then_inc(sem("xn_written"), 16)
                if l < LAYERS:
                    if l == 5:
                        l2_sync(sp)
                    load_blob(sp, l)
                if l == 3:
                    l1_sync(sp)
                if l == 7:
                    l3_sync(sp)
            sp.wait_ge(sem("x_ready"), 1)
            sp.dma_start(d["out"].rearrange("(w p) c -> p w c", p=P), X[:, :, :]).then_inc(sem("out_written"), 16)
            sp.wait_ge(sem("out_written"), 16)

        @block.gpsimd
        def _(pool):
            sort_pool(pool)
            l0_pool(pool)
            if LAYERS > 2:
                l1_pool(pool)
            if LAYERS > 4:
                l2_pool(pool)
            if LAYERS > 6:
                l3_pool(pool)

        @block.vector
        def _(dve):
            link = linker(dve, "vector")
            sort_vector(dve)
            programs = [l0_vector, lambda e: ffn_vector(e, 1), l1_vector, l1f_vector, l2_vector,
                        lambda e: ffn_vector(e, 5), l3_vector, lambda e: ffn_vector(e, 7)]
            for l in range(LAYERS):
                if l:
                    layer_norm_vector(dve, l, link)
                programs[l](dve)
                if l == 0:
                    wait_empty(dve, "l0_back")
            dve.memset(small[:, :], 0.0).then_inc(sem("x_ready"), 1)

        @block.scalar
        def _(act):
            sort_scalar(act)
            xnt_scalar(act, 0)
            programs = [l0_scalar, lambda e: ffn_scalar(e, 1), l1_scalar, l1f_scalar, l2_scalar,
                        lambda e: ffn_scalar(e, 5), l3_scalar, lambda e: ffn_scalar(e, 7)]
            for l in range(LAYERS):
                if l:
                    std_scalar(act, l)
                programs[l](act)

        @block.tensor
        def _(pe):
            sort_tensor(pe)
            xnt_tensor(pe, 0)
            programs = [l0_tensor, lambda e: ffn_tensor(e, 1), l1_tensor, l1f_tensor, l2_tensor,
                        lambda e: ffn_tensor(e, 5), l3_tensor, lambda e: ffn_tensor(e, 7)]
            for l in range(LAYERS):
                programs[l](pe)


DIRECT = ["x", "src", "dst", "edge_attr_128", "edge_attr_256", "edge_attr_54", "edge_type_2", "edge_type_8",
          "edge_weight", "node_type_2", "node_vec"]


def kernel(**inputs):
    import concourse.bacc as bacc
    from concourse.bass_utils import run_bass_kernel_spmd as run

    inputs = {k: np.ascontiguousarray(v) for k, v in inputs.items()}
    nc = bacc.Bacc("TRN2", target_bir_lowering=False, num_devices=1)
    arrays = {k: inputs[k] for k in DIRECT}
    places, widths = [], []
    for l, parts in enumerate(blobs(inputs)):
        at, width = blob_places(parts)
        blob = np.zeros((128, width), np.float32)
        for name, a in parts:
            c, rows, cols = at[name]
            blob[:rows, c:c + cols] = a
        arrays[f"blob{l}"] = blob
        places.append(at)
        widths.append(width)
    d, sent = {}, {}
    for name, a in arrays.items():
        sent[f"in_{name}_dram"] = a
        d[name] = nc.dram_tensor(f"in_{name}_dram", a.shape, mybir.dt.from_np(a.dtype), kind="ExternalInput").ap()
    d["out"] = nc.dram_tensor("out_0_dram", (N, C), mybir.dt.float32, kind="ExternalOutput").ap()
    build(nc, d, places, widths)
    r = run(nc, [sent], core_ids=[0])
    return r.results[0]["out_0_dram"]
```
